# Optimizing a Trainium2 kernel written in Bass

```python
import numpy as np
import jax
import jax.numpy as jnp

def _softmax(x, axis=-1):
    return jax.nn.softmax(x, axis=axis)

def _gelu(x):
    return jax.nn.gelu(x, approximate=True)

def _silu(x):
    return jax.nn.silu(x)

def _sigmoid(x):
    return jax.nn.sigmoid(x)

def _layernorm(x, axis=-1, eps=1e-05):
    m = jnp.mean(x, axis=axis, keepdims=True)
    v = jnp.var(x, axis=axis, keepdims=True)
    return (x - m) / jnp.sqrt(v + eps)

def _scatter_add(tgt, idx, src, axis=0):
    return tgt.at[idx].add(src)

def _segment_sum(src, seg, n):
    return jax.ops.segment_sum(src, seg, n)
kernel_name = 'mk_flamingo_gated_d1_seqx_r8_5054a7'

def setup_inputs(seed: int=0):
    np.random.seed(seed)
    _w = jnp.asarray

    def _rec_inputs():
        import jax
        import jax.numpy as jnp
        _rk = jax.random.key(seed)
        x = 7.22e-05 + 1 * jax.random.normal(jax.random.fold_in(_rk, 1), (8, 128, 512), jnp.float32)
        _lenS = 128 - jax.random.randint(jax.random.fold_in(_rk, 7), (8,), 0, max(1, 128 // 4) + 1, jnp.int32)
        _lenS2 = 128 - jax.random.randint(jax.random.fold_in(_rk, 8), (8,), 0, max(1, 128 // 4) + 1, jnp.int32)
        _ctx_4096P = jax.random.normal(jax.random.fold_in(_rk, 11), (8, 16, 512), jnp.float32)
        _ctx_4096c = jax.random.dirichlet(jax.random.fold_in(_rk, 511), 0.3 * jnp.ones((16,), jnp.float32), (8, 128))
        _ctx_4096t = jnp.einsum('bsk,bkd->bsd', _ctx_4096c, _ctx_4096P)
        _ctx_4096t = _ctx_4096t * jax.lax.rsqrt(jnp.mean(jnp.square(_ctx_4096t)) + 1e-12) * 0.953939
        ctx_4096 = 4.13588e-05 + 0.999923 * (_ctx_4096t + 0.3 * jax.random.normal(jax.random.fold_in(_rk, 611), (8, 128, 512), jnp.float32))
        _validS = jnp.arange(128)[None, :] < _lenS[:, None]
        _validS2 = jnp.arange(128)[None, :] < _lenS2[:, None]
        _causal = jnp.tril(jnp.ones((128, 128), dtype=bool))
        mask_BxSxS2_bk0 = jnp.logical_not(jnp.broadcast_to(_validS2[:, None, :], (8, 128, 128)))
        _g = jax.random.normal(jax.random.fold_in(_rk, 9001), (2, 1), jnp.float32)
        _g = jnp.sign(_g) * jnp.maximum(jnp.abs(_g), 1.0) + (_g == 0) * 1.0
        g_xattn = _g[0]
        g_ffn = _g[1]
        return (x, ctx_4096, mask_BxSxS2_bk0, g_xattn, g_ffn)
    x, ctx_4096, mask_BxSxS2_bk0, g_xattn, g_ffn = _rec_inputs()

    def _L0_xattn_setup():
        import jax, jax.numpy as jnp
        import numpy as np
        B, LQ, LK, D, H, DH = (2, 128, 128, 512, 32, 128)
        EPS = 1e-05

        def _rmsnorm(x, weight):
            var = jnp.mean(jnp.square(x), axis=-1, keepdims=True)
            return x * jax.lax.rsqrt(var + EPS) * weight
        key = jax.random.key(seed)
        ks = jax.random.split(key, 8)
        scale = 0.02
        return {'hidden_states': jax.random.normal(ks[0], (B, LQ, D), jnp.float32), 'key_value_states': jax.random.normal(ks[1], (B, LK, D), jnp.float32), 'attention_mask': jax.random.randint(ks[2], (B, LQ, LK), 0, 2) > 0, 'position_bias': jax.random.normal(ks[3], (H, LQ, LK), jnp.float32), 'ln_weight': jnp.ones((D,), jnp.float32), 'w_q': jax.random.normal(ks[4], (H * DH, D), jnp.float32) * scale, 'w_k': jax.random.normal(ks[5], (H * DH, D), jnp.float32) * scale, 'w_v': jax.random.normal(ks[6], (H * DH, D), jnp.float32) * scale, 'w_out': jax.random.normal(ks[7], (D, H * DH), jnp.float32) * scale}
    _L0_xattn_all = _L0_xattn_setup()
    _L0_xattn_in = {k: v for k, v in _L0_xattn_all.items() if k in ('position_bias', 'ln_weight', 'w_q', 'w_k', 'w_v', 'w_out')}
    del _L0_xattn_all

    def _L0_ffn_setup():
        import jax, jax.numpy as jnp
        import numpy as np
        DIM = 512
        INTER = 128
        E = 16
        GROUPS = 4
        LIM = 2
        K = 2
        SHARED_INTER = 2 * INTER
        SCALE = 1.0
        key = jax.random.key(seed)
        ks = jax.random.split(key, 16)

        def n(k, shape, s=0.02):
            return jax.random.normal(k, shape, jnp.float32) * s
        return {'x': jax.random.normal(ks[0], (1, 256, DIM), jnp.float32), 'router_w': n(ks[1], (DIM, E)), 'router_b': n(ks[2], (E,)), 'router_bias': n(ks[3], (E,), 1.0), 'ew1': n(ks[4], (E, DIM, INTER)), 'eb1': n(ks[5], (E, INTER)), 'ew2': n(ks[6], (E, DIM, INTER)), 'eb2': n(ks[7], (E, INTER)), 'ew3': n(ks[8], (E, INTER, DIM)), 'eb3': n(ks[9], (E, DIM)), 'sw1': n(ks[10], (DIM, SHARED_INTER)), 'sb1': n(ks[11], (SHARED_INTER,)), 'sw2': n(ks[12], (DIM, SHARED_INTER)), 'sb2': n(ks[13], (SHARED_INTER,)), 'sw3': n(ks[14], (SHARED_INTER, DIM)), 'sb3': n(ks[15], (DIM,))}
    _L0_ffn_all = _L0_ffn_setup()
    _L0_ffn_in = {k: v for k, v in _L0_ffn_all.items() if k in ('router_w', 'router_b', 'router_bias', 'ew1', 'eb1', 'ew2', 'eb2', 'ew3', 'eb3', 'sw1', 'sb1', 'sw2', 'sb2', 'sw3', 'sb3')}
    del _L0_ffn_all
    return {'x': x, 'ctx_4096': ctx_4096, 'mask_BxSxS2_bk0': mask_BxSxS2_bk0, 'g_xattn': g_xattn, 'g_ffn': g_ffn, 'L0_xattn_position_bias': _L0_xattn_in['position_bias'], 'L0_xattn_ln_weight': _L0_xattn_in['ln_weight'], 'L0_xattn_w_q': _L0_xattn_in['w_q'], 'L0_xattn_w_k': _L0_xattn_in['w_k'], 'L0_xattn_w_v': _L0_xattn_in['w_v'], 'L0_xattn_w_out': _L0_xattn_in['w_out'], 'L0_ffn_router_w': _L0_ffn_in['router_w'], 'L0_ffn_router_b': _L0_ffn_in['router_b'], 'L0_ffn_router_bias': _L0_ffn_in['router_bias'], 'L0_ffn_ew1': _L0_ffn_in['ew1'], 'L0_ffn_eb1': _L0_ffn_in['eb1'], 'L0_ffn_ew2': _L0_ffn_in['ew2'], 'L0_ffn_eb2': _L0_ffn_in['eb2'], 'L0_ffn_ew3': _L0_ffn_in['ew3'], 'L0_ffn_eb3': _L0_ffn_in['eb3'], 'L0_ffn_sw1': _L0_ffn_in['sw1'], 'L0_ffn_sb1': _L0_ffn_in['sb1'], 'L0_ffn_sw2': _L0_ffn_in['sw2'], 'L0_ffn_sb2': _L0_ffn_in['sb2'], 'L0_ffn_sw3': _L0_ffn_in['sw3'], 'L0_ffn_sb3': _L0_ffn_in['sb3']}

def reference(x, ctx_4096, mask_BxSxS2_bk0, g_xattn, g_ffn, L0_xattn_position_bias, L0_xattn_ln_weight, L0_xattn_w_q, L0_xattn_w_k, L0_xattn_w_v, L0_xattn_w_out, L0_ffn_router_w, L0_ffn_router_b, L0_ffn_router_bias, L0_ffn_ew1, L0_ffn_eb1, L0_ffn_ew2, L0_ffn_eb2, L0_ffn_ew3, L0_ffn_eb3, L0_ffn_sw1, L0_ffn_sb1, L0_ffn_sw2, L0_ffn_sb2, L0_ffn_sw3, L0_ffn_sb3):
    import jax
    import jax.numpy as jnp

    def _L0_xattn_ref(hidden_states, key_value_states, attention_mask, position_bias, ln_weight, w_q, w_k, w_v, w_out):
        import jax, jax.numpy as jnp
        import numpy as np
        B, LQ, LK, D, H, DH = (2, 128, 128, 512, 32, 128)
        EPS = 1e-05

        def _rmsnorm(x, weight):
            var = jnp.mean(jnp.square(x), axis=-1, keepdims=True)
            return x * jax.lax.rsqrt(var + EPS) * weight
        x = _rmsnorm(hidden_states, ln_weight)
        b, lq, _ = x.shape
        lk = key_value_states.shape[1]
        h_q = (x @ w_q.T).reshape(b, lq, H, DH)
        h_k = (key_value_states @ w_k.T).reshape(b, lk, H, DH)
        h_v = (key_value_states @ w_v.T).reshape(b, lk, H, DH)
        score = jnp.einsum('bqhd,bkhd->bhqk', h_q, h_k)
        score = score + position_bias[None]
        m = attention_mask[:, None]
        score = jnp.where(m, score, -jnp.inf)
        score = jax.nn.softmax(score, axis=-1)
        score = jnp.where(m, score, 0.0)
        attn = jnp.einsum('bhqk,bkhd->bqhd', score, h_v).reshape(b, lq, H * DH)
        out = attn @ w_out.T
        return hidden_states + out

    def _L0_ffn_ref(x, router_w, router_b, router_bias, ew1, eb1, ew2, eb2, ew3, eb3, sw1, sb1, sw2, sb2, sw3, sb3):
        import jax, jax.numpy as jnp
        import numpy as np
        DIM = 512
        INTER = 128
        E = 16
        GROUPS = 4
        LIM = 2
        K = 2
        SHARED_INTER = 2 * INTER
        SCALE = 1.0
        shape = x.shape
        xt = x.reshape(-1, DIM)
        T = xt.shape[0]
        logits = xt @ router_w + router_b
        scores = jax.nn.softmax(logits.astype(jnp.float32), axis=-1) + router_bias
        g = scores.reshape(T, GROUPS, E // GROUPS)
        _, gidx = jax.lax.top_k(g.max(axis=-1), LIM)
        keep = jnp.zeros((T, GROUPS), bool).at[jnp.arange(T)[:, None], gidx].set(True)
        masked = jnp.where(keep[:, :, None], g, -jnp.inf).reshape(T, E)
        _, idx = jax.lax.top_k(masked, K)
        vals = (jnp.take_along_axis(scores, idx, axis=1) * SCALE).astype(x.dtype)
        gate = jnp.zeros((T, E), x.dtype).at[jnp.arange(T)[:, None], idx].add(vals)

        def step(y, p):
            w1, b1, w2, b2, w3, b3, ge = p
            h = jax.nn.silu(xt @ w1 + b1) * (xt @ w2 + b2)
            return (y + ge[:, None] * (h @ w3 + b3), None)
        y, _ = jax.lax.scan(step, jnp.zeros_like(xt), (ew1, eb1, ew2, eb2, ew3, eb3, gate.T))
        z = jax.nn.silu(xt @ sw1 + sb1) * (xt @ sw2 + sb2) @ sw3 + sb3
        return (y + z).reshape(shape)
    x = x + jnp.tanh(g_xattn[0]) * _L0_xattn_ref(_layernorm(x, axis=-1), ctx_4096, mask_BxSxS2_bk0, L0_xattn_position_bias, L0_xattn_ln_weight, L0_xattn_w_q, L0_xattn_w_k, L0_xattn_w_v, L0_xattn_w_out)
    x = x + jnp.tanh(g_ffn[0]) * _L0_ffn_ref(_layernorm(x, axis=-1), L0_ffn_router_w, L0_ffn_router_b, L0_ffn_router_bias, L0_ffn_ew1, L0_ffn_eb1, L0_ffn_ew2, L0_ffn_eb2, L0_ffn_ew3, L0_ffn_eb3, L0_ffn_sw1, L0_ffn_sb1, L0_ffn_sw2, L0_ffn_sb2, L0_ffn_sw3, L0_ffn_sb3)
    return x

_drawn_inputs = setup_inputs


def setup_inputs(seed=0):
    import zlib

    import numpy as np

    out = dict(_drawn_inputs(seed))
    spreads = {'L0_xattn_ln_weight': (1.0, 0.537)}
    factors = {'L0_ffn_router_w': 25.632,
     'L0_ffn_router_b': 200.0,
     'L0_ffn_eb1': 37.328,
     'L0_ffn_eb2': 37.029,
     'L0_ffn_sw1': 3.157,
     'L0_ffn_sb1': 8.0,
     'L0_ffn_sw2': 3.073,
     'L0_ffn_sb2': 8.0,
     'L0_ffn_sw3': 3.085,
     'L0_ffn_sb3': 5.416}
    for name, (base, spread) in spreads.items():
        noise = np.random.default_rng([zlib.crc32(name.encode()), seed]).standard_normal(out[name].shape)
        drawn = base * np.exp(spread * noise) if base else spread * noise
        out[name] = jnp.asarray(drawn.astype(out[name].dtype))
    for name, factor in factors.items():
        out[name] = (out[name] * factor).astype(out[name].dtype)
    return out
```

```python
from contextlib import ExitStack

import concourse.bass as bass
from concourse import mybir

F32 = mybir.dt.float32
F32R = mybir.dt.float32r
I32 = mybir.dt.int32
U8 = mybir.dt.uint8
ALU = mybir.AluOpType
ACT = mybir.ActivationFunctionType
AX = mybir.AxisListType

P = 128
B = 8
D = 512
C = D // P
T = B * P
H = 32
G = 4
NG = H // G
HALF = T // 2
BH = B // 2
E = 16
EG = 4
EM = E // EG
SH = 2
NE = SH + E
W12 = 2 * C * P
EPS = 1e-5
BIG = 1e30


def need(eng, sem, count):
    if not isinstance(count, int) or count > 0:
        eng.wait_ge(sem, count)


def build(nc, x, ctxT, mask, gains, pbias, lnw, wqk, wv, wo, w12, w3, rw, rb, b3, out):
    with ExitStack() as stack:
        base = (nc.sbuf_base + 63) // 64 * 64
        top = [0]

        def place(name, shape, dtype, at=None):
            size = 1
            for n in shape[1:]:
                size *= n
            size = (size * (1 if dtype == U8 else 4) + 31) // 32 * 32
            if at is None:
                at, top[0] = top[0], top[0] + size
            return nc.alloc_sbuf_tensor_at(name, shape, dtype, offset=base + at)

        def room(size):
            at, top[0] = top[0], top[0] + size
            return at

        at_ctx_hi, at_ctx_lo = room(C * T * 4), room(C * T * 4)
        ctx_hi = place("ctx_hi", [P, C, T], F32R, at_ctx_hi)
        ctx_lo = place("ctx_lo", [P, C, T], F32R, at_ctx_lo)
        ctx_raw = place("ctx_raw", [P, C, T], F32, at_ctx_lo)
        xT_hi = place("xT_hi", [P, C, T], F32R)
        xT_lo = place("xT_lo", [P, C, T], F32R)
        acc = place("acc", [P, B, D], F32)
        at_wqk = room(4 * W12 * 4)
        wqk_hi = place("wqk_hi", [P, 2, 2, C, P], F32R, at_wqk)
        wqk_lo = place("wqk_lo", [P, 2, 2, C, P], F32R, at_wqk + 2 * W12 * 4)
        wqk_raw = place("wqk_raw", [P, 2, 2, C, P], F32, at_wqk + 2 * W12 * 4)
        at_wv = room(2 * C * D * 4)
        wv_hi = place("wv_hi", [P, C, D], F32R, at_wv)
        wv_lo = place("wv_lo", [P, C, D], F32R, at_wv + C * D * 4)
        wv_raw = place("wv_raw", [P, C, D], F32, at_wv + C * D * 4)
        at_wo = room(2 * G * D * 4)
        wo_hi = place("wo_hi", [P, G, D], F32R, at_wo)
        wo_lo = place("wo_lo", [P, G, D], F32R, at_wo + G * D * 4)
        wo_raw = place("wo_raw", [P, G, D], F32, at_wo + G * D * 4)
        at_v = room(B * G * P * 4)
        v_s = place("v_s", [P, B, G * P], F32, at_v)
        at_attn = room(2 * G * T * 4)
        attn_hi = place("attn_hi", [P, G, T], F32R, at_attn)
        attn_lo = place("attn_lo", [P, G, T], F32R, at_attn + G * T * 4)
        at_qk = room(2 * T * 4)
        qT = place("qT", [P, T], F32, at_qk)
        kT = place("kT", [P, T], F32, at_qk + T * 4)
        at_s = room(T * 4)
        probs = place("probs", [P, 2, BH, P], F32, at_s)
        at_pT = room(T * 4)
        pT = place("pT", [P, 2, HALF], F32, at_pT)
        mask_bias = place("mask_bias", [P, B, P], F32)
        score_bias = place("score_bias", [P, B, P], F32)
        pos_bias = place("pos_bias", [P, 2, P], F32)
        ident = place("ident", [P, P], F32)
        gain = place("gain", [P, 2], F32)
        any_mask = place("any_mask", [P, B], F32)
        neg_max = place("neg_max", [P, 2, BH], F32)
        row_sum = place("row_sum", [P, 2, BH], F32)
        row_inv = place("row_inv", [P, 2, BH], F32)
        row_scale = place("row_scale", [P, 2, BH], F32)
        stats = place("stats", [P, B, 6], F32)
        mean_var = place("mean_var", [P, B, 2], F32)
        rstd = place("rstd", [P, B], F32)
        mean_sq = place("mean_sq", [P, B], F32)
        rms = place("rms", [P, B], F32)
        minus_half = place("minus_half", [P, B], F32)
        assert base + top[0] <= nc.sbuf_usable_end, top[0]

        mask_u8 = place("mask_u8", [P, B, P], U8, at_s)
        sq_scratch = place("sq_scratch", [P, D], F32, at_pT)
        lnw_s = place("lnw_s", [P, D], F32, at_pT + D * 4)
        xn = place("xn", [P, B, D], F32, at_attn)
        x_res = place("x_res", [P, B, D], F32, at_ctx_hi)
        y_acc = place("y_acc", [P, B, D], F32, at_ctx_lo)
        x2n = place("x2n", [P, B, D], F32, at_v)
        w12_hi, w12_lo, w12_raw, w3_hi, w3_lo, w3_raw = [], [], [], [], [], []
        for n, at in enumerate((at_wv, at_wqk)):
            w12_hi.append(place(f"w12_hi{n}", [P, 2, C, P], F32R, at))
            w12_lo.append(place(f"w12_lo{n}", [P, 2, C, P], F32R, at + W12 * 4))
            w12_raw.append(place(f"w12_raw{n}", [P, W12 + 2], F32, at + W12 * 4))
            w3_hi.append(place(f"w3_hi{n}", [P, D], F32R, at + 2 * W12 * 4 + 32))
            w3_lo.append(place(f"w3_lo{n}", [P, D], F32R, at + 2 * W12 * 4 + 32 + D * 4))
            w3_raw.append(place(f"w3_raw{n}", [P, D], F32, at + 2 * W12 * 4 + 32 + D * 4))
        hT_hi = [place(f"hT_hi{n}", [P, T], F32R, at_attn + n * T * 4) for n in range(2)]
        hT_lo = [place(f"hT_lo{n}", [P, T], F32R, at_attn + (2 + n) * T * 4) for n in range(2)]
        silu = place("silu", [P, 2, HALF], F32, at_attn + 4 * T * 4)
        hT = place("hT", [P, 2, HALF], F32, at_attn + 5 * T * 4)
        b3_s = place("b3_s", [E + 1, D], F32, at_qk)
        rw_raw = place("rw_raw", [P, C, E], F32, at_qk + D * 4)
        rw_lo = place("rw_lo", [P, C, E], F32R, at_qk + D * 4)
        rw_hi = place("rw_hi", [P, C, E], F32R, at_qk + D * 4 + C * E * 4)
        rb_s = place("rb_s", [P, 2, E], F32, at_qk + D * 4 + 2 * C * E * 4)
        gT = place("gT", [E + 1, T], F32, at_wo)
        gates = place("gates", [P, NE, B], F32, at_wo + T * 4)
        at = at_wo + T * 4 + NE * B * 4
        gate_now = [place(f"gate_now{n}", [P, B], F32, at + 32 * n) for n in range(2)]
        gate_last = place("gate_last", [P, B], F32, at + 64)
        at += 96
        rt = [place(f"rt{n}", [P, B, E], F32, at + n * B * E * 4) for n in range(10)]
        at += 10 * B * E * 4
        rg = [place(f"rg{n}", [P, B, EG], F32, at + n * B * EG * 4) for n in range(10)]
        at += 10 * B * EG * 4
        r1 = [place(f"r1_{n}", [P, B], F32, at + n * 32) for n in range(10)]
        at += 10 * 32
        rank_i = place("rank_i", [P, B, E], I32, at)
        assert at + B * E * 4 <= at_wo + 2 * G * D * 4

        def bank(name):
            return stack.enter_context(nc.psum_tensor(name, [P, D], F32))

        ps_job = [bank("ps_job0"), bank("ps_job1")]
        ps_score = [bank("ps_score0"), bank("ps_score1")]
        ps_turn = [bank("ps_turn0"), bank("ps_turn1")]
        ps_attn = [bank("ps_attn0"), bank("ps_attn1")]
        ps_h1 = [ps_job[0], ps_attn[0]]
        ps_h2 = [ps_job[1], ps_attn[1]]
        ps_y = [ps_score[0], ps_score[1], ps_turn[0], ps_turn[1]]

        def sem(name):
            return stack.enter_context(nc.semaphore(name))

        ctx_in = [sem(f"ctx_in{c}") for c in range(C)]
        x_in = [sem(f"x_in{t}") for t in range(B)]
        mask_in, gain_in, lnw_in, wv_in, wo_in = map(sem, ("mask_in", "gain_in", "lnw_in", "wv_in", "wo_in"))
        wqk_in = [sem("wqk_in0"), sem("wqk_in1")]
        pos_in = [sem("pos_in0"), sem("pos_in1")]
        x_res_in, rw_in, rb_in, b3_in = map(sem, ("x_res_in", "rw_in", "rb_in", "b3_in"))
        w12_in = [sem("w12_in0"), sem("w12_in1")]
        w3_in = [sem("w3_in0"), sem("w3_in1")]
        ctx_hi_done, ctx_split = sem("ctx_hi_done"), sem("ctx_split")
        wqk_hi_done, wqk_split = sem("wqk_hi_done"), sem("wqk_split")
        wv_hi_done, wv_split = sem("wv_hi_done"), sem("wv_split")
        wo_hi_done, wo_split = sem("wo_hi_done"), sem("wo_split")
        w12_hi_done, w12_split = sem("w12_hi_done"), sem("w12_split")
        w3_hi_done, w3_split = sem("w3_hi_done"), sem("w3_split")
        rw_split = sem("rw_split")
        ident_done, mask_done, gain_done = sem("ident_done"), sem("mask_done"), sem("gain_done")
        rank_done = sem("rank_done")
        var_ready, rstd_ready, half_done = sem("var_ready"), sem("rstd_ready"), sem("half_done")
        xn_ready, xT_psum, xT_hi_done, xT_split = map(sem, ("xn_ready", "xT_psum", "xT_hi_done", "xT_split"))
        qk_psum, qk_sbuf, v_psum, v_sbuf = map(sem, ("qk_psum", "qk_sbuf", "v_psum", "v_sbuf"))
        o_psum, o_added = sem("o_psum"), sem("o_added")
        bias_ready, score_psum, score_biased, max_done, exp_done = map(
            sem, ("bias_ready", "score_psum", "score_biased", "max_done", "exp_done"))
        row_scaled = sem("row_scaled")
        probs_ready, pT_psum, pT_sbuf, attn_psum, attn_hi_done, attn_split = map(
            sem, ("probs_ready", "pT_psum", "pT_sbuf", "attn_psum", "attn_hi_done", "attn_split"))
        logits_psum, logits_read, router_in, router_exp, gates_done = map(
            sem, ("logits_psum", "logits_read", "router_in", "router_exp", "gates_done"))
        h_psum, silu_done, h_gated, h_hi_done, h_split = map(
            sem, ("h_psum", "silu_done", "h_gated", "h_hi_done", "h_split"))
        y_psum, y_added, gate_copied = sem("y_psum"), sem("y_added"), sem("gate_copied")
        gT_psum, gT_sbuf, b3_psum, b3_added = map(sem, ("gT_psum", "gT_sbuf", "b3_psum", "b3_added"))
        final_ready, stored = sem("final_ready"), sem("stored")
        dve_chain = sem("dve_chain")

        block = stack.enter_context(nc.Block())

        @block.sync
        def _(sp):
            for c in range(C):
                sp.dma_start(ctx_raw[:, c], ctxT[:, c]).then_inc(ctx_in[c], 16)
                if c == 1:
                    sp.dma_start(wv_raw[:], wv[0]).then_inc(wv_in, 16)
            for t in range(B):
                sp.dma_start(acc[:, t], x[t]).then_inc(x_in[t], 16)
                if t == 3:
                    sp.dma_start(wqk_raw[:, 0], wqk[0]).then_inc(wqk_in[0], 16)

            def load_step(g, j, first):
                i = G * g + j
                if j == 0 and not first:
                    need(sp, v_psum, B * g)
                    sp.dma_start(wv_raw[:], wv[g]).then_inc(wv_in, 16)
                need(sp, bias_ready, i - 1)
                sp.dma_start(pos_bias[:, j % 2], pbias[i]).then_inc(pos_in[j % 2], 16)
                need(sp, qk_psum, 4 * i)
                sp.dma_start(wqk_raw[:, (j + 1) % 2], wqk[i + 1]).then_inc(wqk_in[(j + 1) % 2], 16)
                if j == 2:
                    need(sp, o_psum, B * g)
                    sp.dma_start(wo_raw[:], wo[g]).then_inc(wo_in, 16)

            for j in range(G):
                load_step(0, j, True)
            with sp.Fori(1, NG) as g:
                for j in range(G):
                    load_step(g, j, False)

            sp.wait_ge(v_psum, B * NG)
            sp.wait_ge(qk_psum, 4 * H)
            sp.dma_start(x_res[:], x.rearrange("t p d -> p t d")).then_inc(x_res_in, 16)
            sp.dma_start(w12_raw[0][:], w12[0]).then_inc(w12_in[0], 16)
            sp.wait_ge(score_psum, 2 * H)
            sp.dma_start(rw_raw[:], rw).then_inc(rw_in, 16)
            sp.dma_start(rb_s[:], rb.partition_broadcast(P)).then_inc(rb_in, 16)
            sp.dma_start(b3_s[:], b3).then_inc(b3_in, 16)

            def expert_load(e, even, last):
                now, then = (0, 1) if even else (1, 0)
                need(sp, y_psum, B * (e - 1))
                sp.dma_start(w3_raw[now][:], w3[e]).then_inc(w3_in[now], 16)
                if not last:
                    need(sp, h_gated, 2 * e)
                    sp.dma_start(w12_raw[then][:], w12[e + 1]).then_inc(w12_in[then], 16)

            sp.wait_ge(wqk_split, H + 1)
            expert_load(0, True, False)
            expert_load(1, False, False)
            expert_load(2, True, False)
            with sp.Fori(1, NE // 2 - 1) as p:
                expert_load(2 * p + 1, False, False)
                expert_load(2 * p + 2, True, False)
            expert_load(NE - 1, False, True)

            for t in range(B):
                sp.wait_ge(final_ready, t + 1)
                sp.dma_start(out[t], y_acc[:, t]).then_inc(stored, 16)
            sp.wait_ge(stored, 16 * B)

        @block.gpsimd
        def _(pool):
            nc.gpsimd.memset(ident[:], 0.0).then_inc(ident_done, 1)
            pool.wait_ge(ident_done, 1)
            nc.gpsimd.affine_select(out=ident[:], in_=ident[:], compare_op=ALU.not_equal, fill=1.0,
                                    base=0, pattern=[[-1, P]], channel_multiplier=1).then_inc(ident_done, 1)

            nc.gpsimd.memset(minus_half[:], -0.5).then_inc(half_done, 1)
            pool.wait_ge(half_done, 1)

            def to_minus_half(dst, src, count):
                pool.wait_ge(var_ready, count)
                nc.gpsimd.tensor_tensor(dst, src, minus_half[:, 0:src.shape[1]], ALU.pow).then_inc(rstd_ready, 1)

            to_minus_half(rstd[:], rstd[:], 1)
            to_minus_half(rms[:], rms[:], 2)

            def bias_step(g, j, first):
                i = G * g + j
                if first and j == 0:
                    pool.wait_ge(mask_done, 1)
                pool.wait_ge(pos_in[j % 2], 16 * (2 * g + j // 2 + 1))
                need(pool, score_biased, 2 * i)
                nc.gpsimd.tensor_tensor(score_bias[:], mask_bias[:],
                                        pos_bias[:, j % 2].unsqueeze(1).broadcast_to([P, B, P]),
                                        ALU.add).then_inc(bias_ready, 1)

            for j in range(G):
                bias_step(0, j, True)
            with pool.Fori(1, NG) as g:
                for j in range(G):
                    bias_step(g, j, False)

            for t in range(B):
                to_minus_half(rstd[:, t:t + 1], rstd[:, t:t + 1], 3 + t)

            pool.wait_ge(o_psum, B * NG)
            nc.gpsimd.iota(rank_i[:], pattern=[[0, B], [-1, E]], base=E, channel_multiplier=0).then_inc(rank_done, 1)
            nc.gpsimd.memset(gates[:, 0:SH, :], 1.0).then_inc(rank_done, 1)

        @block.tensor
        def _(pe):
            def three(psum, pairs):
                n = len(pairs)
                for k, (l_hi, l_lo, r_hi, r_lo) in enumerate(pairs):
                    nc.tensor.matmul(psum, l_lo, r_hi, start=(k == 0), stop=False)
                    nc.tensor.matmul(psum, l_hi, r_lo, start=False, stop=False)
                    last = nc.tensor.matmul(psum, l_hi, r_hi, start=False, stop=(k == n - 1))
                return last

            def cols(t, w=P):
                return slice(t * w, (t + 1) * w)

            def turn_tokens(src, t):
                for c in range(C):
                    last = nc.tensor.transpose(ps_turn[t % 2][:, cols(c)], src[:, t, cols(c)], ident[:])
                last.then_inc(xT_psum, 1)

            def project_qk(g, j, which, half):
                hi, lo = (xT_hi, xT_lo) if which == 0 else (ctx_hi, ctx_lo)
                tok = cols(half, HALF)
                three(ps_job[half][:], [(wqk_hi[:, j % 2, which, c], wqk_lo[:, j % 2, which, c],
                                         hi[:, c, tok], lo[:, c, tok]) for c in range(C)]).then_inc(qk_psum, 1)

            def project_v(t):
                three(ps_job[t % 2][:], [(ctx_hi[:, c, cols(t)], ctx_lo[:, c, cols(t)], wv_hi[:, c], wv_lo[:, c])
                                         for c in range(C)]).then_inc(v_psum, 1)

            def project_out(t):
                three(ps_job[t % 2][:], [(attn_hi[:, s, cols(t)], attn_lo[:, s, cols(t)], wo_hi[:, s], wo_lo[:, s])
                                         for s in range(G)]).then_inc(o_psum, 1)

            def score(i):
                need(pe, qk_sbuf, 4 * i + 4)
                for half in range(2):
                    need(pe, score_biased, 2 * i - 1 + half)
                    for b in range(BH):
                        tok = cols(BH * half + b)
                        last = nc.tensor.matmul(ps_score[half][:, cols(b)], qT[:, tok], kT[:, tok], start=True, stop=True)
                    last.then_inc(score_psum, 1)

            def turn_probs(i):
                for half in range(2):
                    pe.wait_ge(probs_ready, 2 * i + 1 + half)
                    need(pe, pT_sbuf, 2 * i - 1 + half)
                    for b in range(BH):
                        last = nc.tensor.transpose(ps_turn[half][:, cols(b)], probs[:, half, b], ident[:])
                    last.then_inc(pT_psum, 1)

            def attend(i, slot):
                for half in range(2):
                    pe.wait_ge(pT_sbuf, 2 * i + 1 + half)
                    need(pe, attn_split, 2 * i - 1 + half)
                    for b in range(BH):
                        last = nc.tensor.matmul(ps_attn[half][:, cols(b)], v_s[:, BH * half + b, cols(slot)],
                                                pT[:, half, cols(b)], start=True, stop=True)
                    last.then_inc(attn_psum, 1)

            def head_step(g, j, first):
                i = G * g + j
                before = not (first and j == 0)
                if before:
                    score(i - 1)
                if j == 1 and not first:
                    pe.wait_ge(wo_split, g)
                    pe.wait_ge(attn_split, 2 * G * g)
                    for t in range(B):
                        if t < 2:
                            pe.wait_ge(v_sbuf, B * g + B - 1 + t)
                        else:
                            pe.wait_ge(o_added, B * (g - 1) + t - 1)
                        project_out(t)
                pe.wait_ge(wqk_split, i + 1)
                for half in range(2):
                    if j == 1 and not first:
                        pe.wait_ge(o_added, B * (g - 1) + B - 1 + half)
                    elif first and j == 0:
                        pe.wait_ge(v_sbuf, B - 1 + half)
                    else:
                        pe.wait_ge(qk_sbuf, 4 * (i - 1) + 3 + half)
                    project_qk(g, j, 1, half)
                    if first and j == 0:
                        for t in (3 + 2 * half, 4 + 2 * half):
                            turn_when_free(t)
                if first and j == 0:
                    turn_when_free(7)
                    pe.wait_ge(xT_split, B)
                pe.wait_ge(qk_sbuf, 4 * i + 1)
                project_qk(g, j, 0, 0)
                if before:
                    turn_probs(i - 1)
                pe.wait_ge(qk_sbuf, 4 * i + 2)
                project_qk(g, j, 0, 1)
                if before:
                    if j == 1:
                        pe.wait_ge(v_sbuf, B * g + B)
                    attend(i - 1, (j - 1) % G)
                if j == 0 and not first:
                    pe.wait_ge(wv_split, g + 1)
                    for t in range(B):
                        if t < 2:
                            pe.wait_ge(qk_sbuf, 4 * i + 3 + t)
                        else:
                            pe.wait_ge(v_sbuf, B * g + t - 1)
                        project_v(t)

            def turn_when_free(t):
                pe.wait_ge(xn_ready, t + 1)
                need(pe, xT_split, t - 1)
                turn_tokens(xn, t)

            pe.wait_ge(ctx_split, C)
            pe.wait_ge(wv_split, 1)
            pe.wait_ge(ident_done, 2)
            for t in range(B):
                need(pe, v_sbuf, t - 1)
                project_v(t)
                if t >= B - 3:
                    turn_when_free(t - (B - 3))
            for j in range(G):
                head_step(0, j, True)
            with pe.Fori(1, NG) as g:
                for j in range(G):
                    head_step(g, j, False)
            score(H - 1)
            turn_probs(H - 1)
            attend(H - 1, G - 1)

            def turn_x2(t):
                pe.wait_ge(xn_ready, B + t + 1)
                if t < 2:
                    pe.wait_ge(pT_sbuf, 2 * H)
                else:
                    pe.wait_ge(xT_split, B + t - 1)
                turn_tokens(x2n, t)

            pe.wait_ge(wo_split, NG)
            pe.wait_ge(attn_split, 2 * H)
            for t in range(B):
                if t < 2:
                    pe.wait_ge(qk_sbuf, 4 * (H - 1) + 3 + t)
                else:
                    pe.wait_ge(o_added, B * (NG - 1) + t - 1)
                project_out(t)
                if t >= 2:
                    turn_x2(t - 2)
            turn_x2(B - 2)

            def expert_h(e, buf, which, half):
                tok = cols(half, HALF)
                psum = (ps_h1, ps_h2)[which][half]
                three(psum[:], [(w12_hi[buf][:, which, c], w12_lo[buf][:, which, c],
                                 xT_hi[:, c, tok], xT_lo[:, c, tok]) for c in range(C)]).then_inc(h_psum, 1)

            def expert_y(e, buf, t):
                three(ps_y[t % 4][:], [(hT_hi[buf][:, cols(t)], hT_lo[buf][:, cols(t)],
                                        w3_hi[buf][:], w3_lo[buf][:])]).then_inc(y_psum, 1)

            def expert_step(e, even, first):
                now, then = (0, 1) if even else (1, 0)
                pe.wait_ge(w12_split, e + 1)
                n = 0
                for half in range(2):
                    for which in range(2):
                        pe.wait_ge((silu_done, h_gated)[which], 2 * e - 1 + half)
                        expert_h(e, now, which, half)
                        if n == 0:
                            pe.wait_ge(w3_split, e)
                        for t in (2 * n, 2 * n + 1):
                            if t % 4 == 0:
                                pe.wait_ge(h_split, 2 * (e - 1) + t // 4 + 1)
                            if not (first and t < 4):
                                pe.wait_ge(y_added, B * (e - 1) + t - 3)
                            expert_y(e, then, t)
                        n += 1

            pe.wait_ge(w12_split, 1)
            pe.wait_ge(xT_split, B + 4)
            pe.wait_ge(o_added, B * NG)
            expert_h(0, 0, 0, 0)
            expert_h(0, 0, 1, 0)
            turn_x2(B - 1)
            pe.wait_ge(rw_split, 1)
            pe.wait_ge(xT_split, 2 * B)
            for t in range(B):
                last = three(ps_score[0][:, cols(t, E)], [(xT_hi[:, c, cols(t)], xT_lo[:, c, cols(t)],
                                                           rw_hi[:, c], rw_lo[:, c]) for c in range(C)])
            last.then_inc(logits_psum, 1)
            expert_h(0, 0, 0, 1)
            expert_h(0, 0, 1, 1)
            pe.wait_ge(logits_read, 1)
            expert_step(1, False, True)
            expert_step(2, True, False)
            with pe.Fori(1, NE // 2 - 1) as p:
                expert_step(2 * p + 1, False, False)
                expert_step(2 * p + 2, True, False)
            expert_step(NE - 1, False, False)

            pe.wait_ge(gates_done, 1)
            for half in range(2):
                pe.wait_ge((silu_done, h_gated)[half], 2 * NE - 1)
                for b in range(BH):
                    last = nc.tensor.transpose((ps_h1, ps_h2)[half][0][0:E + 1, cols(b)],
                                               gates[:, SH - 1:NE, BH * half + b], ident[:])
                last.then_inc(gT_psum, 1)
            pe.wait_ge(gT_sbuf, 2)
            pe.wait_ge(b3_in, 16)
            for t in range(B):
                need(pe, b3_added, t - 1)
                nc.tensor.matmul((ps_h1, ps_h2)[t % 2][0][:], gT[:, cols(t)], b3_s[:],
                                 start=True, stop=True).then_inc(b3_psum, 1)
            pe.wait_ge(w3_split, NE)
            for t in range(B):
                if t % 4 == 0:
                    pe.wait_ge(h_split, 2 * (NE - 1) + t // 4 + 1)
                pe.wait_ge((y_added, final_ready)[t // 4], B * (NE - 1) + t - 3 if t < 4 else t - 3)
                expert_y(NE - 1, 1, t)

        @block.scalar
        def _(act):
            act.dma_start(gain[:], gains.partition_broadcast(P)).then_inc(gain_in, 16)
            act.dma_start(lnw_s[:], lnw.partition_broadcast(P)).then_inc(lnw_in, 16)
            act.dma_start(mask_u8[:], mask.rearrange("b q k -> q b k")).then_inc(mask_in, 16)

            def copy(dst, src):
                return nc.scalar.activation(dst, src, ACT.Copy)

            def tokens_hi(t, n):
                act.wait_ge(xT_psum, n + 1)
                copy(xT_hi[:, :, t * P:(t + 1) * P],
                     ps_turn[t % 2][:].rearrange("p (c k) -> p c k", c=C)).then_inc(xT_hi_done, 1)

            def exps(i, half):
                act.wait_ge(max_done, 2 * i + 1 + half)
                for b in range(BH):
                    last = nc.scalar.activation(probs[:, half, b], probs[:, half, b], ACT.Exp,
                                                bias=neg_max[:, half, b:b + 1],
                                                accum_out=row_sum[:, half, b:b + 1])
                last.then_inc(exp_done, 1)

            def take_qk(i, n, dst, half):
                act.wait_ge(qk_psum, 4 * i + n + 1)
                copy(dst[:, half * HALF:(half + 1) * HALF], ps_job[half][:]).then_inc(qk_sbuf, 1)

            def take_v(g, t):
                act.wait_ge(v_psum, B * g + t + 1)
                copy(v_s[:, t], ps_job[t % 2][:]).then_inc(v_sbuf, 1)

            def take_pT(i):
                for half in range(2):
                    act.wait_ge(pT_psum, 2 * i + 1 + half)
                    copy(pT[:, half], ps_turn[half][:]).then_inc(pT_sbuf, 1)

            def take_attn_hi(i, slot):
                for half in range(2):
                    act.wait_ge(attn_psum, 2 * i + 1 + half)
                    copy(attn_hi[:, slot, half * HALF:(half + 1) * HALF], ps_attn[half][:]).then_inc(attn_hi_done, 1)

            for c in range(C):
                act.wait_ge(ctx_in[c], 16)
                copy(ctx_hi[:, c], ctx_raw[:, c]).then_inc(ctx_hi_done, 1)
            act.wait_ge(gain_in, 16)
            nc.scalar.activation(gain[:], gain[:], ACT.Tanh).then_inc(gain_done, 1)

            def head_step(g, j, first):
                i = G * g + j
                before = not (first and j == 0)
                if before:
                    exps(i - 1, 0)
                take_qk(i, 0, kT, 0)
                if before:
                    exps(i - 1, 1)
                else:
                    tokens_hi(3, 3)
                    tokens_hi(4, 4)
                take_qk(i, 1, kT, 1)
                if not before:
                    for t in (5, 6, 7):
                        tokens_hi(t, t)
                take_qk(i, 2, qT, 0)
                if before:
                    take_pT(i - 1)
                take_qk(i, 3, qT, 1)
                if before:
                    take_attn_hi(i - 1, (j - 1) % G)
                if j == 0 and not first:
                    for t in range(B):
                        take_v(g, t)

            for t in range(B):
                take_v(0, t)
                if t >= B - 3:
                    tokens_hi(t - (B - 3), t - (B - 3))
            for j in range(G):
                head_step(0, j, True)
            with act.Fori(1, NG) as g:
                for j in range(G):
                    head_step(g, j, False)
            exps(H - 1, 0)
            exps(H - 1, 1)
            take_pT(H - 1)
            take_attn_hi(H - 1, G - 1)

            def split_w12(e, buf, count):
                act.wait_ge(w12_in[buf], count)
                copy(w12_hi[buf][:].rearrange("p w c k -> p (w c k)"), w12_raw[buf][:, 0:W12]).then_inc(w12_hi_done, 1)

            def split_w3(e, buf, count):
                act.wait_ge(w3_in[buf], count)
                copy(w3_hi[buf][:], w3_raw[buf][:]).then_inc(w3_hi_done, 1)

            split_w12(0, 0, 16)
            for t in range(B):
                tokens_hi(t, B + t)
            act.wait_ge(router_in, 1)
            nc.scalar.activation(rt[1][:], rt[1][:], ACT.Exp).then_inc(router_exp, 1)

            def expert_step(e, even, last, loads):
                now, then = (0, 1) if even else (1, 0)
                for half in range(2):
                    act.wait_ge(h_psum, 4 * e + 2 * half + 1)
                    nc.scalar.activation(silu[:, half], ps_h1[half][:], ACT.Silu,
                                         bias=w12_raw[now][:, W12:W12 + 1]).then_inc(silu_done, 1)
                    act.wait_ge(h_gated, 2 * e + half + 1)
                    copy(hT_hi[now][:, half * HALF:(half + 1) * HALF], hT[:, half]).then_inc(h_hi_done, 1)
                    if half == 0:
                        split_w3(e, now, 16 * loads)
                        if not last:
                            split_w12(e + 1, then, 16 * (loads if even else loads + 1))

            expert_step(0, True, False, 1)
            with act.Fori(0, NE // 2 - 1) as p:
                expert_step(2 * p + 1, False, False, p + 1)
                expert_step(2 * p + 2, True, False, p + 2)
            expert_step(NE - 1, False, True, NE // 2)

            for half in range(2):
                act.wait_ge(gT_psum, half + 1)
                copy(gT[:, half * HALF:(half + 1) * HALF], (ps_h1, ps_h2)[half][0][0:E + 1, :]).then_inc(gT_sbuf, 1)

        @block.vector
        def _(dve):
            V = nc.vector
            links = [0]

            def chain(ins):
                links[0] += 1
                ins.then_inc(dve_chain, 1)
                dve.wait_ge(dve_chain, links[0])

            def split(hi, lo, raw, in_sem, in_count, hi_sem, done_sem, count):
                dve.wait_ge(in_sem, in_count)
                V.tensor_copy(hi, raw).then_inc(hi_sem, 1)
                dve.wait_ge(hi_sem, count)
                V.tensor_tensor(lo, raw, hi, ALU.subtract).then_inc(done_sem, 1)

            def tokens_lo(t, n):
                dve.wait_ge(xT_hi_done, n + 1)
                tok = slice(t * P, (t + 1) * P)
                V.tensor_tensor(xT_lo[:, :, tok], ps_turn[t % 2][:].rearrange("p (c k) -> p c k", c=C),
                                xT_hi[:, :, tok], ALU.subtract).then_inc(xT_split, 1)

            for c in range(C):
                dve.wait_ge(ctx_hi_done, c + 1)
                V.tensor_tensor(ctx_lo[:, c], ctx_raw[:, c], ctx_hi[:, c], ALU.subtract).then_inc(ctx_split, 1)
            split(wv_hi[:], wv_lo[:], wv_raw[:], wv_in, 16, wv_hi_done, wv_split, 1)

            for t in range(B):
                dve.wait_ge(x_in[t], 16)
                last = V.bn_stats(stats[:, t], acc[:, t])
            chain(last)
            for t in range(B):
                last = V.bn_aggr(mean_var[:, t], stats[:, t])
            chain(last)
            V.tensor_scalar(rstd[:], mean_var[:, :, 1], EPS, None, ALU.add).then_inc(var_ready, 1)
            dve.wait_ge(rstd_ready, 1)
            for t in range(B):
                last = V.tensor_scalar(acc[:, t], acc[:, t], mean_var[:, t, 0:1], rstd[:, t:t + 1],
                                       ALU.subtract, ALU.mult)
            chain(last)
            for t in range(B):
                chain(V.tensor_tensor_reduce(sq_scratch[:], acc[:, t], acc[:, t], 1.0, 0.0, ALU.mult, ALU.add,
                                             mean_sq[:, t:t + 1]))
            V.tensor_scalar(rms[:], mean_sq[:], 1.0 / D, EPS, ALU.mult, ALU.add).then_inc(var_ready, 1)
            dve.wait_ge(rstd_ready, 2)
            dve.wait_ge(lnw_in, 16)
            for t in range(B):
                V.scalar_tensor_tensor(out=xn[:, t], in0=acc[:, t], scalar=rms[:, t:t + 1], in1=lnw_s[:],
                                       op0=ALU.mult, op1=ALU.mult).then_inc(xn_ready, 1)
            split(wqk_hi[:, 0], wqk_lo[:, 0], wqk_raw[:, 0], wqk_in[0], 16, wqk_hi_done, wqk_split, 1)

            dve.wait_ge(mask_in, 16)
            V.tensor_scalar(mask_bias[:], mask_u8[:], -1.0, BIG, ALU.add, ALU.mult).then_inc(mask_done, 1)
            dve.wait_ge(mask_done, 1)
            chain(V.tensor_reduce(any_mask[:], mask_bias[:], AX.X, ALU.max))
            chain(V.tensor_scalar(any_mask[:], any_mask[:], -1.0, None, ALU.is_ge))
            for t in range(B):
                tokens_lo(t, t)

            def bias_and_max(i):
                dve.wait_ge(bias_ready, i + 1)
                for half in range(2):
                    dve.wait_ge(score_psum, 2 * i + 1 + half)
                    V.tensor_tensor(probs[:, half], ps_score[half][:].rearrange("p (b k) -> p b k", b=BH),
                                    score_bias[:, BH * half:BH * (half + 1)], ALU.add).then_inc(score_biased, 1)
                for half in range(2):
                    dve.wait_ge(score_biased, 2 * i + 1 + half)
                    V.tensor_reduce(neg_max[:, half], probs[:, half], AX.X, ALU.max, negate=True).then_inc(max_done, 1)

            def normalise(i, count):
                for half in range(2):
                    dve.wait_ge(exp_done, 2 * i + 1 + half)
                    V.reciprocal(row_inv[:, half], row_sum[:, half]).then_inc(count, 1)
                    dve.wait_ge(count, 4 * i + 2 * half + 1)
                    V.tensor_tensor(row_scale[:, half], row_inv[:, half], any_mask[:, BH * half:BH * (half + 1)],
                                    ALU.mult).then_inc(count, 1)
                    dve.wait_ge(count, 4 * i + 2 * half + 2)
                    V.tensor_tensor(probs[:, half], probs[:, half],
                                    row_scale[:, half].unsqueeze(2).broadcast_to([P, BH, P]),
                                    ALU.mult).then_inc(probs_ready, 1)

            def take_attn_lo(i, slot):
                for half in range(2):
                    dve.wait_ge(attn_hi_done, 2 * i + 1 + half)
                    tok = slice(half * HALF, (half + 1) * HALF)
                    V.tensor_tensor(attn_lo[:, slot, tok], ps_attn[half][:], attn_hi[:, slot, tok],
                                    ALU.subtract).then_inc(attn_split, 1)

            def add_out(g, t):
                dve.wait_ge(o_psum, B * g + t + 1)
                return V.tensor_tensor(acc[:, t], ps_job[t % 2][:], acc[:, t], ALU.add)

            def head_step(g, j, first):
                i = G * g + j
                before = not (first and j == 0)
                if before:
                    bias_and_max(i - 1)
                if j == 0 and not first:
                    split(wv_hi[:], wv_lo[:], wv_raw[:], wv_in, 16 * (g + 1), wv_hi_done, wv_split, g + 1)
                if j == 1 and not first:
                    for t in range(B):
                        add_out(g - 1, t).then_inc(o_added, 1)
                n = (j + 1) % 2
                if before:
                    normalise(i - 1, row_scaled)
                split(wqk_hi[:, n], wqk_lo[:, n], wqk_raw[:, n], wqk_in[n], 16 * (2 * g + (j + 1) // 2 + 1),
                      wqk_hi_done, wqk_split, i + 2)
                if j == 3:
                    split(wo_hi[:], wo_lo[:], wo_raw[:], wo_in, 16 * (g + 1), wo_hi_done, wo_split, g + 1)
                if before:
                    take_attn_lo(i - 1, (j - 1) % G)

            for j in range(G):
                head_step(0, j, True)
            with dve.Fori(1, NG) as g:
                for j in range(G):
                    head_step(g, j, False)
            bias_and_max(H - 1)
            normalise(H - 1, row_scaled)
            take_attn_lo(H - 1, G - 1)

            dve.wait_ge(gain_done, 1)
            dve.wait_ge(x_res_in, 16)

            def w12_lo_part(buf, count):
                dve.wait_ge(w12_hi_done, count)
                V.tensor_tensor(w12_lo[buf][:].rearrange("p w c k -> p (w c k)"), w12_raw[buf][:, 0:W12],
                                w12_hi[buf][:].rearrange("p w c k -> p (w c k)"), ALU.subtract).then_inc(w12_split, 1)

            w12_lo_part(0, 1)
            dve.wait_ge(rw_in, 16)
            chain(V.tensor_copy(rw_hi[:], rw_raw[:]))
            V.tensor_tensor(rw_lo[:], rw_raw[:], rw_hi[:], ALU.subtract).then_inc(rw_split, 1)

            def normalise_x2(t):
                dve.wait_ge(rstd_ready, 3 + t)
                V.tensor_scalar(x2n[:, t], acc[:, t], mean_var[:, t, 0:1], rstd[:, t:t + 1],
                                ALU.subtract, ALU.mult).then_inc(xn_ready, 1)

            for t in range(B):
                add_out(NG - 1, t).then_inc(o_added, 1)
                dve.wait_ge(o_added, B * (NG - 1) + t + 1)
                chain(V.scalar_tensor_tensor(out=acc[:, t], in0=acc[:, t], scalar=gain[:, 0:1], in1=x_res[:, t],
                                             op0=ALU.mult, op1=ALU.add))
                chain(V.bn_stats(stats[:, t], acc[:, t]))
                chain(V.bn_aggr(mean_var[:, t], stats[:, t]))
                V.tensor_scalar(rstd[:, t:t + 1], mean_var[:, t, 1:2], EPS, None, ALU.add).then_inc(var_ready, 1)
                if t >= 1:
                    normalise_x2(t - 1)
                if t >= 3:
                    tokens_lo(t - 3, B + t - 3)
            normalise_x2(B - 1)
            for t in range(B - 3, B):
                tokens_lo(t, B + t)

            def along(a, n):
                return a.unsqueeze(2).broadcast_to([P, B, n])

            def pick_first(src, rank, tiles, ones, n):
                chain(V.tensor_reduce(ones[0][:], src[:], AX.X, ALU.max))
                chain(V.tensor_tensor(tiles[0][:], src[:], along(ones[0][:], n), ALU.is_equal))
                chain(V.tensor_tensor(tiles[1][:], tiles[0][:], rank, ALU.mult))
                chain(V.tensor_reduce(ones[1][:], tiles[1][:], AX.X, ALU.max))
                chain(V.tensor_tensor(tiles[2][:], tiles[1][:], along(ones[1][:], n), ALU.is_equal))
                return tiles[2]

            def pick_two(src, less, rank, tiles, ones, n):
                one = pick_first(src, rank, tiles[0:3], ones[0:2], n)
                chain(V.scalar_tensor_tensor(out=less[:], in0=one[:], scalar=-BIG, in1=src[:],
                                             op0=ALU.mult, op1=ALU.add))
                two = pick_first(less, rank, tiles[3:6], ones[2:4], n)
                chain(V.tensor_tensor(tiles[6][:], one[:], two[:], ALU.add))
                return tiles[6]

            logits, shifted = rt[0], rt[1]
            dve.wait_ge(logits_psum, 1)
            dve.wait_ge(rb_in, 16)
            V.tensor_tensor(logits[:], ps_score[0][:, 0:B * E].rearrange("p (t e) -> p t e", t=B),
                            rb_s[:, 0].unsqueeze(1).broadcast_to([P, B, E]), ALU.add).then_inc(logits_read, 1)
            dve.wait_ge(logits_read, 1)
            chain(V.tensor_reduce(r1[0][:], logits[:], AX.X, ALU.max))
            V.tensor_tensor(shifted[:], logits[:], along(r1[0][:], E), ALU.subtract).then_inc(router_in, 1)
            dve.wait_ge(rank_done, 2)
            rank = rt[2]
            chain(V.tensor_copy(rank[:], rank_i[:]))
            dve.wait_ge(router_exp, 1)
            chain(V.tensor_reduce(r1[1][:], shifted[:], AX.X, ALU.add))
            chain(V.reciprocal(r1[2][:], r1[1][:]))
            chain(V.tensor_tensor(shifted[:], shifted[:], along(r1[2][:], E), ALU.mult))
            scores = rt[0]
            chain(V.tensor_tensor(scores[:], shifted[:], rb_s[:, 1].unsqueeze(1).broadcast_to([P, B, E]), ALU.add))
            chain(V.tensor_reduce(rg[0][:], scores[:].rearrange("p t (g m) -> p t g m", g=EG), AX.X, ALU.max))
            keep = pick_two(rg[0], rg[1], rank[:, :, 0:EG], rg[2:9], r1[3:7], EG)
            chain(V.tensor_scalar(rg[9][:], keep[:], -1.0, BIG, ALU.add, ALU.mult))
            kept = rt[1]
            chain(V.tensor_tensor(kept[:].rearrange("p t (g m) -> p (t g) m", g=EG),
                                  scores[:].rearrange("p t (g m) -> p (t g) m", g=EG),
                                  rg[9][:].rearrange("p t g -> p (t g)").unsqueeze(2).broadcast_to([P, B * EG, EM]),
                                  ALU.add))
            chosen = pick_two(kept, rt[9], rank[:], [rt[3], rt[4], rt[5], rt[6], rt[7], rt[8], rt[3]], r1[3:7], E)
            V.tensor_tensor(gates[:, SH:NE, :].rearrange("p e t -> p t e"), chosen[:], scores[:],
                            ALU.mult).then_inc(gates_done, 1)
            dve.wait_ge(gates_done, 1)

            def gate_h(e, now, half):
                dve.wait_ge(h_psum, 4 * e + 2 * half + 2)
                dve.wait_ge(silu_done, 2 * e + half + 1)
                V.scalar_tensor_tensor(out=hT[:, half], in0=ps_h2[half][:], scalar=w12_raw[now][:, W12 + 1:W12 + 2],
                                       in1=silu[:, half], op0=ALU.add, op1=ALU.mult).then_inc(h_gated, 1)

            def h_lo(e, now, half):
                dve.wait_ge(h_hi_done, 2 * e + half + 1)
                tok = slice(half * HALF, (half + 1) * HALF)
                V.tensor_tensor(hT_lo[now][:, tok], hT[:, half], hT_hi[now][:, tok], ALU.subtract).then_inc(h_split, 1)

            def add_y(e, then, t, first):
                dve.wait_ge(y_psum, B * e + t + 1)
                gate = gate_now[then][:, t:t + 1]
                if first:
                    V.tensor_scalar(y_acc[:, t], ps_y[t % 4][:], gate, None, ALU.mult).then_inc(y_added, 1)
                else:
                    V.scalar_tensor_tensor(out=y_acc[:, t], in0=ps_y[t % 4][:], scalar=gate, in1=y_acc[:, t],
                                           op0=ALU.mult, op1=ALU.add).then_inc(y_added, 1)

            def expert_step(e, even, first, last):
                now, then = (0, 1) if even else (1, 0)
                V.tensor_copy(gate_now[then][:], gates[:, e - 1, :]).then_inc(gate_copied, 1)
                dve.wait_ge(gate_copied, e)
                add_y(e - 1, then, 0, first)
                add_y(e - 1, then, 1, first)
                gate_h(e, now, 0)
                add_y(e - 1, then, 2, first)
                add_y(e - 1, then, 3, first)
                h_lo(e, now, 0)
                w3_lo_part(now, e + 1)
                if not last:
                    w12_lo_part(then, e + 2)
                add_y(e - 1, then, 4, first)
                add_y(e - 1, then, 5, first)
                gate_h(e, now, 1)
                add_y(e - 1, then, 6, first)
                add_y(e - 1, then, 7, first)
                h_lo(e, now, 1)

            def w3_lo_part(buf, count):
                dve.wait_ge(w3_hi_done, count)
                V.tensor_tensor(w3_lo[buf][:], w3_raw[buf][:], w3_hi[buf][:], ALU.subtract).then_inc(w3_split, 1)

            gate_h(0, 0, 0)
            h_lo(0, 0, 0)
            w3_lo_part(0, 1)
            w12_lo_part(1, 2)
            gate_h(0, 0, 1)
            h_lo(0, 0, 1)
            expert_step(1, False, True, False)
            expert_step(2, True, False, False)
            with dve.Fori(1, NE // 2 - 1) as p:
                expert_step(2 * p + 1, False, False, False)
                expert_step(2 * p + 2, True, False, False)
            expert_step(NE - 1, False, False, True)

            dve.wait_ge(y_added, B * (NE - 1))
            chain(V.tensor_scalar(gate_last[:], gates[:, NE - 1, :], gain[:, 1:2], None, ALU.mult))
            for t in range(B):
                dve.wait_ge(b3_psum, t + 1)
                V.tensor_tensor(y_acc[:, t], (ps_h1, ps_h2)[t % 2][0][:], y_acc[:, t], ALU.add).then_inc(b3_added, 1)
            for t in range(B):
                dve.wait_ge(b3_added, t + 1)
                last = V.scalar_tensor_tensor(out=acc[:, t], in0=y_acc[:, t], scalar=gain[:, 1:2], in1=acc[:, t],
                                              op0=ALU.mult, op1=ALU.add)
            chain(last)
            for t in range(B):
                dve.wait_ge(y_psum, B * (NE - 1) + t + 1)
                V.scalar_tensor_tensor(out=y_acc[:, t], in0=ps_y[t % 4][:], scalar=gate_last[:, t:t + 1],
                                       in1=acc[:, t], op0=ALU.mult, op1=ALU.add).then_inc(final_ready, 1)


def kernel(x, ctx_4096, mask_BxSxS2_bk0, g_xattn, g_ffn, L0_xattn_position_bias, L0_xattn_ln_weight,
           L0_xattn_w_q, L0_xattn_w_k, L0_xattn_w_v, L0_xattn_w_out, L0_ffn_router_w, L0_ffn_router_b,
           L0_ffn_router_bias, L0_ffn_ew1, L0_ffn_eb1, L0_ffn_ew2, L0_ffn_eb2, L0_ffn_ew3, L0_ffn_eb3,
           L0_ffn_sw1, L0_ffn_sb1, L0_ffn_sw2, L0_ffn_sb2, L0_ffn_sw3, L0_ffn_sb3):
    import numpy as np
    import concourse.bacc as bacc
    from concourse.bass_utils import run_bass_kernel_spmd as run

    def chunks(wT, width):
        return wT.reshape(C, P, -1, width).transpose(2, 1, 0, 3)

    wq = chunks(np.asarray(L0_xattn_w_q).T, P)
    wk = chunks(np.asarray(L0_xattn_w_k).T, P)
    wqk = np.stack([wq, wk], axis=2)
    wqk = np.concatenate([wqk, wqk[:1]])
    wv = chunks(np.asarray(L0_xattn_w_v).T, G * P)
    wo = np.asarray(L0_xattn_w_out).T.reshape(NG, G, P, D).transpose(0, 2, 1, 3)

    def expert_in(shared, routed):
        return np.concatenate([chunks(np.asarray(shared), P),
                               np.asarray(routed).reshape(E, C, P, P).transpose(0, 2, 1, 3)])

    def expert_bias(shared, routed):
        return np.concatenate([np.asarray(shared).reshape(SH, P), np.asarray(routed)])[:, :, None]

    w12 = np.concatenate([expert_in(L0_ffn_sw1, L0_ffn_ew1).reshape(NE, P, C * P),
                          expert_in(L0_ffn_sw2, L0_ffn_ew2).reshape(NE, P, C * P),
                          expert_bias(L0_ffn_sb1, L0_ffn_eb1), expert_bias(L0_ffn_sb2, L0_ffn_eb2)], axis=2)
    w3 = np.concatenate([np.asarray(L0_ffn_sw3).reshape(SH, P, D), np.asarray(L0_ffn_ew3)])
    arrays = {
        "x": np.asarray(x),
        "ctxT": np.asarray(ctx_4096).reshape(T, C, P).transpose(2, 1, 0),
        "mask": np.asarray(mask_BxSxS2_bk0),
        "gains": np.concatenate([np.asarray(g_xattn), np.asarray(g_ffn)]),
        "pbias": np.asarray(L0_xattn_position_bias),
        "lnw": np.asarray(L0_xattn_ln_weight),
        "wqk": wqk,
        "wv": wv,
        "wo": wo,
        "w12": w12,
        "w3": w3,
        "rw": np.asarray(L0_ffn_router_w).reshape(C, P, E).transpose(1, 0, 2),
        "rb": np.stack([np.asarray(L0_ffn_router_b), np.asarray(L0_ffn_router_bias)]),
        "b3": np.concatenate([np.asarray(L0_ffn_sb3)[None], np.asarray(L0_ffn_eb3)]),
    }
    nc = bacc.Bacc("TRN2", target_bir_lowering=False, num_devices=1)
    args = []
    for name in arrays:
        a = arrays[name] = np.ascontiguousarray(arrays[name])
        args.append(nc.dram_tensor(f"{name}_dram", a.shape, mybir.dt.from_np(a.dtype), kind="ExternalInput").ap())
    out = nc.dram_tensor("out_dram", (B, P, D), F32, kind="ExternalOutput").ap()
    build(nc, *args, out)
    result = run(nc, [{f"{name}_dram": a for name, a in arrays.items()}], core_ids=[0])
    return result.results[0]["out_dram"]
```

```python
from contextlib import ExitStack

import concourse.bass as bass
from concourse import mybir

F32 = mybir.dt.float32
F32R = mybir.dt.float32r
I32 = mybir.dt.int32
U8 = mybir.dt.uint8
ALU = mybir.AluOpType
ACT = mybir.ActivationFunctionType
AX = mybir.AxisListType

P = 128
B = 8
D = 512
C = D // P
T = B * P
H = 32
G = 4
NG = H // G
HALF = T // 2
BH = B // 2
E = 16
EG = 4
EM = E // EG
SH = 2
TOP = 2
NB = (TOP * T + E * (P - 1)) // P
NS = NB + 1
assert NS == H
W12 = 2 * C * P
EPS = 1e-5
BIG = 1e30


def need(eng, sem, count):
    if not isinstance(count, int) or count > 0:
        eng.wait_ge(sem, count)


def build(nc, x, ctxT, mask, gains, pbias, lnw, wqk, wv, wo, sw12, sw3, ew12, eb12, ew3, rw, rb, b3, out):
    with ExitStack() as stack:
        base = (nc.sbuf_base + 63) // 64 * 64
        top = [0]

        def place(name, shape, dtype, at=None):
            size = 1
            for n in shape[1:]:
                size *= n
            size = (size * (1 if dtype == U8 else 4) + 31) // 32 * 32
            if at is None:
                at, top[0] = top[0], top[0] + size
            return nc.alloc_sbuf_tensor_at(name, shape, dtype, offset=base + at)

        def room(size):
            at, top[0] = top[0], top[0] + size
            return at

        at_ctx_hi, at_ctx_lo = room(C * T * 4), room(C * T * 4)
        ctx_hi = place("ctx_hi", [P, C, T], F32R, at_ctx_hi)
        ctx_lo = place("ctx_lo", [P, C, T], F32R, at_ctx_lo)
        ctx_raw = place("ctx_raw", [P, C, T], F32, at_ctx_lo)
        at_wqk = room(4 * W12 * 4)
        wqk_hi = place("wqk_hi", [P, 2, 2, C, P], F32R, at_wqk)
        wqk_lo = place("wqk_lo", [P, 2, 2, C, P], F32R, at_wqk + 2 * W12 * 4)
        wqk_raw = place("wqk_raw", [P, 2, 2, C, P], F32, at_wqk + 2 * W12 * 4)
        at_wv = room(2 * C * D * 4)
        wv_hi = place("wv_hi", [P, C, D], F32R, at_wv)
        wv_lo = place("wv_lo", [P, C, D], F32R, at_wv + C * D * 4)
        wv_raw = place("wv_raw", [P, C, D], F32, at_wv + C * D * 4)
        at_xT = room(2 * C * T * 4)
        xT_hi = place("xT_hi", [P, C, T], F32R, at_xT)
        xT_lo = place("xT_lo", [P, C, T], F32R, at_xT + C * T * 4)
        acc = place("acc", [P, B, D], F32)
        at_wo = room(2 * G * D * 4)
        wo_hi = place("wo_hi", [P, G, D], F32R, at_wo)
        wo_lo = place("wo_lo", [P, G, D], F32R, at_wo + G * D * 4)
        wo_raw = place("wo_raw", [P, G, D], F32, at_wo + G * D * 4)
        at_v = room(B * G * P * 4)
        v_s = place("v_s", [P, B, G * P], F32, at_v)
        at_attn = room(2 * G * T * 4)
        attn_hi = place("attn_hi", [P, G, T], F32R, at_attn)
        attn_lo = place("attn_lo", [P, G, T], F32R, at_attn + G * T * 4)
        at_qk = room(2 * T * 4)
        qT = place("qT", [P, T], F32, at_qk)
        kT = place("kT", [P, T], F32, at_qk + T * 4)
        at_s = room(T * 4)
        probs = place("probs", [P, 2, BH, P], F32, at_s)
        at_pT = room(T * 4)
        pT = place("pT", [P, 2, HALF], F32, at_pT)
        mask_bias = place("mask_bias", [P, B, P], F32)
        score_bias = place("score_bias", [P, B, P], F32)
        pos_bias = place("pos_bias", [P, 2, P], F32)
        at_end_scores = top[0]
        ident = place("ident", [P, P], F32)
        gain = place("gain", [P, 2], F32)
        any_mask = place("any_mask", [P, B], F32)
        neg_max = place("neg_max", [P, 2, BH], F32)
        row_sum = place("row_sum", [P, 2, BH], F32)
        row_inv = place("row_inv", [P, 2, BH], F32)
        row_scale = place("row_scale", [P, 2, BH], F32)
        stats = place("stats", [P, B, 6], F32)
        mean_var = place("mean_var", [P, B, 2], F32)
        rstd = place("rstd", [P, B], F32)
        neg_mean = place("neg_mean", [P, B], F32)
        shift = place("shift", [P, B], F32)
        rms_scale = place("rms_scale", [P, B], F32)
        rms_shift = place("rms_shift", [P, B], F32)
        rms = place("rms", [P, B], F32)
        minus_half = place("minus_half", [P, B], F32)
        zeros = place("zeros", [P, D], F32)
        ones = place("ones", [P, P], F32)
        before = place("before", [P, P], F32)
        rw_raw = place("rw_raw", [P, C, E], F32)
        rw_hi = place("rw_hi", [P, C, E], F32R)
        rw_lo = place("rw_lo", [P, C, E], F32R)
        rb_s = place("rb_s", [P, 2, E], F32)
        assert base + top[0] <= nc.sbuf_usable_end, top[0]

        mask_u8 = place("mask_u8", [P, B, P], U8, at_s)
        lnw_s = place("lnw_s", [P, D], F32, at_pT + D * 4)
        xn = place("xn", [P, B, D], F32, at_attn)
        x2n = place("x2n", [P, B, D], F32, at_v)
        x_res = place("x_res", [P, B, D], F32, at_wv)
        w12_hi, w12_lo, w12_raw, w3_hi, w3_lo, w3_raw = [], [], [], [], [], []
        for n in range(SH):
            at = at_qk + n * (2 * W12 + 8 + 2 * D) * 4
            w12_hi.append(place(f"w12_hi{n}", [P, 2, C, P], F32R, at))
            w12_lo.append(place(f"w12_lo{n}", [P, 2, C, P], F32R, at + W12 * 4))
            w12_raw.append(place(f"w12_raw{n}", [P, W12 + 2], F32, at + W12 * 4))
            at += (2 * W12 + 8) * 4
            w3_hi.append(place(f"w3_hi{n}", [P, D], F32R, at))
            w3_lo.append(place(f"w3_lo{n}", [P, D], F32R, at + D * 4))
            w3_raw.append(place(f"w3_raw{n}", [P, D], F32, at + D * 4))
        assert at + 2 * D * 4 <= at_end_scores
        hT_hi = [place(f"hT_hi{n}", [P, T], F32R, at_attn + n * T * 4) for n in range(SH)]
        hT_lo = [place(f"hT_lo{n}", [P, T], F32R, at_attn + (SH + n) * T * 4) for n in range(SH)]
        silu = place("silu", [P, 2, HALF], F32, at_attn + 2 * SH * T * 4)
        hT = place("hT", [P, 2, HALF], F32, at_attn + (2 * SH + 1) * T * 4)
        b3_s = place("b3_s", [E + 1, D], F32, at_attn + (2 * SH + 2) * T * 4)
        logitsT = place("logitsT", [E, T], F32, at_attn + (2 * SH + 2) * T * 4 + D * 4)
        gT = place("gT", [E + 1, T], F32, at_attn + (2 * SH + 2) * T * 4 + D * 4)
        assert at_ctx_hi + E * W12 * 4 <= at_xT
        ew12_s = place("ew12_s", [P, E, C, 2 * P], F32, at_ctx_hi)
        cursor = [at_xT]

        def two(name, cols):
            at, cursor[0] = cursor[0], cursor[0] + 2 * cols * 4
            return [place(f"{name}{n}", [P, cols], F32, at + n * cols * 4) for n in range(2)]

        xb, xbT, w3b, y_out = two("xb", D), two("xbT", D), two("w3b", D), two("y_out", D)
        bias_b, h_b, silu_b, h_gate_b, hT_b = (two("bias_b", 2 * P), two("h_b", 2 * P), two("silu_b", P),
                                               two("h_gate_b", P), two("hT_b", P))
        assert cursor[0] <= at_xT + 2 * C * T * 4
        y_pick = place("y_pick", [P, TOP, B, D], F32, at_ctx_hi)
        cursor = [at_wo]

        def small(name, shape, dtype=F32):
            size = 4
            for n in shape[1:]:
                size *= n
            at, cursor[0] = cursor[0], cursor[0] + (size + 31) // 32 * 32
            return place(name, shape, dtype, at)

        gates = small("gates", [P, 1 + E, B])
        rt = [small(f"rt{n}", [P, B, E]) for n in range(11)]
        rg = [small(f"rg{n}", [P, B, EG]) for n in range(10)]
        r1 = [small(f"r1_{n}", [P, B]) for n in range(7)]
        rank_i = small("rank_i", [P, B, E], I32)
        cum = small("cum", [P, B + 1, E])
        blocks_i = small("blocks_i", [P, E], I32)
        scan = [small(f"scan{n}", [P, E // 2 + E]) for n in range(2)]
        nblocks = small("nblocks", [P, E])
        first_slot = small("first_slot", [P, E])
        slot_f = [small(f"slot_f{n}", [P, B]) for n in range(TOP)]
        slot_i = [small(f"slot_i{n}", [P, B], I32) for n in range(TOP)]
        gate_f = [small(f"gate_f{n}", [P, B]) for n in range(TOP)]
        block_no_i = small("block_no_i", [1, NS], I32)
        block_no = small("block_no", [1, NS])
        ended = small("ended", [1, NS, E])
        owner_f = small("owner_f", [1, NS])
        owner = small("owner", [1, NS], I32)
        assert cursor[0] <= at_wo + 2 * G * D * 4

        def bank(name):
            return stack.enter_context(nc.psum_tensor(name, [P, D], F32))

        ps_job = [bank("ps_job0"), bank("ps_job1")]
        ps_score = [bank("ps_score0"), bank("ps_score1")]
        ps_turn = [bank("ps_turn0"), bank("ps_turn1")]
        ps_attn = [bank("ps_attn0"), bank("ps_attn1")]
        ps_first_v = ps_turn + ps_job + ps_score + ps_attn
        ps_out = ps_job + ps_score
        ps_h1 = [ps_job[0], ps_attn[0]]
        ps_h2 = [ps_job[1], ps_attn[1]]

        x_slots = nc.dram_tensor("x_slots", (NS * P, D), F32, kind="Internal").ap()
        y_slots = nc.dram_tensor("y_slots", (NB * P, D), F32, kind="Internal").ap()
        x_slot_blocks = x_slots.rearrange("(b p) d -> b p d", p=P)
        y_slot_blocks = y_slots.rearrange("(b p) d -> b p d", p=P)

        def sem(name):
            return stack.enter_context(nc.semaphore(name))

        ctx_in = [sem(f"ctx_in{c}") for c in range(C)]
        x_in = [sem(f"x_in{t}") for t in range(B)]
        mask_in, gain_in, lnw_in, wv_in, wo_in = map(sem, ("mask_in", "gain_in", "lnw_in", "wv_in", "wo_in"))
        wqk_in = [sem("wqk_in0"), sem("wqk_in1")]
        pos_in = [sem("pos_in0"), sem("pos_in1")]
        x_res_in, rw_in, rb_in, b3_in = map(sem, ("x_res_in", "rw_in", "rb_in", "b3_in"))
        w12_in = [sem("w12_in0"), sem("w12_in1")]
        w3_in = [sem("w3_in0"), sem("w3_in1")]
        ew12_in = sem("ew12_in")
        xb_in = [sem("xb_in0"), sem("xb_in1")]
        w3b_in = [sem("w3b_in0"), sem("w3b_in1")]
        bias_b_in = [sem("bias_b_in0"), sem("bias_b_in1")]
        cleared, scattered = sem("cleared"), sem("scattered")
        y_stored = [sem("y_stored0"), sem("y_stored1")]
        y_pick_in = [sem(f"y_pick_in{t}") for t in range(B)]
        ctx_hi_done, ctx_split = sem("ctx_hi_done"), sem("ctx_split")
        wqk_hi_done, wqk_split = sem("wqk_hi_done"), sem("wqk_split")
        wv_hi_done, wv_split = sem("wv_hi_done"), sem("wv_split")
        wo_hi_done, wo_split = sem("wo_hi_done"), sem("wo_split")
        w12_hi_done, w12_split = sem("w12_hi_done"), sem("w12_split")
        w3_hi_done, w3_split = sem("w3_hi_done"), sem("w3_split")
        rw_split = sem("rw_split")
        x_normed, acc_scaled, residual_added, shift_ready, logits_copied, logitsT_psum = map(
            sem, ("x_normed", "acc_scaled", "residual_added", "shift_ready", "logits_copied", "logitsT_psum"))
        ident_done, mask_done, gain_done = sem("ident_done"), sem("mask_done"), sem("gain_done")
        rank_done, rms_ready, ln_ready = map(sem, ("rank_done", "rms_ready", "ln_ready"))
        var_ready, rstd_ready, half_done = sem("var_ready"), sem("rstd_ready"), sem("half_done")
        xn_ready, xT_psum, xT_hi_done, xT_split = map(sem, ("xn_ready", "xT_psum", "xT_hi_done", "xT_split"))
        qk_psum, qk_sbuf, v_psum, v_sbuf = map(sem, ("qk_psum", "qk_sbuf", "v_psum", "v_sbuf"))
        o_psum, o_added = sem("o_psum"), sem("o_added")
        bias_ready, score_psum, score_biased, max_done, exp_done = map(
            sem, ("bias_ready", "score_psum", "score_biased", "max_done", "exp_done"))
        row_scaled = sem("row_scaled")
        probs_ready, pT_psum, pT_sbuf, attn_psum, attn_hi_done, attn_split = map(
            sem, ("probs_ready", "pT_psum", "pT_sbuf", "attn_psum", "attn_hi_done", "attn_split"))
        logits_psum, logits_read, router_in, router_exp, gates_done = map(
            sem, ("logits_psum", "logits_read", "router_in", "router_exp", "gates_done"))
        h_psum, silu_done, h_gated, h_hi_done, h_split = map(
            sem, ("h_psum", "silu_done", "h_gated", "h_hi_done", "h_split"))
        gT_psum, gT_sbuf, shared_psum, shared_added = map(
            sem, ("gT_psum", "gT_sbuf", "shared_psum", "shared_added"))
        const_done, counts_ready, rank_psum, slots_ready, owner_ready = map(
            sem, ("const_done", "counts_ready", "rank_psum", "slots_ready", "owner_ready"))
        xbT_psum, xbT_sbuf, hb_psum, hb_biased, silu_b_done, hb_gated, hbT_psum, hbT_sbuf, yb_psum, yb_sbuf = map(
            sem, ("xbT_psum", "xbT_sbuf", "hb_psum", "hb_biased", "silu_b_done", "hb_gated", "hbT_psum",
                  "hbT_sbuf", "yb_psum", "yb_sbuf"))
        final_ready, stored = sem("final_ready"), sem("stored")
        dve_chain = sem("dve_chain")

        block = stack.enter_context(nc.Block())

        def pair_loop(eng, step):
            step(0, 0, -1)
            step(1, 1, 0)
            step(2, 0, 0)
            with eng.Fori(1, NB // 2 - 2) as pair:
                step(2 * pair + 1, 1, pair)
                step(2 * pair + 2, 0, pair)
            for b in range(NB - 4, NB):
                step(b, b % 2, (b - 1) // 2)

        @block.sync
        def _(sp):
            for c in range(C):
                sp.dma_start(ctx_raw[:, c], ctxT[:, c]).then_inc(ctx_in[c], 16)
                sp.dma_start(wv_raw[:, c], wv[0, :, c]).then_inc(ctx_in[c], 16)
            for t in range(B):
                sp.dma_start(acc[:, t], x[t]).then_inc(x_in[t], 16)
            sp.dma_start(wqk_raw[:, 0], wqk[0]).then_inc(wqk_in[0], 16)

            def load_step(g, j, first):
                i = G * g + j
                if j == 0 and not first:
                    need(sp, v_psum, B * g)
                    sp.dma_start(wv_raw[:], wv[g]).then_inc(wv_in, 16)
                need(sp, bias_ready, i - 1)
                sp.dma_start(pos_bias[:, j % 2], pbias[i]).then_inc(pos_in[j % 2], 16)
                need(sp, qk_psum, 4 * i)
                sp.dma_start(wqk_raw[:, (j + 1) % 2], wqk[i + 1]).then_inc(wqk_in[(j + 1) % 2], 16)
                sp.dma_start(x_slot_blocks[i], zeros[:]).then_inc(cleared, 16)
                if j == 2:
                    need(sp, o_psum, B * g)
                    sp.dma_start(wo_raw[:], wo[g]).then_inc(wo_in, 16)

            sp.dma_start(rw_raw[:], rw).then_inc(rw_in, 16)
            sp.dma_start(rb_s[:], rb.partition_broadcast(P)).then_inc(rb_in, 16)
            sp.wait_ge(const_done, 1)
            for j in range(G):
                load_step(0, j, True)
            with sp.Fori(1, NG) as g:
                for j in range(G):
                    load_step(g, j, False)

            sp.wait_ge(v_psum, B * NG)
            sp.dma_start(x_res[:], x.rearrange("t p d -> p t d")).then_inc(x_res_in, 16)
            sp.wait_ge(attn_psum, 2 * H)
            for n in range(SH):
                sp.dma_start(w12_raw[n][:], sw12[n]).then_inc(w12_in[n], 16)
                sp.dma_start(w3_raw[n][:], sw3[n]).then_inc(w3_in[n], 16)
            sp.wait_ge(wqk_split, H + 1)
            sp.wait_ge(residual_added, B)
            for n in range(0, E, E // 4):
                sp.dma_start(ew12_s[:, n:n + E // 4], ew12[n:n + E // 4].rearrange("e p c k -> p e c k"))\
                  .then_inc(ew12_in, 16)
            sp.wait_ge(o_psum, B * NG)
            sp.dma_start(b3_s[:], b3).then_inc(b3_in, 16)

            def load_x(b, k):
                sp.dma_start(xb[k][:], x_slot_blocks[b]).then_inc(xb_in[k], 16)

            def owner_of(b):
                return sp.value_load(owner[0:1, bass.ds(b, 1)], min_val=0, max_val=E - 1)

            def load_bias(e, k):
                sp.dma_start(bias_b[k][:], eb12[e].partition_broadcast(P)).then_inc(bias_b_in[k], 16)

            def load_w3(e, k):
                sp.dma_start(w3b[k][:], ew3[e]).then_inc(w3b_in[k], 16)

            def store_y(b, k):
                sp.wait_ge(yb_sbuf, b + 1)
                sp.dma_start(y_slot_blocks[b], y_out[k][:]).then_inc(y_stored[k], 16)

            def block_step(b, k, pair):
                static = isinstance(b, int)
                more = not (static and b + 1 >= NB)
                if more:
                    e = owner_of(b + 1)
                    need(sp, hb_biased, b)
                    load_bias(e, 1 - k)
                if not (static and b + 4 >= NB):
                    sp.wait_ge(xbT_psum, b + 3)
                    load_x(b + 4, k)
                if more:
                    need(sp, yb_psum, b)
                    load_w3(e, 1 - k)
                if not (static and b == 0):
                    store_y(b - 1, 1 - k)

            sp.wait_ge(h_psum, 4 * SH)
            sp.wait_ge(owner_ready, 1)
            e_first = owner_of(0)
            load_bias(e_first, 0)
            load_w3(e_first, 0)
            sp.wait_ge(scattered, 16 * TOP * B)
            load_x(0, 0)
            load_x(1, 1)
            for k in range(2):
                sp.wait_ge(xbT_psum, k + 1)
                load_x(k + 2, k)
            pair_loop(sp, block_step)
            store_y(NB - 1, (NB - 1) % 2)

            for t in range(B):
                sp.wait_ge(final_ready, t + 1)
                sp.dma_start(out[t], y_pick[:, 1, t]).then_inc(stored, 16)
            sp.wait_ge(stored, 16 * B)

        @block.gpsimd
        def _(pool):
            nc.gpsimd.memset(ident[:], 0.0).then_inc(ident_done, 1)
            pool.wait_ge(ident_done, 1)
            nc.gpsimd.affine_select(out=ident[:], in_=ident[:], compare_op=ALU.not_equal, fill=1.0,
                                    base=0, pattern=[[-1, P]], channel_multiplier=1).then_inc(ident_done, 1)

            nc.gpsimd.memset(zeros[:], 0.0).then_inc(const_done, 1)
            nc.gpsimd.memset(ones[:], 1.0).then_inc(const_done, 1)
            nc.gpsimd.memset(before[:], 1.0).then_inc(const_done, 1)
            pool.wait_ge(const_done, 3)
            nc.gpsimd.affine_select(out=before[:], in_=before[:], compare_op=ALU.is_gt, fill=0.0,
                                    base=0, pattern=[[1, P]], channel_multiplier=-1).then_inc(const_done, 1)
            nc.gpsimd.memset(minus_half[:], -0.5).then_inc(half_done, 1)
            pool.wait_ge(half_done, 1)

            def to_minus_half(dst, src, count):
                pool.wait_ge(var_ready, count)
                nc.gpsimd.tensor_tensor(dst, src, minus_half[:, 0:src.shape[1]], ALU.pow).then_inc(rstd_ready, 1)

            to_minus_half(rstd[:], rstd[:], 1)
            to_minus_half(rms[:], rms[:], 2)

            def bias_step(g, j, first):
                i = G * g + j
                if first and j == 0:
                    pool.wait_ge(mask_done, 1)
                pool.wait_ge(pos_in[j % 2], 16 * (2 * g + j // 2 + 1))
                need(pool, score_biased, 2 * i)
                nc.gpsimd.tensor_tensor(score_bias[:], mask_bias[:],
                                        pos_bias[:, j % 2].unsqueeze(1).broadcast_to([P, B, P]),
                                        ALU.add).then_inc(bias_ready, 1)

            for j in range(G):
                bias_step(0, j, True)
            with pool.Fori(1, NG) as g:
                for j in range(G):
                    bias_step(g, j, False)

            pool.wait_ge(o_added, B * (NG - 1))
            pool.wait_ge(gain_done, 1)
            pool.wait_ge(x_res_in, 16)
            for t in range(B):
                nc.gpsimd.tensor_scalar(acc[:, t], acc[:, t], gain[:, 0:1], None, ALU.mult).then_inc(acc_scaled, 1)
                pool.wait_ge(acc_scaled, t + 1)
                nc.gpsimd.tensor_tensor(acc[:, t], acc[:, t], x_res[:, t], ALU.add).then_inc(residual_added, 1)

            for t in range(B):
                to_minus_half(rstd[:, t:t + 1], rstd[:, t:t + 1], 3 + t)
                pool.wait_ge(rstd_ready, 3 + t)
                nc.gpsimd.tensor_tensor(shift[:, t:t + 1], neg_mean[:, t:t + 1], rstd[:, t:t + 1],
                                        ALU.mult).then_inc(shift_ready, 1)

            pool.wait_ge(o_psum, B * NG)
            nc.gpsimd.iota(rank_i[:], pattern=[[0, B], [-1, E]], base=E, channel_multiplier=0).then_inc(rank_done, 1)
            nc.gpsimd.iota(block_no_i[:], pattern=[[1, NS]], base=0, channel_multiplier=0).then_inc(rank_done, 1)
            nc.gpsimd.memset(gates[:, 0:1, :], 1.0).then_inc(rank_done, 1)
            for n in range(2):
                nc.gpsimd.memset(scan[n][:, 0:E // 2], 0.0).then_inc(rank_done, 1)
            nc.gpsimd.memset(cum[:, 0, :], 0.0).then_inc(rank_done, 1)

            pool.wait_ge(xn_ready, 2 * B)
            pool.wait_ge(cleared, 16 * NS)
            pool.wait_ge(slots_ready, 1)
            for t in range(B):
                for n in range(TOP):
                    nc.gpsimd.indirect_dma_start(
                        out=x_slots, out_offset=bass.IndirectOffsetOnAxis(ap=slot_i[n][:, t:t + 1], axis=0),
                        in_=x2n[:, t], in_offset=None, bounds_check=NB * P - 1, oob_is_err=False).then_inc(scattered, 16)
            pool.wait_ge(hb_psum, NB)
            for k in range(2):
                pool.wait_ge(y_stored[k], 16 * ((NB + 1 - k) // 2))
            for t in range(B):
                for n in range(TOP):
                    nc.gpsimd.indirect_dma_start(
                        out=y_pick[:, n, t], out_offset=None, in_=y_slots,
                        in_offset=bass.IndirectOffsetOnAxis(ap=slot_i[n][:, t:t + 1], axis=0),
                        bounds_check=NB * P - 1, oob_is_err=False).then_inc(y_pick_in[t], 16)

        @block.tensor
        def _(pe):
            def three(psum, pairs, closed=True):
                n = len(pairs)
                for k, (l_hi, l_lo, r_hi, r_lo) in enumerate(pairs):
                    nc.tensor.matmul(psum, l_lo, r_hi, start=(k == 0), stop=False)
                    nc.tensor.matmul(psum, l_hi, r_lo, start=False, stop=False)
                    last = nc.tensor.matmul(psum, l_hi, r_hi, start=False, stop=(closed and k == n - 1))
                return last

            def cols(t, w=P):
                return slice(t * w, (t + 1) * w)

            def turn_tokens(src, t):
                for c in range(C):
                    last = nc.tensor.transpose(ps_turn[t % 2][:, cols(c)], src[:, t, cols(c)], ident[:])
                last.then_inc(xT_psum, 1)

            def project_qk(g, j, which, half):
                hi, lo = (xT_hi, xT_lo) if which == 0 else (ctx_hi, ctx_lo)
                tok = cols(half, HALF)
                three(ps_job[half][:], [(wqk_hi[:, j % 2, which, c], wqk_lo[:, j % 2, which, c],
                                         hi[:, c, tok], lo[:, c, tok]) for c in range(C)]).then_inc(qk_psum, 1)

            def project_v(t):
                three(ps_job[t % 2][:], [(ctx_hi[:, c, cols(t)], ctx_lo[:, c, cols(t)], wv_hi[:, c], wv_lo[:, c])
                                         for c in range(C)]).then_inc(v_psum, 1)

            def project_out(t):
                three(ps_job[t % 2][:], [(attn_hi[:, s, cols(t)], attn_lo[:, s, cols(t)], wo_hi[:, s], wo_lo[:, s])
                                         for s in range(G)]).then_inc(o_psum, 1)

            def score(i):
                need(pe, qk_sbuf, 4 * i + 4)
                for half in range(2):
                    need(pe, score_biased, 2 * i - 1 + half)
                    for b in range(BH):
                        tok = cols(BH * half + b)
                        last = nc.tensor.matmul(ps_score[half][:, cols(b)], qT[:, tok], kT[:, tok], start=True, stop=True)
                    last.then_inc(score_psum, 1)

            def turn_probs(i):
                for half in range(2):
                    pe.wait_ge(probs_ready, 2 * i + 1 + half)
                    need(pe, pT_sbuf, 2 * i - 1 + half)
                    for b in range(BH):
                        last = nc.tensor.transpose(ps_turn[half][:, cols(b)], probs[:, half, b], ident[:])
                    last.then_inc(pT_psum, 1)

            def attend(i, slot):
                for half in range(2):
                    pe.wait_ge(pT_sbuf, 2 * i + 1 + half)
                    need(pe, attn_split, 2 * i - 1 + half)
                    for b in range(BH):
                        last = nc.tensor.matmul(ps_attn[half][:, cols(b)], v_s[:, BH * half + b, cols(slot)],
                                                pT[:, half, cols(b)], start=True, stop=True)
                    last.then_inc(attn_psum, 1)

            def head_step(g, j, first):
                i = G * g + j
                before = not (first and j == 0)
                if before:
                    score(i - 1)
                if j == 1 and not first:
                    pe.wait_ge(wo_split, g)
                    pe.wait_ge(attn_split, 2 * G * g)
                    for t in range(B):
                        if t < 2:
                            pe.wait_ge(v_sbuf, B * g + B - 1 + t)
                        else:
                            pe.wait_ge(o_added, B * (g - 1) + t - 1)
                        project_out(t)
                pe.wait_ge(wqk_split, i + 1)
                for half in range(2):
                    if j == 1 and not first:
                        pe.wait_ge(o_added, B * (g - 1) + B - 1 + half)
                    elif first and j == 0:
                        pe.wait_ge(v_sbuf, 3 + half)
                    else:
                        pe.wait_ge(qk_sbuf, 4 * (i - 1) + 3 + half)
                    project_qk(g, j, 1, half)
                    if first and j == 0:
                        for t in (2 * half, 2 * half + 1):
                            turn_when_free(t)
                if first and j == 0:
                    turn_when_free(4)
                    turn_when_free(5)
                    pe.wait_ge(xT_split, BH)
                pe.wait_ge(qk_sbuf, 4 * i + 1)
                project_qk(g, j, 0, 0)
                if first and j == 0:
                    turn_when_free(6)
                    turn_when_free(7)
                    pe.wait_ge(xT_split, B)
                if before:
                    turn_probs(i - 1)
                pe.wait_ge(qk_sbuf, 4 * i + 2)
                project_qk(g, j, 0, 1)
                if before:
                    if j == 1:
                        pe.wait_ge(v_sbuf, B * g + B)
                    attend(i - 1, (j - 1) % G)
                if j == 0 and not first:
                    pe.wait_ge(wv_split, C + g)
                    for t in range(B):
                        if t < 2:
                            pe.wait_ge(qk_sbuf, 4 * i + 3 + t)
                        else:
                            pe.wait_ge(v_sbuf, B * g + t - 1)
                        project_v(t)

            def turn_when_free(t):
                pe.wait_ge(xn_ready, t + 1)
                if t < 2:
                    pe.wait_ge(v_sbuf, t + 1)
                else:
                    pe.wait_ge(xT_split, t - 1)
                turn_tokens(xn, t)

            for c in range(C):
                pe.wait_ge(ctx_split, c + 1)
                pe.wait_ge(wv_split, c + 1)
                for t in range(B):
                    psum, lhs_hi, lhs_lo = ps_first_v[t][:], ctx_hi[:, c, cols(t)], ctx_lo[:, c, cols(t)]
                    nc.tensor.matmul(psum, lhs_lo, wv_hi[:, c], start=(c == 0), stop=False)
                    nc.tensor.matmul(psum, lhs_hi, wv_lo[:, c], start=False, stop=False)
                    last = nc.tensor.matmul(psum, lhs_hi, wv_hi[:, c], start=False, stop=(c == C - 1))
                    if c == C - 1:
                        last.then_inc(v_psum, 1)
            pe.wait_ge(ident_done, 2)
            for j in range(G):
                head_step(0, j, True)
            with pe.Fori(1, NG) as g:
                for j in range(G):
                    head_step(g, j, False)

            def out_part(t, heads):
                for s in heads:
                    psum = ps_out[t % 4][:]
                    nc.tensor.matmul(psum, attn_lo[:, s, cols(t)], wo_hi[:, s], start=(s == 0), stop=False)
                    nc.tensor.matmul(psum, attn_hi[:, s, cols(t)], wo_lo[:, s], start=False, stop=False)
                    last = nc.tensor.matmul(psum, attn_hi[:, s, cols(t)], wo_hi[:, s], start=False, stop=(s == G - 1))
                if s == G - 1:
                    last.then_inc(o_psum, 1)

            def out_ahead(t):
                if t < 2:
                    pe.wait_ge(qk_sbuf, 4 * (H - 1) + 3 + t)
                else:
                    pe.wait_ge(score_biased, 2 * (H - 1) + t - 1)
                out_part(t, range(G - 1))

            def turn_x2(t):
                pe.wait_ge(xn_ready, B + t + 1)
                if t < 2:
                    pe.wait_ge(pT_sbuf, 2 * H)
                else:
                    pe.wait_ge(xT_split, B + t - 1)
                turn_tokens(x2n, t)

            score(H - 1)
            pe.wait_ge(wo_split, NG)
            pe.wait_ge(attn_split, 2 * (H - 1))
            out_ahead(0)
            out_ahead(1)
            turn_probs(H - 1)
            out_ahead(2)
            attend(H - 1, G - 1)
            out_ahead(3)
            for t in range(4):
                pe.wait_ge(attn_split, 2 * H)
                out_part(t, [G - 1])
            for t in range(4, B):
                pe.wait_ge(o_added, B * (NG - 1) + t - 3)
                out_part(t, range(G))
                if t == 4:
                    turn_x2(0)
                turn_x2(t - 3)

            def shared_h(n, which, half):
                tok = cols(half, HALF)
                psum = (ps_h1, ps_h2)[which][half]
                if n:
                    pe.wait_ge((silu_done, h_gated)[which], half + 1)
                three(psum[:], [(w12_hi[n][:, which, c], w12_lo[n][:, which, c],
                                 xT_hi[:, c, tok], xT_lo[:, c, tok]) for c in range(C)]).then_inc(h_psum, 1)

            turn_x2(5)
            pe.wait_ge(w12_split, 1)
            pe.wait_ge(xT_split, B + 4)
            pe.wait_ge(o_added, B * (NG - 1) + 6)
            shared_h(0, 0, 0)
            turn_x2(6)
            shared_h(0, 1, 0)
            turn_x2(7)
            pe.wait_ge(rw_split, 1)
            pe.wait_ge(o_added, B * NG)
            for half in range(2):
                pe.wait_ge(xT_split, B + BH * (half + 1))
                tok = cols(half, HALF)
                three(ps_score[half][0:E, :], [(rw_hi[:, c], rw_lo[:, c], xT_hi[:, c, tok], xT_lo[:, c, tok])
                                               for c in range(C)]).then_inc(logitsT_psum, 1)
            shared_h(0, 0, 1)
            pe.wait_ge(logits_copied, 2)
            for t in range(B):
                last = nc.tensor.transpose(ps_score[0][:, cols(t, E)], logitsT[:, cols(t)], ident[0:E, 0:E])
            last.then_inc(logits_psum, 1)
            shared_h(0, 1, 1)
            pe.wait_ge(w12_split, 2)
            shared_h(1, 0, 0)
            shared_h(1, 1, 0)
            pe.wait_ge(const_done, 4)
            pe.wait_ge(counts_ready, 1)
            masks = rt[10]
            nc.tensor.matmul(ps_score[1][:, 0:B * E], before[:], masks[:].rearrange("p t e -> p (t e)"),
                             start=True, stop=False)
            nc.tensor.matmul(ps_score[1][:, 0:B * E], ones[:], cum[:, 0:B].rearrange("p t e -> p (t e)"),
                             start=False, stop=True)
            nc.tensor.matmul(ps_score[1][:, B * E:(B + 1) * E], ones[:], cum[:, B],
                             start=True, stop=True).then_inc(rank_psum, 1)
            shared_h(1, 0, 1)
            shared_h(1, 1, 1)
            pe.wait_ge(gates_done, 1)
            pe.wait_ge(logits_read, 1)
            for half in range(2):
                for b in range(BH):
                    last = nc.tensor.transpose((ps_score, ps_turn)[half][0][0:E + 1, cols(b)],
                                               gates[:, :, BH * half + b], ident[:])
                last.then_inc(gT_psum, 1)
            for n in range(SH):
                pe.wait_ge(w3_split, n + 1)
            for t in range(B):
                if t % 4 == 0:
                    pe.wait_ge(h_split, 2 * (SH - 1) + t // 4 + 1)
                if t < 2:
                    pe.wait_ge((silu_done, h_gated)[t], 2 * SH - 1)
                else:
                    pe.wait_ge(shared_added, t - 1)
                three(ps_job[t % 2][:], [(hT_hi[n][:, cols(t)], hT_lo[n][:, cols(t)], w3_hi[n][:], w3_lo[n][:])
                                         for n in range(SH)], closed=False)
                if t == 0:
                    pe.wait_ge(gT_sbuf, 2)
                    pe.wait_ge(b3_in, 16)
                nc.tensor.matmul(ps_job[t % 2][:], gT[:, cols(t)], b3_s[:], start=False, stop=True)\
                  .then_inc(shared_psum, 1)

            def turn_x(b, k, loads):
                pe.wait_ge(xb_in[k], 16 * loads)
                need(pe, xbT_sbuf, b - 1)
                for c in range(C):
                    last = nc.tensor.transpose(ps_turn[k][:, cols(c)], xb[k][:, cols(c)], ident[:])
                last.then_inc(xbT_psum, 1)

            def turn_h(b, k):
                pe.wait_ge(hb_gated, b + 1)
                need(pe, hbT_sbuf, b - 1)
                nc.tensor.transpose(ps_score[k][:, 0:P], h_gate_b[k][:], ident[:]).then_inc(hbT_psum, 1)

            def block_y(b, k, loads):
                pe.wait_ge(hbT_sbuf, b + 1)
                pe.wait_ge(w3b_in[k], 16 * loads)
                need(pe, yb_sbuf, b - 1)
                nc.tensor.matmul(ps_job[k][:], hT_b[k][:], w3b[k][:], start=True, stop=True).then_inc(yb_psum, 1)

            def block_step(b, k, pair):
                static = isinstance(b, int)
                later = not (static and b == 0)
                e = pe.value_load(owner[0:1, bass.ds(b, 1)], min_val=0, max_val=E - 1)
                pe.wait_ge(xbT_sbuf, b + 1)
                need(pe, hb_biased, b - 1)
                for c in range(C):
                    last = nc.tensor.matmul(ps_attn[k][:, 0:2 * P], xbT[k][:, cols(c)], ew12_s[:, e, c],
                                            start=(c == 0), stop=(c == C - 1))
                    if c == 1 and later:
                        turn_h(b - 1, 1 - k)
                last.then_inc(hb_psum, 1)
                if not (static and b + 2 >= NB):
                    turn_x(b + 2, k, pair + 2 + (1 - k))
                if later:
                    block_y(b - 1, 1 - k, pair + 1)

            pe.wait_ge(owner_ready, 1)
            pe.wait_ge(ew12_in, 16 * 4)
            turn_x(0, 0, 1)
            turn_x(1, 1, 1)
            pe.wait_ge(shared_added, B)
            pair_loop(pe, block_step)
            turn_h(NB - 1, 0)
            block_y(NB - 1, 0, NB // 2 + 1)

        @block.scalar
        def _(act):
            act.dma_start(gain[:], gains.partition_broadcast(P)).then_inc(gain_in, 16)
            act.dma_start(lnw_s[:], lnw.partition_broadcast(P)).then_inc(lnw_in, 16)
            act.dma_start(mask_u8[:], mask.rearrange("b q k -> q b k")).then_inc(mask_in, 16)

            def copy(dst, src):
                return nc.scalar.activation(dst, src, ACT.Copy)

            def tokens_hi(t, n):
                act.wait_ge(xT_psum, n + 1)
                copy(xT_hi[:, :, t * P:(t + 1) * P],
                     ps_turn[t % 2][:].rearrange("p (c k) -> p c k", c=C)).then_inc(xT_hi_done, 1)

            def exps(i, half):
                act.wait_ge(max_done, 2 * i + 1 + half)
                for b in range(BH):
                    last = nc.scalar.activation(probs[:, half, b], probs[:, half, b], ACT.Exp,
                                                bias=neg_max[:, half, b:b + 1],
                                                accum_out=row_sum[:, half, b:b + 1])
                last.then_inc(exp_done, 1)

            def take_qk(i, n, dst, half):
                act.wait_ge(qk_psum, 4 * i + n + 1)
                copy(dst[:, half * HALF:(half + 1) * HALF], ps_job[half][:]).then_inc(qk_sbuf, 1)

            def take_v(g, t):
                act.wait_ge(v_psum, B * g + t + 1)
                copy(v_s[:, t], ps_job[t % 2][:]).then_inc(v_sbuf, 1)

            def take_pT(i):
                for half in range(2):
                    act.wait_ge(pT_psum, 2 * i + 1 + half)
                    copy(pT[:, half], ps_turn[half][:]).then_inc(pT_sbuf, 1)

            def take_attn_hi(i, slot):
                for half in range(2):
                    act.wait_ge(attn_psum, 2 * i + 1 + half)
                    copy(attn_hi[:, slot, half * HALF:(half + 1) * HALF], ps_attn[half][:]).then_inc(attn_hi_done, 1)

            def scaled(dst, src, scale, shift):
                return nc.scalar.activation(dst, src, ACT.Identity, bias=shift, scale=scale)

            act.wait_ge(gain_in, 16)
            nc.scalar.activation(gain[:], gain[:], ACT.Tanh).then_inc(gain_done, 1)
            for c in range(C):
                act.wait_ge(ctx_in[c], 32)
                copy(ctx_hi[:, c], ctx_raw[:, c]).then_inc(ctx_hi_done, 1)
            act.wait_ge(rms_ready, 1)
            for t in range(B):
                scaled(xn[:, t], acc[:, t], rms_scale[:, t:t + 1], rms_shift[:, t:t + 1]).then_inc(x_normed, 1)

            def head_step(g, j, first):
                i = G * g + j
                before = not (first and j == 0)
                if before:
                    exps(i - 1, 0)
                take_qk(i, 0, kT, 0)
                if before:
                    exps(i - 1, 1)
                else:
                    tokens_hi(0, 0)
                    tokens_hi(1, 1)
                take_qk(i, 1, kT, 1)
                if not before:
                    for t in range(2, 6):
                        tokens_hi(t, t)
                take_qk(i, 2, qT, 0)
                if before:
                    take_pT(i - 1)
                else:
                    tokens_hi(6, 6)
                    tokens_hi(7, 7)
                take_qk(i, 3, qT, 1)
                if before:
                    take_attn_hi(i - 1, (j - 1) % G)
                if j == 0 and not first:
                    for t in range(B):
                        take_v(g, t)

            for t in range(B):
                act.wait_ge(v_psum, t + 1)
                copy(v_s[:, t], ps_first_v[t][:]).then_inc(v_sbuf, 1)
            for j in range(G):
                head_step(0, j, True)
                if j == 0:
                    for t in range(B):
                        scaled(acc[:, t], acc[:, t], rstd[:, t:t + 1], shift[:, t:t + 1]).then_inc(ln_ready, 1)
            with act.Fori(1, NG) as g:
                for j in range(G):
                    head_step(g, j, False)
            exps(H - 1, 0)
            exps(H - 1, 1)
            take_pT(H - 1)
            take_attn_hi(H - 1, G - 1)

            def split_w12(n):
                act.wait_ge(w12_in[n], 16)
                copy(w12_hi[n][:].rearrange("p w c k -> p (w c k)"), w12_raw[n][:, 0:W12]).then_inc(w12_hi_done, 1)

            def split_w3(n):
                act.wait_ge(w3_in[n], 16)
                copy(w3_hi[n][:], w3_raw[n][:]).then_inc(w3_hi_done, 1)

            def normalise_x2(t):
                act.wait_ge(shift_ready, t + 1)
                scaled(x2n[:, t], acc[:, t], rstd[:, t:t + 1], shift[:, t:t + 1]).then_inc(xn_ready, 1)

            for t in range(B):
                normalise_x2(t)
                if t >= 1:
                    tokens_hi(t - 1, B + t - 1)
                if t in (1, 3):
                    split_w12(t // 2)
                if t in (4, 5):
                    split_w3(t - 4)
            tokens_hi(B - 1, 2 * B - 1)
            for half in range(2):
                act.wait_ge(logitsT_psum, half + 1)
                copy(logitsT[:, half * HALF:(half + 1) * HALF], ps_score[half][0:E, :]).then_inc(logits_copied, 1)
            act.wait_ge(router_in, 1)
            nc.scalar.activation(rt[1][:], rt[1][:], ACT.Exp).then_inc(router_exp, 1)
            for n in range(SH):
                for half in range(2):
                    act.wait_ge(h_psum, 4 * n + 2 * half + 1)
                    nc.scalar.activation(silu[:, half], ps_h1[half][:], ACT.Silu,
                                         bias=w12_raw[n][:, W12:W12 + 1]).then_inc(silu_done, 1)
                    act.wait_ge(h_gated, 2 * n + half + 1)
                    copy(hT_hi[n][:, half * HALF:(half + 1) * HALF], hT[:, half]).then_inc(h_hi_done, 1)
            for half in range(2):
                act.wait_ge(gT_psum, half + 1)
                copy(gT[:, half * HALF:(half + 1) * HALF], (ps_score, ps_turn)[half][0][0:E + 1, :]).then_inc(gT_sbuf, 1)

            def take_xbT(b, k):
                act.wait_ge(xbT_psum, b + 1)
                copy(xbT[k][:], ps_turn[k][:]).then_inc(xbT_sbuf, 1)

            def take_y(b, k, stores):
                act.wait_ge(yb_psum, b + 1)
                need(act, y_stored[k], 16 * stores)
                copy(y_out[k][:], ps_job[k][:]).then_inc(yb_sbuf, 1)

            def block_step(b, k, pair):
                static = isinstance(b, int)
                act.wait_ge(hb_biased, b + 1)
                nc.scalar.activation(silu_b[k][:], h_b[k][:, 0:P], ACT.Silu).then_inc(silu_b_done, 1)
                if not (static and b + 2 >= NB):
                    take_xbT(b + 2, k)
                if not (static and b == 0):
                    take_y(b - 1, 1 - k, pair)

            take_xbT(0, 0)
            take_xbT(1, 1)
            pair_loop(act, block_step)
            take_y(NB - 1, 0, NB // 2)

        @block.vector
        def _(dve):
            V = nc.vector
            links = [0]

            def chain(ins):
                links[0] += 1
                ins.then_inc(dve_chain, 1)
                dve.wait_ge(dve_chain, links[0])

            def split(hi, lo, raw, in_sem, in_count, hi_sem, done_sem, count):
                dve.wait_ge(in_sem, in_count)
                V.tensor_copy(hi, raw).then_inc(hi_sem, 1)
                dve.wait_ge(hi_sem, count)
                V.tensor_tensor(lo, raw, hi, ALU.subtract).then_inc(done_sem, 1)

            def tokens_lo(t, n):
                dve.wait_ge(xT_hi_done, n + 1)
                tok = slice(t * P, (t + 1) * P)
                V.tensor_tensor(xT_lo[:, :, tok], ps_turn[t % 2][:].rearrange("p (c k) -> p c k", c=C),
                                xT_hi[:, :, tok], ALU.subtract).then_inc(xT_split, 1)

            for c in range(C):
                dve.wait_ge(ctx_in[c], 32)
                V.tensor_copy(wv_hi[:, c], wv_raw[:, c]).then_inc(wv_hi_done, 1)
                dve.wait_ge(ctx_hi_done, c + 1)
                V.tensor_tensor(ctx_lo[:, c], ctx_raw[:, c], ctx_hi[:, c], ALU.subtract).then_inc(ctx_split, 1)
                dve.wait_ge(wv_hi_done, c + 1)
                V.tensor_tensor(wv_lo[:, c], wv_raw[:, c], wv_hi[:, c], ALU.subtract).then_inc(wv_split, 1)

            for t in range(B):
                dve.wait_ge(x_in[t], 16)
                last = V.bn_stats(stats[:, t], acc[:, t])
            chain(last)
            for t in range(B):
                last = V.bn_aggr(mean_var[:, t], stats[:, t])
            chain(last)
            V.tensor_scalar(rstd[:], mean_var[:, :, 1], EPS, None, ALU.add).then_inc(var_ready, 1)
            dve.wait_ge(rstd_ready, 1)
            V.scalar_tensor_tensor(out=shift[:], in0=mean_var[:, :, 0], scalar=-1.0, in1=rstd[:],
                                   op0=ALU.mult, op1=ALU.mult)
            chain(V.tensor_tensor(rms[:], mean_var[:, :, 1], rstd[:], ALU.mult))
            chain(V.tensor_tensor(rms[:], rms[:], rstd[:], ALU.mult))
            V.tensor_scalar(rms[:], rms[:], EPS, None, ALU.add).then_inc(var_ready, 1)
            dve.wait_ge(rstd_ready, 2)
            V.tensor_tensor(rms_shift[:], shift[:], rms[:], ALU.mult)
            V.tensor_tensor(rms_scale[:], rstd[:], rms[:], ALU.mult).then_inc(rms_ready, 1)
            split(wqk_hi[:, 0], wqk_lo[:, 0], wqk_raw[:, 0], wqk_in[0], 16, wqk_hi_done, wqk_split, 1)
            dve.wait_ge(lnw_in, 16)
            for t in range(B):
                dve.wait_ge(x_normed, t + 1)
                V.tensor_tensor(xn[:, t], xn[:, t], lnw_s[:], ALU.mult).then_inc(xn_ready, 1)

            dve.wait_ge(mask_in, 16)
            V.tensor_scalar(mask_bias[:], mask_u8[:], -1.0, BIG, ALU.add, ALU.mult).then_inc(mask_done, 1)
            dve.wait_ge(mask_done, 1)
            chain(V.tensor_reduce(any_mask[:], mask_bias[:], AX.X, ALU.max))
            chain(V.tensor_scalar(any_mask[:], any_mask[:], -1.0, None, ALU.is_ge))
            for t in range(B):
                tokens_lo(t, t)

            dve.wait_ge(rw_in, 16)
            chain(V.tensor_copy(rw_hi[:], rw_raw[:]))
            V.tensor_tensor(rw_lo[:], rw_raw[:], rw_hi[:], ALU.subtract).then_inc(rw_split, 1)

            def bias_and_max(i):
                dve.wait_ge(bias_ready, i + 1)
                for half in range(2):
                    dve.wait_ge(score_psum, 2 * i + 1 + half)
                    V.tensor_tensor(probs[:, half], ps_score[half][:].rearrange("p (b k) -> p b k", b=BH),
                                    score_bias[:, BH * half:BH * (half + 1)], ALU.add).then_inc(score_biased, 1)
                for half in range(2):
                    dve.wait_ge(score_biased, 2 * i + 1 + half)
                    V.tensor_reduce(neg_max[:, half], probs[:, half], AX.X, ALU.max, negate=True).then_inc(max_done, 1)

            def normalise(i, count):
                for half in range(2):
                    dve.wait_ge(exp_done, 2 * i + 1 + half)
                    V.reciprocal(row_inv[:, half], row_sum[:, half]).then_inc(count, 1)
                    dve.wait_ge(count, 4 * i + 2 * half + 1)
                    V.tensor_tensor(row_scale[:, half], row_inv[:, half], any_mask[:, BH * half:BH * (half + 1)],
                                    ALU.mult).then_inc(count, 1)
                    dve.wait_ge(count, 4 * i + 2 * half + 2)
                    V.tensor_tensor(probs[:, half], probs[:, half],
                                    row_scale[:, half].unsqueeze(2).broadcast_to([P, BH, P]),
                                    ALU.mult).then_inc(probs_ready, 1)

            def take_attn_lo(i, slot):
                for half in range(2):
                    dve.wait_ge(attn_hi_done, 2 * i + 1 + half)
                    tok = slice(half * HALF, (half + 1) * HALF)
                    V.tensor_tensor(attn_lo[:, slot, tok], ps_attn[half][:], attn_hi[:, slot, tok],
                                    ALU.subtract).then_inc(attn_split, 1)

            def add_out(g, t):
                dve.wait_ge(o_psum, B * g + t + 1)
                return V.tensor_tensor(acc[:, t], ps_job[t % 2][:], acc[:, t], ALU.add)

            def head_step(g, j, first):
                i = G * g + j
                before = not (first and j == 0)
                if before:
                    bias_and_max(i - 1)
                if j == 0 and not first:
                    split(wv_hi[:], wv_lo[:], wv_raw[:], wv_in, 16 * g, wv_hi_done, wv_split, C + g)
                if j == 1 and not first:
                    for t in range(B):
                        add_out(g - 1, t).then_inc(o_added, 1)
                n = (j + 1) % 2
                if before:
                    normalise(i - 1, row_scaled)
                split(wqk_hi[:, n], wqk_lo[:, n], wqk_raw[:, n], wqk_in[n], 16 * (2 * g + (j + 1) // 2 + 1),
                      wqk_hi_done, wqk_split, i + 2)
                if j == 3:
                    split(wo_hi[:], wo_lo[:], wo_raw[:], wo_in, 16 * (g + 1), wo_hi_done, wo_split, g + 1)
                if before:
                    take_attn_lo(i - 1, (j - 1) % G)

            for j in range(G):
                head_step(0, j, True)
            dve.wait_ge(ln_ready, B)
            with dve.Fori(1, NG) as g:
                for j in range(G):
                    head_step(g, j, False)
            bias_and_max(H - 1)
            normalise(H - 1, row_scaled)
            take_attn_lo(H - 1, G - 1)

            def w12_lo_part(buf, count):
                dve.wait_ge(w12_hi_done, count)
                V.tensor_tensor(w12_lo[buf][:].rearrange("p w c k -> p (w c k)"), w12_raw[buf][:, 0:W12],
                                w12_hi[buf][:].rearrange("p w c k -> p (w c k)"), ALU.subtract).then_inc(w12_split, 1)

            def w3_lo_part(buf, count):
                dve.wait_ge(w3_hi_done, count)
                V.tensor_tensor(w3_lo[buf][:], w3_raw[buf][:], w3_hi[buf][:], ALU.subtract).then_inc(w3_split, 1)

            for t in range(B):
                dve.wait_ge(o_psum, B * (NG - 1) + t + 1)
                dve.wait_ge(residual_added, t + 1)
                V.scalar_tensor_tensor(out=acc[:, t], in0=ps_out[t % 4][:], scalar=gain[:, 0:1], in1=acc[:, t],
                                       op0=ALU.mult, op1=ALU.add).then_inc(o_added, 1)
                dve.wait_ge(o_added, B * (NG - 1) + t + 1)
                chain(V.bn_stats(stats[:, t], acc[:, t]))
                chain(V.bn_aggr(mean_var[:, t], stats[:, t]))
                V.tensor_scalar(neg_mean[:, t:t + 1], mean_var[:, t, 0:1], -1.0, None, ALU.mult)
                V.tensor_scalar(rstd[:, t:t + 1], mean_var[:, t, 1:2], EPS, None, ALU.add).then_inc(var_ready, 1)
                if t >= 3:
                    tokens_lo(t - 3, B + t - 3)
                if t in (3, 5):
                    w12_lo_part(t // 4, t // 4 + 1)
            for t in range(B - 3, B):
                tokens_lo(t, B + t)
            for n in range(SH):
                w3_lo_part(n, n + 1)

            def gate_h(n, half):
                dve.wait_ge(h_psum, 4 * n + 2 * half + 2)
                dve.wait_ge(silu_done, 2 * n + half + 1)
                V.scalar_tensor_tensor(out=hT[:, half], in0=ps_h2[half][:], scalar=w12_raw[n][:, W12 + 1:W12 + 2],
                                       in1=silu[:, half], op0=ALU.add, op1=ALU.mult).then_inc(h_gated, 1)

            def h_lo(n, half):
                dve.wait_ge(h_hi_done, 2 * n + half + 1)
                tok = slice(half * HALF, (half + 1) * HALF)
                V.tensor_tensor(hT_lo[n][:, tok], hT[:, half], hT_hi[n][:, tok], ALU.subtract).then_inc(h_split, 1)

            def along(a, n):
                return a.unsqueeze(2).broadcast_to([P, B, n])

            def pick_first(src, rank, tiles, ones, n):
                chain(V.tensor_reduce(ones[0][:], src[:], AX.X, ALU.max))
                chain(V.tensor_tensor(tiles[0][:], src[:], along(ones[0][:], n), ALU.is_equal))
                chain(V.tensor_tensor(tiles[1][:], tiles[0][:], rank, ALU.mult))
                chain(V.tensor_reduce(ones[1][:], tiles[1][:], AX.X, ALU.max))
                chain(V.tensor_tensor(tiles[2][:], tiles[1][:], along(ones[1][:], n), ALU.is_equal))
                return tiles[2]

            def pick_two(src, less, rank, tiles, ones, n):
                one = pick_first(src, rank, tiles[0:3], ones[0:2], n)
                chain(V.scalar_tensor_tensor(out=less[:], in0=one[:], scalar=-BIG, in1=src[:],
                                             op0=ALU.mult, op1=ALU.add))
                two = pick_first(less, rank, tiles[3:6], ones[2:4], n)
                return one, two

            logits, shifted = rt[0], rt[1]
            dve.wait_ge(logits_psum, 1)
            dve.wait_ge(rb_in, 16)
            V.tensor_tensor(logits[:], ps_score[0][:, 0:B * E].rearrange("p (t e) -> p t e", t=B),
                            rb_s[:, 0].unsqueeze(1).broadcast_to([P, B, E]), ALU.add).then_inc(logits_read, 1)
            dve.wait_ge(logits_read, 1)
            chain(V.tensor_reduce(r1[0][:], logits[:], AX.X, ALU.max))
            V.tensor_tensor(shifted[:], logits[:], along(r1[0][:], E), ALU.subtract).then_inc(router_in, 1)
            gate_h(0, 0)
            dve.wait_ge(rank_done, 6)
            rank = rt[2]
            V.tensor_copy(block_no[:], block_no_i[:])
            chain(V.tensor_copy(rank[:], rank_i[:]))
            dve.wait_ge(router_exp, 1)
            chain(V.tensor_reduce(r1[1][:], shifted[:], AX.X, ALU.add))
            chain(V.reciprocal(r1[2][:], r1[1][:]))
            chain(V.tensor_tensor(shifted[:], shifted[:], along(r1[2][:], E), ALU.mult))
            scores = rt[0]
            chain(V.tensor_tensor(scores[:], shifted[:], rb_s[:, 1].unsqueeze(1).broadcast_to([P, B, E]), ALU.add))
            chain(V.tensor_reduce(rg[0][:], scores[:].rearrange("p t (g m) -> p t g m", g=EG), AX.X, ALU.max))
            one, two = pick_two(rg[0], rg[1], rank[:, :, 0:EG], rg[2:8], r1[3:7], EG)
            chain(V.tensor_tensor(rg[8][:], one[:], two[:], ALU.add))
            chain(V.tensor_scalar(rg[9][:], rg[8][:], -1.0, BIG, ALU.add, ALU.mult))
            kept = rt[1]
            chain(V.tensor_tensor(kept[:].rearrange("p t (g m) -> p (t g) m", g=EG),
                                  scores[:].rearrange("p t (g m) -> p (t g) m", g=EG),
                                  rg[9][:].rearrange("p t g -> p (t g)").unsqueeze(2).broadcast_to([P, B * EG, EM]),
                                  ALU.add))
            picked = pick_two(kept, rt[9], rank[:], rt[3:9], r1[3:7], E)
            masks = rt[10]
            chain(V.tensor_tensor(masks[:], picked[0][:], picked[1][:], ALU.add))
            V.tensor_tensor(gates[:, 1:1 + E, :].rearrange("p e t -> p t e"), masks[:], scores[:],
                            ALU.mult).then_inc(gates_done, 1)
            for t in range(B - 1):
                chain(V.tensor_tensor(cum[:, t + 1], cum[:, t], masks[:, t], ALU.add))
            V.tensor_tensor(cum[:, B], cum[:, B - 1], masks[:, B - 1], ALU.add).then_inc(counts_ready, 1)
            h_lo(0, 0)
            gate_h(0, 1)
            h_lo(0, 1)
            gate_h(1, 0)
            h_lo(1, 0)

            dve.wait_ge(rank_psum, 1)
            chain(V.tensor_scalar(blocks_i[:], ps_score[1][:, B * E:(B + 1) * E], float(P - 1), None, ALU.add))
            chain(V.tensor_scalar(blocks_i[:], blocks_i[:], P.bit_length() - 1, None, ALU.arith_shift_right))
            V.tensor_copy(nblocks[:], blocks_i[:])
            chain(V.tensor_copy(scan[0][:, E // 2:], blocks_i[:]))
            src, dst = scan
            for d in (1, 2, 4, 8):
                chain(V.tensor_tensor(dst[:, E // 2:], src[:, E // 2:], src[:, E // 2 - d:E // 2 + E - d], ALU.add))
                src, dst = dst, src
            end = src[:, E // 2:]
            chain(V.tensor_tensor(first_slot[:], end, nblocks[:], ALU.subtract))
            slots = rt[2]
            chain(V.scalar_tensor_tensor(
                out=slots[:], in0=first_slot[:].unsqueeze(1).broadcast_to([P, B, E]), scalar=float(P),
                in1=ps_score[1][:, 0:B * E].rearrange("p (t e) -> p t e", t=B), op0=ALU.mult, op1=ALU.add))
            for n in range(TOP):
                chain(V.tensor_tensor(rt[9][:], picked[n][:], slots[:], ALU.mult))
                chain(V.tensor_reduce(slot_f[n][:], rt[9][:], AX.X, ALU.add))
                last = V.tensor_copy(slot_i[n][:], slot_f[n][:])
            last.then_inc(slots_ready, 1)
            chain(V.tensor_tensor(ended[:], block_no[:].unsqueeze(2).broadcast_to([1, NS, E]),
                                  end[0:1].unsqueeze(1).broadcast_to([1, NS, E]), ALU.is_ge))
            chain(V.tensor_reduce(owner_f[:], ended[:], AX.X, ALU.add))
            V.tensor_scalar(owner[:], owner_f[:], float(E - 1), None, ALU.min).then_inc(owner_ready, 1)
            gate_h(1, 1)
            h_lo(1, 1)
            for n in range(TOP):
                chain(V.tensor_tensor(rt[9][:], picked[n][:], scores[:], ALU.mult))
                chain(V.tensor_reduce(gate_f[n][:], rt[9][:], AX.X, ALU.add))
                chain(V.tensor_scalar(gate_f[n][:], gate_f[n][:], gain[:, 1:2], None, ALU.mult))
            for t in range(B):
                dve.wait_ge(shared_psum, t + 1)
                V.scalar_tensor_tensor(out=acc[:, t], in0=ps_job[t % 2][:], scalar=gain[:, 1:2], in1=acc[:, t],
                                       op0=ALU.mult, op1=ALU.add).then_inc(shared_added, 1)

            def take_hT(b, k):
                dve.wait_ge(hbT_psum, b + 1)
                V.tensor_copy(hT_b[k][:], ps_score[k][:, 0:P]).then_inc(hbT_sbuf, 1)

            def block_step(b, k, pair):
                if not (isinstance(b, int) and b == 0):
                    take_hT(b - 1, 1 - k)
                dve.wait_ge(hb_psum, b + 1)
                dve.wait_ge(bias_b_in[k], 16 * (pair + 2 - k))
                V.tensor_tensor(h_b[k][:], ps_attn[k][:, 0:2 * P], bias_b[k][:], ALU.add).then_inc(hb_biased, 1)
                dve.wait_ge(silu_b_done, b + 1)
                V.tensor_tensor(h_gate_b[k][:], silu_b[k][:], h_b[k][:, P:2 * P], ALU.mult).then_inc(hb_gated, 1)

            pair_loop(dve, block_step)
            take_hT(NB - 1, 0)

            for t in range(B):
                dve.wait_ge(y_pick_in[t], 16 * TOP)
                chain(V.scalar_tensor_tensor(out=acc[:, t], in0=y_pick[:, 0, t], scalar=gate_f[0][:, t:t + 1],
                                             in1=acc[:, t], op0=ALU.mult, op1=ALU.add))
                V.scalar_tensor_tensor(out=y_pick[:, 1, t], in0=y_pick[:, 1, t], scalar=gate_f[1][:, t:t + 1],
                                       in1=acc[:, t], op0=ALU.mult, op1=ALU.add).then_inc(final_ready, 1)


def kernel(x, ctx_4096, mask_BxSxS2_bk0, g_xattn, g_ffn, L0_xattn_position_bias, L0_xattn_ln_weight,
           L0_xattn_w_q, L0_xattn_w_k, L0_xattn_w_v, L0_xattn_w_out, L0_ffn_router_w, L0_ffn_router_b,
           L0_ffn_router_bias, L0_ffn_ew1, L0_ffn_eb1, L0_ffn_ew2, L0_ffn_eb2, L0_ffn_ew3, L0_ffn_eb3,
           L0_ffn_sw1, L0_ffn_sb1, L0_ffn_sw2, L0_ffn_sb2, L0_ffn_sw3, L0_ffn_sb3):
    import numpy as np
    import concourse.bacc as bacc
    from concourse.bass_utils import run_bass_kernel_spmd as run

    def chunks(wT, width):
        return wT.reshape(C, P, -1, width).transpose(2, 1, 0, 3)

    wq = chunks(np.asarray(L0_xattn_w_q).T, P)
    wk = chunks(np.asarray(L0_xattn_w_k).T, P)
    wqk = np.stack([wq, wk], axis=2)
    wqk = np.concatenate([wqk, wqk[:1]])
    wv = chunks(np.asarray(L0_xattn_w_v).T, G * P)
    wo = np.asarray(L0_xattn_w_out).T.reshape(NG, G, P, D).transpose(0, 2, 1, 3)

    sw12 = np.concatenate([chunks(np.asarray(L0_ffn_sw1), P).reshape(SH, P, C * P),
                           chunks(np.asarray(L0_ffn_sw2), P).reshape(SH, P, C * P),
                           np.asarray(L0_ffn_sb1).reshape(SH, P, 1), np.asarray(L0_ffn_sb2).reshape(SH, P, 1)], axis=2)
    ew12 = np.concatenate([np.asarray(L0_ffn_ew1).reshape(E, C, P, P), np.asarray(L0_ffn_ew2).reshape(E, C, P, P)],
                          axis=3).transpose(0, 2, 1, 3)
    arrays = {
        "x": np.asarray(x),
        "ctxT": np.asarray(ctx_4096).reshape(T, C, P).transpose(2, 1, 0),
        "mask": np.asarray(mask_BxSxS2_bk0),
        "gains": np.concatenate([np.asarray(g_xattn), np.asarray(g_ffn)]),
        "pbias": np.asarray(L0_xattn_position_bias),
        "lnw": np.asarray(L0_xattn_ln_weight),
        "wqk": wqk,
        "wv": wv,
        "wo": wo,
        "sw12": sw12,
        "sw3": np.asarray(L0_ffn_sw3).reshape(SH, P, D),
        "ew12": ew12,
        "eb12": np.concatenate([np.asarray(L0_ffn_eb1), np.asarray(L0_ffn_eb2)], axis=1),
        "ew3": np.asarray(L0_ffn_ew3),
        "rw": np.asarray(L0_ffn_router_w).reshape(C, P, E).transpose(1, 0, 2),
        "rb": np.stack([np.asarray(L0_ffn_router_b), np.asarray(L0_ffn_router_bias)]),
        "b3": np.concatenate([np.asarray(L0_ffn_sb3)[None], np.asarray(L0_ffn_eb3)]),
    }
    nc = bacc.Bacc("TRN2", target_bir_lowering=False, num_devices=1)
    args = []
    for name in arrays:
        a = arrays[name] = np.ascontiguousarray(arrays[name])
        args.append(nc.dram_tensor(f"{name}_dram", a.shape, mybir.dt.from_np(a.dtype), kind="ExternalInput").ap())
    out = nc.dram_tensor("out_dram", (B, P, D), F32, kind="ExternalOutput").ap()
    build(nc, *args, out)
    result = run(nc, [{f"{name}_dram": a for name, a in arrays.items()}], core_ids=[0])
    return result.results[0]["out_dram"]
```

```python
from contextlib import ExitStack

import concourse.bass as bass
from concourse import mybir

F32 = mybir.dt.float32
F32R = mybir.dt.float32r
I32 = mybir.dt.int32
U8 = mybir.dt.uint8
ALU = mybir.AluOpType
ACT = mybir.ActivationFunctionType
AX = mybir.AxisListType

P = 128
B = 8
D = 512
C = D // P
T = B * P
H = 32
G = 4
NG = H // G
HALF = T // 2
BH = B // 2
E = 16
EG = 4
EM = E // EG
SH = 2
TOP = 2
NB = (TOP * T + E * (P - 1)) // P
NS = NB + 1
assert NS == H
GP = 32
W12 = 2 * C * P
EPS = 1e-5
BIG = 1e30


def need(eng, sem, count):
    if not isinstance(count, int) or count > 0:
        eng.wait_ge(sem, count)


def build(nc, x, ctxT, mask, gains, pbias, lnw, wqk, wv, wo, sw12, sw3, ew12, eb12, ew3, rw, rb, b3, out):
    with ExitStack() as stack:
        base = (nc.sbuf_base + 63) // 64 * 64
        top = [0]

        def place(name, shape, dtype, at=None):
            size = 1
            for n in shape[1:]:
                size *= n
            size = (size * (1 if dtype == U8 else 4) + 31) // 32 * 32
            if at is None:
                at, top[0] = top[0], top[0] + size
            return nc.alloc_sbuf_tensor_at(name, shape, dtype, offset=base + at)

        def room(size):
            at, top[0] = top[0], top[0] + size
            return at

        at_ctx_hi, at_ctx_lo = room(C * T * 4), room(C * T * 4)
        ctx_hi = place("ctx_hi", [P, C, T], F32R, at_ctx_hi)
        ctx_lo = place("ctx_lo", [P, C, T], F32R, at_ctx_lo)
        ctx_raw = place("ctx_raw", [P, C, T], F32, at_ctx_lo)
        at_wqk = room(4 * W12 * 4)
        wqk_hi = place("wqk_hi", [P, 2, 2, C, P], F32R, at_wqk)
        wqk_lo = place("wqk_lo", [P, 2, 2, C, P], F32R, at_wqk + 2 * W12 * 4)
        wqk_raw = place("wqk_raw", [P, 2, 2, C, P], F32, at_wqk + 2 * W12 * 4)
        at_wv = room(2 * C * D * 4)
        wv_hi = place("wv_hi", [P, C, D], F32R, at_wv)
        wv_lo = place("wv_lo", [P, C, D], F32R, at_wv + C * D * 4)
        wv_raw = place("wv_raw", [P, C, D], F32, at_wv + C * D * 4)
        at_xT = room(2 * C * T * 4)
        xT_hi = place("xT_hi", [P, C, T], F32R, at_xT)
        xT_lo = place("xT_lo", [P, C, T], F32R, at_xT + C * T * 4)
        acc = place("acc", [P, B, D], F32)
        at_wo = room(2 * G * D * 4)
        wo_hi = place("wo_hi", [P, G, D], F32R, at_wo)
        wo_lo = place("wo_lo", [P, G, D], F32R, at_wo + G * D * 4)
        wo_raw = place("wo_raw", [P, G, D], F32, at_wo + G * D * 4)
        at_v = room(B * G * P * 4)
        v_s = place("v_s", [P, B, G * P], F32, at_v)
        at_attn = room(2 * G * T * 4)
        attn_hi = place("attn_hi", [P, G, T], F32R, at_attn)
        attn_lo = place("attn_lo", [P, G, T], F32R, at_attn + G * T * 4)
        at_qk = room(2 * T * 4)
        qT = place("qT", [P, T], F32, at_qk)
        kT = place("kT", [P, T], F32, at_qk + T * 4)
        at_s = room(T * 4)
        probs = place("probs", [P, 2, BH, P], F32, at_s)
        at_pT = room(T * 4)
        pT = place("pT", [P, 2, HALF], F32, at_pT)
        mask_bias = place("mask_bias", [P, B, P], F32)
        score_bias = place("score_bias", [P, B, P], F32)
        pos_bias = place("pos_bias", [P, 2, P], F32)
        at_end_scores = top[0]
        ident = place("ident", [P, P], F32)
        gain = place("gain", [P, 2], F32)
        any_mask = place("any_mask", [P, B], F32)
        neg_max = place("neg_max", [P, 2, BH], F32)
        row_sum = place("row_sum", [P, 2, BH], F32)
        row_inv = place("row_inv", [P, 2, BH], F32)
        row_scale = place("row_scale", [P, 2, BH], F32)
        stats = place("stats", [P, B, 6], F32)
        mean_var = place("mean_var", [P, B, 2], F32)
        rstd = place("rstd", [P, B], F32)
        neg_mean = place("neg_mean", [P, B], F32)
        shift = place("shift", [P, B], F32)
        rms_scale = place("rms_scale", [P, B], F32)
        rms_shift = place("rms_shift", [P, B], F32)
        rms = place("rms", [P, B], F32)
        minus_half = place("minus_half", [P, B], F32)
        zeros = place("zeros", [P, D], F32)
        ones = place("ones", [P, P], F32)
        before = place("before", [P, P], F32)
        rw_raw = place("rw_raw", [P, C, E], F32)
        rw_hi = place("rw_hi", [P, C, E], F32R)
        rw_lo = place("rw_lo", [P, C, E], F32R)
        rb_s = place("rb_s", [P, 2, E], F32)
        assert base + top[0] <= nc.sbuf_usable_end, top[0]

        mask_u8 = place("mask_u8", [P, B, P], U8, at_s)
        lnw_s = place("lnw_s", [P, D], F32, at_pT + D * 4)
        xn = place("xn", [P, B, D], F32, at_attn)
        x2n = place("x2n", [P, B, D], F32, at_v)
        x_res = place("x_res", [P, B, D], F32, at_wv)
        w12_hi, w12_lo, w12_raw, w3_hi, w3_lo, w3_raw = [], [], [], [], [], []
        for n in range(SH):
            at = at_qk + n * (2 * W12 + 8) * 4
            w12_hi.append(place(f"w12_hi{n}", [P, 2, C, P], F32R, at))
            w12_lo.append(place(f"w12_lo{n}", [P, 2, C, P], F32R, at + W12 * 4))
            w12_raw.append(place(f"w12_raw{n}", [P, W12 + 2], F32, at + W12 * 4))
            at = at_qk + SH * (2 * W12 + 8) * 4 + n * 2 * D * 4
            w3_hi.append(place(f"w3_hi{n}", [P, D], F32R, at))
            w3_lo.append(place(f"w3_lo{n}", [P, D], F32R, at + D * 4))
            w3_raw.append(place(f"w3_raw{n}", [P, D], F32, at + D * 4))
        assert at + 2 * D * 4 <= at_end_scores
        hT_hi = [place(f"hT_hi{n}", [P, T], F32R, at_attn + n * T * 4) for n in range(SH)]
        hT_lo = [place(f"hT_lo{n}", [P, T], F32R, at_attn + (SH + n) * T * 4) for n in range(SH)]
        silu = place("silu", [P, 2, HALF], F32, at_attn + 2 * SH * T * 4)
        hT = place("hT", [P, 2, HALF], F32, at_attn + (2 * SH + 1) * T * 4)
        at_b3 = at_attn + (2 * SH + 2) * T * 4
        b3_raw = place("b3_raw", [3 * GP, D], F32, at_b3)
        b3_s = place("b3_s", [3 * GP, D], F32R, at_b3 + D * 4)
        logitsT = place("logitsT", [E, T], F32, at_b3 + 2 * D * 4)
        gT = place("gT", [3 * GP, T], F32R, at_b3 + 2 * D * 4)
        assert at_ctx_hi + E * W12 * 4 <= at_xT
        ew12_s = place("ew12_s", [P, E, C, 2 * P], F32, at_ctx_hi)
        w3_s = place("w3_s", [P, E, D], F32, at_xT)
        cursor = [at_qk]

        def two(name, cols):
            at, cursor[0] = cursor[0], cursor[0] + 2 * cols * 4
            return [place(f"{name}{n}", [P, cols], F32, at + n * cols * 4) for n in range(2)]

        xb, xbT, y_out, bias_b, h_b = (two("xb", D), two("xbT", D), two("y_out", D), two("bias_b", 2 * P),
                                       two("h_b", 2 * P))
        assert cursor[0] <= at_qk + SH * (2 * W12 + 8) * 4
        cursor = [at_attn + 2 * SH * T * 4]
        silu_b, h_gate_b, hT_b = two("silu_b", P), two("h_gate_b", P), two("hT_b", P)
        assert cursor[0] <= at_attn + (2 * SH + 2) * T * 4
        y_pick = place("y_pick", [P, TOP, B, D], F32, at_ctx_hi)
        cursor = [at_wo]

        def small(name, shape, dtype=F32):
            size = 4
            for n in shape[1:]:
                size *= n
            at, cursor[0] = cursor[0], cursor[0] + (size + 31) // 32 * 32
            return place(name, shape, dtype, at)

        gates = small("gates", [P, 1 + E, B])
        gates3 = small("gates3", [P, B, 3, GP])
        rt = [small(f"rt{n}", [P, B, E]) for n in range(11)]
        rg = [small(f"rg{n}", [P, B, EG]) for n in range(10)]
        r1 = [small(f"r1_{n}", [P, B]) for n in range(7)]
        rank_i = small("rank_i", [P, B, E], I32)
        cum = small("cum", [P, B + 1, E])
        masks_before = small("masks_before", [P, 2 * B, E])
        at_sums = cursor[0]
        sums = [small(f"sums{n}", [P, 2 * B, E]) for n in range(2)]
        blocks_i = small("blocks_i", [P, E], I32)
        scan = [small(f"scan{n}", [P, E // 2 + E]) for n in range(2)]
        nblocks = small("nblocks", [P, E])
        first_slot = small("first_slot", [P, E])
        slot_f = [small(f"slot_f{n}", [P, B]) for n in range(TOP)]
        slot_i = [small(f"slot_i{n}", [P, B], I32) for n in range(TOP)]
        gate_raw = small("gate_raw", [P, TOP, B])
        gate_f = small("gate_f", [P, TOP, B])
        block_no_i = small("block_no_i", [1, NS], I32)
        block_no = small("block_no", [1, NS])
        gates_hi = place("gates_hi", [P, 1 + E, B], F32R, at_sums)
        ended = place("ended", [1, NS, E], F32, at_sums)
        owner_f = small("owner_f", [1, NS])
        owner = small("owner", [1, NS], I32)
        round_up_i = small("round_up_i", [1, 2], I32)
        round_up = small("round_up", [1, 2])
        stores_i = small("stores_i", [1, 2], I32)
        assert cursor[0] <= at_wo + 2 * G * D * 4, cursor[0] - at_wo

        def bank(name):
            return stack.enter_context(nc.psum_tensor(name, [P, D], F32))

        ps_job = [bank("ps_job0"), bank("ps_job1")]
        ps_score = [bank("ps_score0"), bank("ps_score1")]
        ps_turn = [bank("ps_turn0"), bank("ps_turn1")]
        ps_attn = [bank("ps_attn0"), bank("ps_attn1")]
        ps_first_v = ps_job + ps_turn + ps_score + ps_attn
        ps_out = ps_job + ps_score
        ps_x = ps_turn + ps_score + ps_attn + ps_turn
        ps_x2 = ps_turn * (B // 2)
        ps_h1 = [ps_job[0], ps_attn[0]]
        ps_h2 = [ps_job[1], ps_attn[1]]

        x_slots = nc.dram_tensor("x_slots", (NS * P, D), F32, kind="Internal").ap()
        y_slots = nc.dram_tensor("y_slots", (NS * P, D), F32, kind="Internal").ap()
        x_slot_blocks = x_slots.rearrange("(b p) d -> b p d", p=P)
        y_slot_blocks = y_slots.rearrange("(b p) d -> b p d", p=P)

        def sem(name):
            return stack.enter_context(nc.semaphore(name))

        ctx_in = [sem(f"ctx_in{c}") for c in range(C)]
        x_in = [sem(f"x_in{t}") for t in range(B)]
        mask_in, gain_in, lnw_in, wv_in, wo_in = map(sem, ("mask_in", "gain_in", "lnw_in", "wv_in", "wo_in"))
        wqk_in = [sem("wqk_in0"), sem("wqk_in1")]
        pos_in = [sem("pos_in0"), sem("pos_in1")]
        x_res_in, rw_in, rb_in, b3_in = map(sem, ("x_res_in", "rw_in", "rb_in", "b3_in"))
        w12_in = [sem("w12_in0"), sem("w12_in1")]
        w3_in = [sem("w3_in0"), sem("w3_in1")]
        ew12_in, ew3_in = sem("ew12_in"), sem("ew3_in")
        xb_in = [sem("xb_in0"), sem("xb_in1")]
        bias_b_in = [sem("bias_b_in0"), sem("bias_b_in1")]
        cleared, scattered = sem("cleared"), sem("scattered")
        y_stored = [sem("y_stored0"), sem("y_stored1")]
        y_pick_in = [sem(f"y_pick_in{t}") for t in range(B)]
        ctx_hi_done, ctx_split = sem("ctx_hi_done"), sem("ctx_split")
        wqk_hi_done, wqk_split = sem("wqk_hi_done"), sem("wqk_split")
        wv_hi_done, wv_split = sem("wv_hi_done"), sem("wv_split")
        wo_hi_done, wo_split = sem("wo_hi_done"), sem("wo_split")
        w12_hi_done, w12_split = sem("w12_hi_done"), sem("w12_split")
        w3_hi_done, w3_split = sem("w3_hi_done"), sem("w3_split")
        rw_split = sem("rw_split")
        x_normed, residual_added, shift_ready, logits_copied, logitsT_psum = map(
            sem, ("x_normed", "residual_added", "shift_ready", "logits_copied", "logitsT_psum"))
        ident_done, mask_done, gain_done = sem("ident_done"), sem("mask_done"), sem("gain_done")
        rank_done, rms_ready, ln_ready = map(sem, ("rank_done", "rms_ready", "ln_ready"))
        var_ready, rstd_ready, half_done = sem("var_ready"), sem("rstd_ready"), sem("half_done")
        xn_ready, xT_psum, xT_hi_done, xT_split = map(sem, ("xn_ready", "xT_psum", "xT_hi_done", "xT_split"))
        qk_psum, qk_sbuf, v_psum, v_sbuf = map(sem, ("qk_psum", "qk_sbuf", "v_psum", "v_sbuf"))
        o_psum, o_added = sem("o_psum"), sem("o_added")
        bias_ready, score_psum, score_biased, max_done, exp_done = map(
            sem, ("bias_ready", "score_psum", "score_biased", "max_done", "exp_done"))
        row_scaled = sem("row_scaled")
        probs_ready, pT_psum, pT_sbuf, attn_psum, attn_hi_done, attn_split = map(
            sem, ("probs_ready", "pT_psum", "pT_sbuf", "attn_psum", "attn_hi_done", "attn_split"))
        logits_psum, logits_read, router_in, router_exp, gates_done = map(
            sem, ("logits_psum", "logits_read", "router_in", "router_exp", "gates_done"))
        h_psum, silu_done, h_gated, h_hi_done, h_split = map(
            sem, ("h_psum", "silu_done", "h_gated", "h_hi_done", "h_split"))
        gT_psum, gT_sbuf, shared_psum, shared_added = map(
            sem, ("gT_psum", "gT_sbuf", "shared_psum", "shared_added"))
        const_done, counts_ready, rank_psum, slots_ready, owner_ready = map(
            sem, ("const_done", "counts_ready", "rank_psum", "slots_ready", "owner_ready"))
        xbT_psum, xbT_sbuf, hb_psum, hb_biased, silu_b_done, hb_gated, hbT_psum, hbT_sbuf, yb_psum, yb_sbuf = map(
            sem, ("xbT_psum", "xbT_sbuf", "hb_psum", "hb_biased", "silu_b_done", "hb_gated", "hbT_psum",
                  "hbT_sbuf", "yb_psum", "yb_sbuf"))
        gate_raw_ready, stores_known, gate_ready, y_scaled, first_added = map(
            sem, ("gate_raw_ready", "stores_known", "gate_ready", "y_scaled", "first_added"))
        b3_hi_done, b3_split, gates_hi_done = map(sem, ("b3_hi_done", "b3_split", "gates_hi_done"))
        final_ready, stored = sem("final_ready"), sem("stored")
        dve_chain = sem("dve_chain")

        block = stack.enter_context(nc.Block())

        def pair_loop(eng, step):
            step(0, 0, -1)
            step(1, 1, 0)
            step(2, 0, 0)
            with eng.Fori(1, NB // 2 - 2) as pair:
                step(2 * pair + 1, 1, pair)
                step(2 * pair + 2, 0, pair)
            for b in range(NB - 4, NB):
                step(b, b % 2, (b - 1) // 2)

        @block.sync
        def _(sp):
            for c in range(C):
                sp.dma_start(ctx_raw[:, c], ctxT[:, c]).then_inc(ctx_in[c], 16)
                sp.dma_start(wv_raw[:, c], wv[0, :, c]).then_inc(ctx_in[c], 16)
            for t in range(B):
                sp.dma_start(acc[:, t], x[t]).then_inc(x_in[t], 16)
            sp.dma_start(wqk_raw[:, 0], wqk[0]).then_inc(wqk_in[0], 16)

            def load_step(g, j, first):
                i = G * g + j
                if j == 0 and not first:
                    need(sp, v_psum, B * g)
                    sp.dma_start(wv_raw[:], wv[g]).then_inc(wv_in, 16)
                need(sp, bias_ready, i - 1)
                sp.dma_start(pos_bias[:, j % 2], pbias[i]).then_inc(pos_in[j % 2], 16)
                need(sp, qk_psum, 4 * i)
                sp.dma_start(wqk_raw[:, (j + 1) % 2], wqk[i + 1]).then_inc(wqk_in[(j + 1) % 2], 16)
                sp.dma_start(x_slot_blocks[i], zeros[:]).then_inc(cleared, 16)
                sp.dma_start(y_slot_blocks[i], zeros[:]).then_inc(cleared, 16)
                if j == 2:
                    need(sp, o_psum, B * g)
                    sp.dma_start(wo_raw[:], wo[g]).then_inc(wo_in, 16)

            sp.dma_start(rw_raw[:], rw).then_inc(rw_in, 16)
            sp.dma_start(rb_s[:], rb.partition_broadcast(P)).then_inc(rb_in, 16)
            sp.wait_ge(const_done, 1)
            for j in range(G):
                load_step(0, j, True)
            with sp.Fori(1, NG) as g:
                for j in range(G):
                    load_step(g, j, False)

            sp.wait_ge(v_psum, B * NG)
            sp.dma_start(x_res[:], x.rearrange("t p d -> p t d")).then_inc(x_res_in, 16)
            sp.wait_ge(attn_psum, 2 * H)
            for n in range(SH):
                sp.dma_start(w12_raw[n][:], sw12[n]).then_inc(w12_in[n], 16)
                sp.dma_start(w3_raw[n][:], sw3[n]).then_inc(w3_in[n], 16)
            sp.wait_ge(wqk_split, H + 1)
            sp.wait_ge(residual_added, B)
            for n in range(0, E, E // 4):
                sp.dma_start(ew12_s[:, n:n + E // 4], ew12[n:n + E // 4].rearrange("e p c k -> p e c k"))\
                  .then_inc(ew12_in, 16)
            sp.wait_ge(o_psum, B * NG)
            sp.dma_start(b3_raw[:], b3).then_inc(b3_in, 16)

            def load_x(b, k):
                sp.dma_start(xb[k][:], x_slot_blocks[b]).then_inc(xb_in[k], 16)

            def owner_of(b):
                return sp.value_load(owner[0:1, bass.ds(b, 1)], min_val=0, max_val=E - 1)

            def load_bias(e, k):
                sp.dma_start(bias_b[k][:], eb12[e].partition_broadcast(P)).then_inc(bias_b_in[k], 16)

            def store_y(b, k):
                sp.wait_ge(yb_sbuf, b + 1)
                sp.dma_start(y_slot_blocks[b], y_out[k][:]).then_inc(y_stored[k], 16)

            def block_step(b, k, pair):
                static = isinstance(b, int)
                if not (static and b + 1 >= NB):
                    e = owner_of(b + 1)
                    need(sp, hb_biased, b)
                    load_bias(e, 1 - k)
                if not (static and b + 4 >= NB):
                    sp.wait_ge(xbT_psum, b + 3)
                    load_x(b + 4, k)
                if not (static and b == 0):
                    store_y(b - 1, 1 - k)

            sp.wait_ge(h_psum, 4 * SH)
            def load_w3(n):
                some = slice(n * E // 4, (n + 1) * E // 4)
                sp.dma_start(w3_s[:, some], ew3[some].rearrange("e p d -> p e d")).then_inc(ew3_in, 16)

            load_w3(0)
            load_w3(1)
            load_w3(2)
            sp.wait_ge(h_gated, 2 * SH)
            sp.wait_ge(owner_ready, 1)
            load_bias(owner_of(0), 0)
            sp.wait_ge(scattered, 16 * TOP * B)
            load_x(0, 0)
            load_x(1, 1)
            for k in range(2):
                sp.wait_ge(xbT_psum, k + 1)
                load_x(k + 2, k)
            load_w3(3)
            pair_loop(sp, block_step)
            store_y(NB - 1, (NB - 1) % 2)

            for t in range(B):
                sp.wait_ge(final_ready, t + 1)
                sp.dma_start(out[t], y_pick[:, 1, t]).then_inc(stored, 16)
            sp.wait_ge(stored, 16 * B)

        @block.gpsimd
        def _(pool):
            nc.gpsimd.memset(ident[:], 0.0).then_inc(ident_done, 1)
            pool.wait_ge(ident_done, 1)
            nc.gpsimd.affine_select(out=ident[:], in_=ident[:], compare_op=ALU.not_equal, fill=1.0,
                                    base=0, pattern=[[-1, P]], channel_multiplier=1).then_inc(ident_done, 1)

            nc.gpsimd.memset(zeros[:], 0.0).then_inc(const_done, 1)
            nc.gpsimd.memset(ones[:], 1.0).then_inc(const_done, 1)
            nc.gpsimd.memset(before[:], 1.0).then_inc(const_done, 1)
            pool.wait_ge(const_done, 3)
            nc.gpsimd.affine_select(out=before[:], in_=before[:], compare_op=ALU.is_gt, fill=0.0,
                                    base=0, pattern=[[1, P]], channel_multiplier=-1).then_inc(const_done, 1)
            nc.gpsimd.memset(minus_half[:], -0.5).then_inc(half_done, 1)
            pool.wait_ge(half_done, 1)

            def to_minus_half(dst, src, count):
                pool.wait_ge(var_ready, count)
                nc.gpsimd.tensor_tensor(dst, src, minus_half[:, 0:src.shape[1]], ALU.pow).then_inc(rstd_ready, 1)

            to_minus_half(rstd[:], rstd[:], 1)
            to_minus_half(rms[:], rms[:], 2)

            def bias_step(g, j, first):
                i = G * g + j
                if first and j == 0:
                    pool.wait_ge(mask_done, 1)
                pool.wait_ge(pos_in[j % 2], 16 * (2 * g + j // 2 + 1))
                need(pool, score_biased, 2 * i)
                nc.gpsimd.tensor_tensor(score_bias[:], mask_bias[:],
                                        pos_bias[:, j % 2].unsqueeze(1).broadcast_to([P, B, P]),
                                        ALU.add).then_inc(bias_ready, 1)

            for j in range(G):
                bias_step(0, j, True)
            with pool.Fori(1, NG) as g:
                for j in range(G):
                    bias_step(g, j, False)

            for t in range(B):
                to_minus_half(rstd[:, t:t + 1], rstd[:, t:t + 1], 3 + t)
                pool.wait_ge(rstd_ready, 3 + t)
                nc.gpsimd.tensor_tensor(shift[:, t:t + 1], neg_mean[:, t:t + 1], rstd[:, t:t + 1],
                                        ALU.mult).then_inc(shift_ready, 1)

            pool.wait_ge(o_psum, B * NG)
            nc.gpsimd.iota(rank_i[:], pattern=[[0, B], [-1, E]], base=E, channel_multiplier=0).then_inc(rank_done, 1)
            nc.gpsimd.iota(block_no_i[:], pattern=[[1, NS]], base=0, channel_multiplier=0).then_inc(rank_done, 1)
            nc.gpsimd.memset(gates[:, 0:1, :], 1.0).then_inc(rank_done, 1)
            nc.gpsimd.memset(gates3[:], 0.0).then_inc(rank_done, 1)
            nc.gpsimd.iota(round_up_i[:], pattern=[[-1, 2]], base=1, channel_multiplier=0).then_inc(rank_done, 1)
            for n in range(2):
                nc.gpsimd.memset(scan[n][:, 0:E // 2], 0.0).then_inc(rank_done, 1)
            nc.gpsimd.memset(cum[:, 0, :], 0.0).then_inc(rank_done, 1)
            for padded in (masks_before, sums[0], sums[1]):
                nc.gpsimd.memset(padded[:, 0:B], 0.0).then_inc(rank_done, 1)

            pool.wait_ge(xn_ready, 2 * B)
            pool.wait_ge(cleared, 2 * 16 * NS)
            for n in range(TOP):
                pool.wait_ge(slots_ready, n + 1)
                for t in range(B):
                    nc.gpsimd.indirect_dma_start(
                        out=x_slots, out_offset=bass.IndirectOffsetOnAxis(ap=slot_i[n][:, t:t + 1], axis=0),
                        in_=x2n[:, t], in_offset=None, bounds_check=NB * P - 1, oob_is_err=False).then_inc(scattered, 16)
            pool.wait_ge(shared_added, B)
            pool.wait_ge(gate_raw_ready, 1)
            pool.wait_ge(stores_known, 1)
            stores = [pool.value_load(stores_i[0:1, k:k + 1], min_val=P, max_val=16 * NB) for k in range(2)]
            for k in range(2):
                pool.wait_ge(y_stored[k], stores[k])
            nc.gpsimd.tensor_tensor(gate_f[:].rearrange("p n t -> p (n t)"), gate_raw[:].rearrange("p n t -> p (n t)"),
                                    gain[:, 1:2].broadcast_to([P, TOP * B]), ALU.mult).then_inc(gate_ready, 1)

            def pick_up(t):
                for n in range(TOP):
                    nc.gpsimd.indirect_dma_start(
                        out=y_pick[:, n, t], out_offset=None, in_=y_slots,
                        in_offset=bass.IndirectOffsetOnAxis(ap=slot_i[n][:, t:t + 1], axis=0),
                        bounds_check=NB * P - 1, oob_is_err=False).then_inc(y_pick_in[t], 16)

            def add_first(t):
                pool.wait_ge(y_pick_in[t], 16 * TOP)
                nc.gpsimd.tensor_tensor(y_pick[:, 0, t], y_pick[:, 0, t], gate_f[:, 0, t:t + 1].broadcast_to([P, D]),
                                        ALU.mult).then_inc(y_scaled, 1)
                pool.wait_ge(y_scaled, t + 1)
                nc.gpsimd.tensor_tensor(acc[:, t], acc[:, t], y_pick[:, 0, t], ALU.add).then_inc(first_added, 1)

            pool.wait_ge(gate_ready, 1)
            for t in range(B):
                pick_up(t)
                if t >= 2:
                    add_first(t - 2)
            for t in range(B - 2, B):
                add_first(t)

        @block.tensor
        def _(pe):
            def three(psum, pairs, closed=True):
                n = len(pairs)
                for k, (l_hi, l_lo, r_hi, r_lo) in enumerate(pairs):
                    nc.tensor.matmul(psum, l_lo, r_hi, start=(k == 0), stop=False)
                    nc.tensor.matmul(psum, l_hi, r_lo, start=False, stop=False)
                    last = nc.tensor.matmul(psum, l_hi, r_hi, start=False, stop=(closed and k == n - 1))
                return last

            def cols(t, w=P):
                return slice(t * w, (t + 1) * w)

            def turn_tokens(src, t, psum):
                for c in range(C):
                    last = nc.tensor.transpose(psum[t][:, cols(c)], src[:, t, cols(c)], ident[:])
                last.then_inc(xT_psum, 1)

            def project_qk(g, j, which, half):
                hi, lo = (xT_hi, xT_lo) if which == 0 else (ctx_hi, ctx_lo)
                tok = cols(half, HALF)
                three(ps_job[half][:], [(wqk_hi[:, j % 2, which, c], wqk_lo[:, j % 2, which, c],
                                         hi[:, c, tok], lo[:, c, tok]) for c in range(C)]).then_inc(qk_psum, 1)

            def project_v(t):
                three(ps_job[t % 2][:], [(ctx_hi[:, c, cols(t)], ctx_lo[:, c, cols(t)], wv_hi[:, c], wv_lo[:, c])
                                         for c in range(C)]).then_inc(v_psum, 1)

            def project_out(t):
                three(ps_job[t % 2][:], [(attn_hi[:, s, cols(t)], attn_lo[:, s, cols(t)], wo_hi[:, s], wo_lo[:, s])
                                         for s in range(G)]).then_inc(o_psum, 1)

            def score(i):
                need(pe, qk_sbuf, 4 * i + 4)
                for half in range(2):
                    need(pe, score_biased, 2 * i - 1 + half)
                    for b in range(BH):
                        tok = cols(BH * half + b)
                        last = nc.tensor.matmul(ps_score[half][:, cols(b)], qT[:, tok], kT[:, tok], start=True, stop=True)
                    last.then_inc(score_psum, 1)

            def turn_probs(i):
                for half in range(2):
                    pe.wait_ge(probs_ready, 2 * i + 1 + half)
                    need(pe, pT_sbuf, 2 * i - 1 + half)
                    for b in range(BH):
                        last = nc.tensor.transpose(ps_turn[half][:, cols(b)], probs[:, half, b], ident[:])
                    last.then_inc(pT_psum, 1)

            def attend(i, slot):
                for half in range(2):
                    pe.wait_ge(pT_sbuf, 2 * i + 1 + half)
                    need(pe, attn_split, 2 * i - 1 + half)
                    for b in range(BH):
                        last = nc.tensor.matmul(ps_attn[half][:, cols(b)], v_s[:, BH * half + b, cols(slot)],
                                                pT[:, half, cols(b)], start=True, stop=True)
                    last.then_inc(attn_psum, 1)

            def head_step(g, j, first):
                i = G * g + j
                before = not (first and j == 0)
                if before:
                    score(i - 1)
                if j == 1 and not first:
                    pe.wait_ge(wo_split, g)
                    pe.wait_ge(attn_split, 2 * G * g)
                    for t in range(B):
                        if t < 2:
                            pe.wait_ge(v_sbuf, B * g + B - 1 + t)
                        else:
                            pe.wait_ge(o_added, B * (g - 1) + t - 1)
                        project_out(t)
                pe.wait_ge(wqk_split, i + 1)
                for half in range(2):
                    if j == 1 and not first:
                        pe.wait_ge(o_added, B * (g - 1) + B - 1 + half)
                    elif first and j == 0:
                        pe.wait_ge(v_sbuf, 1 + half)
                    else:
                        pe.wait_ge(qk_sbuf, 4 * (i - 1) + 3 + half)
                    project_qk(g, j, 1, half)
                    if first and j == 0:
                        for t in range(3 * half, 3 * half + 3):
                            turn_when_free(t)
                if first and j == 0:
                    turn_when_free(6)
                    turn_when_free(7)
                    pe.wait_ge(xT_split, BH)
                pe.wait_ge(qk_sbuf, 4 * i + 1)
                project_qk(g, j, 0, 0)
                if first and j == 0:
                    pe.wait_ge(xT_split, B)
                if before:
                    turn_probs(i - 1)
                pe.wait_ge(qk_sbuf, 4 * i + 2)
                project_qk(g, j, 0, 1)
                if before:
                    if j == 1:
                        pe.wait_ge(v_sbuf, B * g + B)
                    attend(i - 1, (j - 1) % G)
                if j == 0 and not first:
                    pe.wait_ge(wv_split, C + g)
                    for t in range(B):
                        if t < 2:
                            pe.wait_ge(qk_sbuf, 4 * i + 3 + t)
                        else:
                            pe.wait_ge(v_sbuf, B * g + t - 1)
                        project_v(t)

            def turn_when_free(t):
                pe.wait_ge(xn_ready, t + 1)
                if t < 6:
                    pe.wait_ge(v_sbuf, ps_first_v.index(ps_x[t]) + 1)
                else:
                    pe.wait_ge(xT_split, t - 5)
                turn_tokens(xn, t, ps_x)

            for c in range(C):
                pe.wait_ge(ctx_hi_done, c + 1)
                pe.wait_ge(wv_split, c + 1)
                for t in range(B):
                    psum, lhs_hi, lhs_lo = ps_first_v[t][:], ctx_hi[:, c, cols(t)], ctx_lo[:, c, cols(t)]
                    nc.tensor.matmul(psum, lhs_hi, wv_lo[:, c], start=(c == 0), stop=False)
                    nc.tensor.matmul(psum, lhs_hi, wv_hi[:, c], start=False, stop=False)
                    if t == 0:
                        pe.wait_ge(ctx_split, c + 1)
                    last = nc.tensor.matmul(psum, lhs_lo, wv_hi[:, c], start=False, stop=(c == C - 1))
                    if c == C - 1:
                        last.then_inc(v_psum, 1)
            pe.wait_ge(ident_done, 2)
            for j in range(G):
                head_step(0, j, True)
            with pe.Fori(1, NG) as g:
                for j in range(G):
                    head_step(g, j, False)

            def out_part(t, heads):
                for s in heads:
                    psum = ps_out[t % 4][:]
                    nc.tensor.matmul(psum, attn_lo[:, s, cols(t)], wo_hi[:, s], start=(s == 0), stop=False)
                    nc.tensor.matmul(psum, attn_hi[:, s, cols(t)], wo_lo[:, s], start=False, stop=False)
                    last = nc.tensor.matmul(psum, attn_hi[:, s, cols(t)], wo_hi[:, s], start=False, stop=(s == G - 1))
                if s == G - 1:
                    last.then_inc(o_psum, 1)

            def out_ahead(t):
                if t < 2:
                    pe.wait_ge(qk_sbuf, 4 * (H - 1) + 3 + t)
                else:
                    pe.wait_ge(score_biased, 2 * (H - 1) + t - 1)
                out_part(t, range(G - 1))

            def turn_x2(t):
                pe.wait_ge(xn_ready, B + t + 1)
                if t < 2:
                    pe.wait_ge(pT_sbuf, 2 * H)
                else:
                    pe.wait_ge(xT_split, B + t - 1)
                turn_tokens(x2n, t, ps_x2)

            score(H - 1)
            pe.wait_ge(wo_split, NG)
            pe.wait_ge(attn_split, 2 * (H - 1))
            out_ahead(0)
            out_ahead(1)
            turn_probs(H - 1)
            out_ahead(2)
            attend(H - 1, G - 1)
            out_ahead(3)
            for t in range(4):
                pe.wait_ge(attn_split, 2 * H)
                out_part(t, [G - 1])
            for t in range(4, B):
                pe.wait_ge(o_added, B * (NG - 1) + t - 3)
                out_part(t, range(G))
                if t == 4:
                    turn_x2(0)
                turn_x2(t - 3)

            def shared_h(n, which, half, chunks=range(C)):
                tok = cols(half, HALF)
                psum = (ps_h1, ps_h2)[which][half]
                if n:
                    pe.wait_ge((silu_done, h_gated)[which], half + 1)
                for c in chunks:
                    w_hi, w_lo = w12_hi[n][:, which, c], w12_lo[n][:, which, c]
                    nc.tensor.matmul(psum[:], w_lo, xT_hi[:, c, tok], start=(c == 0), stop=False)
                    nc.tensor.matmul(psum[:], w_hi, xT_lo[:, c, tok], start=False, stop=False)
                    last = nc.tensor.matmul(psum[:], w_hi, xT_hi[:, c, tok], start=False, stop=(c == C - 1))
                if C - 1 in chunks:
                    last.then_inc(h_psum, 1)

            pe.wait_ge(w12_split, 1)
            pe.wait_ge(xT_split, B + 4)
            pe.wait_ge(o_added, B * (NG - 1) + 6)
            shared_h(0, 0, 0)
            turn_x2(5)
            turn_x2(6)
            shared_h(0, 1, 0)
            turn_x2(7)
            pe.wait_ge(rw_split, 1)
            pe.wait_ge(o_added, B * NG)
            for half in range(2):
                pe.wait_ge(xT_split, B + BH * (half + 1))
                tok = cols(half, HALF)
                three(ps_score[half][0:E, :], [(rw_hi[:, c], rw_lo[:, c], xT_hi[:, c, tok], xT_lo[:, c, tok])
                                               for c in range(C)]).then_inc(logitsT_psum, 1)
            def turn_logits(half):
                pe.wait_ge(logits_copied, half + 1)
                for t in range(BH * half, BH * (half + 1)):
                    last = nc.tensor.transpose(ps_turn[0][:, cols(t, E)], logitsT[:, cols(t)], ident[0:E, 0:E])
                last.then_inc(logits_psum, 1)

            turn_logits(0)
            shared_h(0, 0, 1, range(0, 1))
            turn_logits(1)
            shared_h(0, 0, 1, range(1, C))
            shared_h(0, 1, 1)
            pe.wait_ge(w12_split, 2)
            shared_h(1, 0, 0)
            shared_h(1, 1, 0)
            shared_h(1, 0, 1)
            shared_h(1, 1, 1)
            pe.wait_ge(const_done, 4)
            pe.wait_ge(counts_ready, 1)
            masks = rt[10]
            nc.tensor.matmul(ps_score[1][:, 0:B * E], before[:], masks[:].rearrange("p t e -> p (t e)"),
                             start=True, stop=False)
            nc.tensor.matmul(ps_score[1][:, 0:B * E], ones[:], cum[:, 0:B].rearrange("p t e -> p (t e)"),
                             start=False, stop=True)
            nc.tensor.matmul(ps_score[1][:, B * E:(B + 1) * E], ones[:], cum[:, B],
                             start=True, stop=True).then_inc(rank_psum, 1)
            pe.wait_ge(gates_done, 3)
            pe.wait_ge(logits_read, 1)
            for half in range(2):
                for b in range(BH):
                    last = nc.tensor.transpose((ps_score, ps_turn)[half][0][0:3 * GP, cols(b)],
                                               gates3[:, BH * half + b].rearrange("p n e -> p (n e)"), ident[:])
                last.then_inc(gT_psum, 1)
            for n in range(SH):
                pe.wait_ge(w3_split, n + 1)
            for t in range(B):
                if t % 4 == 0:
                    pe.wait_ge(h_split, 2 * (SH - 1) + t // 4 + 1)
                if t < 2:
                    pe.wait_ge((silu_done, h_gated)[t], 2 * SH - 1)
                else:
                    pe.wait_ge(shared_added, t - 1)
                three(ps_job[t % 2][:], [(hT_hi[n][:, cols(t)], hT_lo[n][:, cols(t)], w3_hi[n][:], w3_lo[n][:])
                                         for n in range(SH)], closed=False)
                if t == 0:
                    pe.wait_ge(gT_sbuf, 2)
                    pe.wait_ge(b3_split, 2)
                nc.tensor.matmul(ps_job[t % 2][:], gT[:, cols(t)], b3_s[:], start=False, stop=True)\
                  .then_inc(shared_psum, 1)

            def turn_x(b, k, loads):
                pe.wait_ge(xb_in[k], 16 * loads)
                need(pe, xbT_sbuf, b - 1)
                for c in range(C):
                    last = nc.tensor.transpose(ps_turn[k][:, cols(c)], xb[k][:, cols(c)], ident[:])
                last.then_inc(xbT_psum, 1)

            def turn_h(b, k):
                pe.wait_ge(hb_gated, b + 1)
                need(pe, hbT_sbuf, b - 1)
                nc.tensor.transpose(ps_score[k][:, 0:P], h_gate_b[k][:], ident[:]).then_inc(hbT_psum, 1)

            def owner_of(b):
                return pe.value_load(owner[0:1, bass.ds(b, 1)], min_val=0, max_val=E - 1)

            def block_y(b, k, e):
                pe.wait_ge(hbT_sbuf, b + 1)
                need(pe, yb_sbuf, b - 1)
                nc.tensor.matmul(ps_job[k][:], hT_b[k][:], w3_s[:, e], start=True, stop=True).then_inc(yb_psum, 1)

            def block_step(b, k, pair):
                static = isinstance(b, int)
                later = not (static and b == 0)
                e = owner_of(b)
                pe.wait_ge(xbT_sbuf, b + 1)
                need(pe, hb_biased, b - 1)
                for c in range(C):
                    last = nc.tensor.matmul(ps_attn[k][:, 0:2 * P], xbT[k][:, cols(c)], ew12_s[:, e, c],
                                            start=(c == 0), stop=(c == C - 1))
                    if c == 1 and later:
                        turn_h(b - 1, 1 - k)
                last.then_inc(hb_psum, 1)
                e_before = owner_of(b - 1) if not static and k == 1 else held[0]
                held[0] = e
                if not (static and b + 2 >= NB):
                    turn_x(b + 2, k, pair + 2 + (1 - k))
                if later:
                    if static and b == 1:
                        pe.wait_ge(ew3_in, 16 * 4)
                    block_y(b - 1, 1 - k, e_before)

            pe.wait_ge(owner_ready, 1)
            pe.wait_ge(ew12_in, 16 * 4)
            turn_x(0, 0, 1)
            turn_x(1, 1, 1)
            pe.wait_ge(shared_added, B)
            held = [None]
            pair_loop(pe, block_step)
            turn_h(NB - 1, 0)
            block_y(NB - 1, 0, held[0])

        @block.scalar
        def _(act):
            act.dma_start(gain[:], gains.partition_broadcast(P)).then_inc(gain_in, 16)
            act.dma_start(lnw_s[:], lnw.partition_broadcast(P)).then_inc(lnw_in, 16)
            act.dma_start(mask_u8[:], mask.rearrange("b q k -> q b k")).then_inc(mask_in, 16)

            def copy(dst, src):
                return nc.scalar.activation(dst, src, ACT.Copy)

            def tokens_hi(t, n, psum):
                act.wait_ge(xT_psum, n + 1)
                copy(xT_hi[:, :, t * P:(t + 1) * P],
                     psum[t][:].rearrange("p (c k) -> p c k", c=C)).then_inc(xT_hi_done, 1)

            def exps(i, half):
                act.wait_ge(max_done, 2 * i + 1 + half)
                for b in range(BH):
                    last = nc.scalar.activation(probs[:, half, b], probs[:, half, b], ACT.Exp,
                                                bias=neg_max[:, half, b:b + 1],
                                                accum_out=row_sum[:, half, b:b + 1])
                last.then_inc(exp_done, 1)

            def take_qk(i, n, dst, half):
                act.wait_ge(qk_psum, 4 * i + n + 1)
                copy(dst[:, half * HALF:(half + 1) * HALF], ps_job[half][:]).then_inc(qk_sbuf, 1)

            def take_v(g, t):
                act.wait_ge(v_psum, B * g + t + 1)
                copy(v_s[:, t], ps_job[t % 2][:]).then_inc(v_sbuf, 1)

            def take_pT(i):
                for half in range(2):
                    act.wait_ge(pT_psum, 2 * i + 1 + half)
                    copy(pT[:, half], ps_turn[half][:]).then_inc(pT_sbuf, 1)

            def take_attn_hi(i, slot):
                for half in range(2):
                    act.wait_ge(attn_psum, 2 * i + 1 + half)
                    copy(attn_hi[:, slot, half * HALF:(half + 1) * HALF], ps_attn[half][:]).then_inc(attn_hi_done, 1)

            def scaled(dst, src, scale, shift):
                return nc.scalar.activation(dst, src, ACT.Identity, bias=shift, scale=scale)

            act.wait_ge(gain_in, 16)
            nc.scalar.activation(gain[:], gain[:], ACT.Tanh).then_inc(gain_done, 1)
            for c in range(C):
                act.wait_ge(ctx_in[c], 32)
                copy(ctx_hi[:, c], ctx_raw[:, c]).then_inc(ctx_hi_done, 1)
            act.wait_ge(rms_ready, 1)
            def take_first_v(t):
                act.wait_ge(v_psum, t + 1)
                copy(v_s[:, t], ps_first_v[t][:]).then_inc(v_sbuf, 1)

            for t in range(B):
                scaled(xn[:, t], acc[:, t], rms_scale[:, t:t + 1], rms_shift[:, t:t + 1]).then_inc(x_normed, 1)
                if t >= 1:
                    take_first_v(t - 1)
            take_first_v(B - 1)

            def head_step(g, j, first):
                i = G * g + j
                before = not (first and j == 0)
                if before:
                    exps(i - 1, 0)
                take_qk(i, 0, kT, 0)
                if before:
                    exps(i - 1, 1)
                else:
                    for t in range(3):
                        tokens_hi(t, t, ps_x)
                take_qk(i, 1, kT, 1)
                if not before:
                    for t in range(3, B):
                        tokens_hi(t, t, ps_x)
                take_qk(i, 2, qT, 0)
                if before:
                    take_pT(i - 1)
                take_qk(i, 3, qT, 1)
                if before:
                    take_attn_hi(i - 1, (j - 1) % G)
                if j == 0 and not first:
                    for t in range(B):
                        take_v(g, t)

            for j in range(G):
                head_step(0, j, True)
                for t in (2 * j, 2 * j + 1):
                    scaled(acc[:, t], acc[:, t], rstd[:, t:t + 1], shift[:, t:t + 1]).then_inc(ln_ready, 1)
            with act.Fori(1, NG) as g:
                for j in range(G):
                    head_step(g, j, False)
            exps(H - 1, 0)
            exps(H - 1, 1)
            take_pT(H - 1)
            take_attn_hi(H - 1, G - 1)

            def split_w12(n):
                act.wait_ge(w12_in[n], 16)
                copy(w12_hi[n][:].rearrange("p w c k -> p (w c k)"), w12_raw[n][:, 0:W12]).then_inc(w12_hi_done, 1)

            def split_w3(n):
                act.wait_ge(w3_in[n], 16)
                copy(w3_hi[n][:], w3_raw[n][:]).then_inc(w3_hi_done, 1)

            def normalise_x2(t):
                act.wait_ge(shift_ready, t + 1)
                scaled(x2n[:, t], acc[:, t], rstd[:, t:t + 1], shift[:, t:t + 1]).then_inc(xn_ready, 1)

            for t in range(B):
                normalise_x2(t)
                if t >= 1:
                    tokens_hi(t - 1, B + t - 1, ps_x2)
                if t in (1, 3):
                    split_w12(t // 2)
                if t in (4, 5):
                    split_w3(t - 4)
            tokens_hi(B - 1, 2 * B - 1, ps_x2)
            for half in range(2):
                act.wait_ge(logitsT_psum, half + 1)
                copy(logitsT[:, half * HALF:(half + 1) * HALF], ps_score[half][0:E, :]).then_inc(logits_copied, 1)
            act.wait_ge(router_in, 1)
            nc.scalar.activation(rt[1][:], rt[1][:], ACT.Exp).then_inc(router_exp, 1)
            for n in range(SH):
                for half in range(2):
                    act.wait_ge(h_psum, 4 * n + 2 * half + 1)
                    nc.scalar.activation(silu[:, half], ps_h1[half][:], ACT.Silu,
                                         bias=w12_raw[n][:, W12:W12 + 1]).then_inc(silu_done, 1)
                    act.wait_ge(h_gated, 2 * n + half + 1)
                    copy(hT_hi[n][:, half * HALF:(half + 1) * HALF], hT[:, half]).then_inc(h_hi_done, 1)
            for half in range(2):
                act.wait_ge(gT_psum, half + 1)
                copy(gT[:, half * HALF:(half + 1) * HALF], (ps_score, ps_turn)[half][0][0:3 * GP, :]).then_inc(gT_sbuf, 1)

            def take_xbT(b, k):
                act.wait_ge(xbT_psum, b + 1)
                copy(xbT[k][:], ps_turn[k][:]).then_inc(xbT_sbuf, 1)

            def take_y(b, k, stores):
                act.wait_ge(yb_psum, b + 1)
                need(act, y_stored[k], 16 * stores)
                copy(y_out[k][:], ps_job[k][:]).then_inc(yb_sbuf, 1)

            def block_step(b, k, pair):
                static = isinstance(b, int)
                act.wait_ge(hb_biased, b + 1)
                nc.scalar.activation(silu_b[k][:], h_b[k][:, 0:P], ACT.Silu).then_inc(silu_b_done, 1)
                if not (static and b + 2 >= NB):
                    take_xbT(b + 2, k)
                if not (static and b == 0):
                    take_y(b - 1, 1 - k, pair)

            take_xbT(0, 0)
            take_xbT(1, 1)
            pair_loop(act, block_step)
            take_y(NB - 1, 0, NB // 2)

        @block.vector
        def _(dve):
            V = nc.vector
            links = [0]

            def chain(ins):
                links[0] += 1
                ins.then_inc(dve_chain, 1)
                dve.wait_ge(dve_chain, links[0])

            def split(hi, lo, raw, in_sem, in_count, hi_sem, done_sem, count):
                dve.wait_ge(in_sem, in_count)
                V.tensor_copy(hi, raw).then_inc(hi_sem, 1)
                dve.wait_ge(hi_sem, count)
                V.tensor_tensor(lo, raw, hi, ALU.subtract).then_inc(done_sem, 1)

            def tokens_lo(t, n, psum):
                dve.wait_ge(xT_hi_done, n + 1)
                tok = slice(t * P, (t + 1) * P)
                V.tensor_tensor(xT_lo[:, :, tok], psum[t][:].rearrange("p (c k) -> p c k", c=C),
                                xT_hi[:, :, tok], ALU.subtract).then_inc(xT_split, 1)

            for c in range(C):
                dve.wait_ge(ctx_in[c], 32)
                V.tensor_copy(wv_hi[:, c], wv_raw[:, c]).then_inc(wv_hi_done, 1)
                dve.wait_ge(wv_hi_done, c + 1)
                V.tensor_tensor(wv_lo[:, c], wv_raw[:, c], wv_hi[:, c], ALU.subtract).then_inc(wv_split, 1)
                dve.wait_ge(ctx_hi_done, c + 1)
                V.tensor_tensor(ctx_lo[:, c], ctx_raw[:, c], ctx_hi[:, c], ALU.subtract).then_inc(ctx_split, 1)

            for t in range(B):
                dve.wait_ge(x_in[t], 16)
                last = V.bn_stats(stats[:, t], acc[:, t])
            chain(last)
            for t in range(B):
                last = V.bn_aggr(mean_var[:, t], stats[:, t])
            chain(last)
            V.tensor_scalar(rstd[:], mean_var[:, :, 1], EPS, None, ALU.add).then_inc(var_ready, 1)
            dve.wait_ge(wqk_in[0], 16)
            V.tensor_copy(wqk_hi[:, 0], wqk_raw[:, 0]).then_inc(wqk_hi_done, 1)
            dve.wait_ge(rstd_ready, 1)
            V.scalar_tensor_tensor(out=shift[:], in0=mean_var[:, :, 0], scalar=-1.0, in1=rstd[:],
                                   op0=ALU.mult, op1=ALU.mult)
            chain(V.tensor_tensor(rms[:], mean_var[:, :, 1], rstd[:], ALU.mult))
            chain(V.tensor_tensor(rms[:], rms[:], rstd[:], ALU.mult))
            V.tensor_scalar(rms[:], rms[:], EPS, None, ALU.add).then_inc(var_ready, 1)
            dve.wait_ge(wqk_hi_done, 1)
            V.tensor_tensor(wqk_lo[:, 0], wqk_raw[:, 0], wqk_hi[:, 0], ALU.subtract).then_inc(wqk_split, 1)
            dve.wait_ge(rstd_ready, 2)
            V.tensor_tensor(rms_shift[:], shift[:], rms[:], ALU.mult)
            V.tensor_tensor(rms_scale[:], rstd[:], rms[:], ALU.mult).then_inc(rms_ready, 1)
            dve.wait_ge(lnw_in, 16)
            for t in range(B):
                dve.wait_ge(x_normed, t + 1)
                V.tensor_tensor(xn[:, t], xn[:, t], lnw_s[:], ALU.mult).then_inc(xn_ready, 1)

            for t in range(B):
                tokens_lo(t, t, ps_x)

            dve.wait_ge(mask_in, 16)
            V.tensor_scalar(mask_bias[:], mask_u8[:], -1.0, BIG, ALU.add, ALU.mult).then_inc(mask_done, 1)
            dve.wait_ge(mask_done, 1)
            chain(V.tensor_reduce(any_mask[:], mask_bias[:], AX.X, ALU.max))
            chain(V.tensor_scalar(any_mask[:], any_mask[:], -1.0, None, ALU.is_ge))

            dve.wait_ge(rw_in, 16)
            chain(V.tensor_copy(rw_hi[:], rw_raw[:]))
            V.tensor_tensor(rw_lo[:], rw_raw[:], rw_hi[:], ALU.subtract).then_inc(rw_split, 1)

            def bias_and_max(i):
                dve.wait_ge(bias_ready, i + 1)
                for half in range(2):
                    dve.wait_ge(score_psum, 2 * i + 1 + half)
                    V.tensor_tensor(probs[:, half], ps_score[half][:].rearrange("p (b k) -> p b k", b=BH),
                                    score_bias[:, BH * half:BH * (half + 1)], ALU.add).then_inc(score_biased, 1)
                for half in range(2):
                    dve.wait_ge(score_biased, 2 * i + 1 + half)
                    V.tensor_reduce(neg_max[:, half], probs[:, half], AX.X, ALU.max, negate=True).then_inc(max_done, 1)

            def normalise(i, count):
                for half in range(2):
                    dve.wait_ge(exp_done, 2 * i + 1 + half)
                    V.reciprocal(row_inv[:, half], row_sum[:, half]).then_inc(count, 1)
                    dve.wait_ge(count, 4 * i + 2 * half + 1)
                    V.tensor_tensor(row_scale[:, half], row_inv[:, half], any_mask[:, BH * half:BH * (half + 1)],
                                    ALU.mult).then_inc(count, 1)
                    dve.wait_ge(count, 4 * i + 2 * half + 2)
                    V.tensor_tensor(probs[:, half], probs[:, half],
                                    row_scale[:, half].unsqueeze(2).broadcast_to([P, BH, P]),
                                    ALU.mult).then_inc(probs_ready, 1)

            def take_attn_lo(i, slot):
                for half in range(2):
                    dve.wait_ge(attn_hi_done, 2 * i + 1 + half)
                    tok = slice(half * HALF, (half + 1) * HALF)
                    V.tensor_tensor(attn_lo[:, slot, tok], ps_attn[half][:], attn_hi[:, slot, tok],
                                    ALU.subtract).then_inc(attn_split, 1)

            def add_out(g, t):
                dve.wait_ge(o_psum, B * g + t + 1)
                return V.tensor_tensor(acc[:, t], ps_job[t % 2][:], acc[:, t], ALU.add)

            def head_step(g, j, first):
                i = G * g + j
                before = not (first and j == 0)
                if before:
                    bias_and_max(i - 1)
                if j == 0 and not first:
                    split(wv_hi[:], wv_lo[:], wv_raw[:], wv_in, 16 * g, wv_hi_done, wv_split, C + g)
                if j == 1 and not first:
                    for t in range(B):
                        add_out(g - 1, t).then_inc(o_added, 1)
                n = (j + 1) % 2
                if before:
                    normalise(i - 1, row_scaled)
                split(wqk_hi[:, n], wqk_lo[:, n], wqk_raw[:, n], wqk_in[n], 16 * (2 * g + (j + 1) // 2 + 1),
                      wqk_hi_done, wqk_split, i + 2)
                if j == 3:
                    split(wo_hi[:], wo_lo[:], wo_raw[:], wo_in, 16 * (g + 1), wo_hi_done, wo_split, g + 1)
                if before:
                    take_attn_lo(i - 1, (j - 1) % G)

            for j in range(G):
                head_step(0, j, True)
            dve.wait_ge(ln_ready, B)
            with dve.Fori(1, NG) as g:
                for j in range(G):
                    head_step(g, j, False)
            def add_residual(t):
                V.scalar_tensor_tensor(out=acc[:, t], in0=acc[:, t], scalar=gain[:, 0:1], in1=x_res[:, t],
                                       op0=ALU.mult, op1=ALU.add).then_inc(residual_added, 1)

            bias_and_max(H - 1)
            dve.wait_ge(gain_done, 1)
            dve.wait_ge(x_res_in, 16)
            dve.wait_ge(o_added, B * (NG - 1))
            for t in range(2):
                add_residual(t)
            normalise(H - 1, row_scaled)
            for t in range(2, B):
                add_residual(t)
            take_attn_lo(H - 1, G - 1)

            def w12_lo_part(buf, count):
                dve.wait_ge(w12_hi_done, count)
                V.tensor_tensor(w12_lo[buf][:].rearrange("p w c k -> p (w c k)"), w12_raw[buf][:, 0:W12],
                                w12_hi[buf][:].rearrange("p w c k -> p (w c k)"), ALU.subtract).then_inc(w12_split, 1)

            def w3_lo_part(buf, count):
                dve.wait_ge(w3_hi_done, count)
                V.tensor_tensor(w3_lo[buf][:], w3_raw[buf][:], w3_hi[buf][:], ALU.subtract).then_inc(w3_split, 1)

            for t in range(B):
                dve.wait_ge(o_psum, B * (NG - 1) + t + 1)
                dve.wait_ge(residual_added, t + 1)
                V.scalar_tensor_tensor(out=acc[:, t], in0=ps_out[t % 4][:], scalar=gain[:, 0:1], in1=acc[:, t],
                                       op0=ALU.mult, op1=ALU.add).then_inc(o_added, 1)
                dve.wait_ge(o_added, B * (NG - 1) + t + 1)
                chain(V.bn_stats(stats[:, t], acc[:, t]))
                chain(V.bn_aggr(mean_var[:, t], stats[:, t]))
                V.tensor_scalar(neg_mean[:, t:t + 1], mean_var[:, t, 0:1], -1.0, None, ALU.mult)
                V.tensor_scalar(rstd[:, t:t + 1], mean_var[:, t, 1:2], EPS, None, ALU.add).then_inc(var_ready, 1)
                if t == 3:
                    w12_lo_part(0, 1)
                for n in {3: [0], 4: [1], 5: [2, 3], 7: [4]}.get(t, []):
                    tokens_lo(n, B + n, ps_x2)
            for t in range(B - 3, B):
                tokens_lo(t, B + t, ps_x2)
            w12_lo_part(1, 2)
            for n in range(SH):
                w3_lo_part(n, n + 1)

            def gate_h(n, half):
                dve.wait_ge(h_psum, 4 * n + 2 * half + 2)
                need(dve, h_split, 2 * (n - 1) + half + 1 if n else 0)
                dve.wait_ge(silu_done, 2 * n + half + 1)
                V.scalar_tensor_tensor(out=hT[:, half], in0=ps_h2[half][:], scalar=w12_raw[n][:, W12 + 1:W12 + 2],
                                       in1=silu[:, half], op0=ALU.add, op1=ALU.mult).then_inc(h_gated, 1)

            def h_lo(n, half):
                dve.wait_ge(h_hi_done, 2 * n + half + 1)
                tok = slice(half * HALF, (half + 1) * HALF)
                V.tensor_tensor(hT_lo[n][:, tok], hT[:, half], hT_hi[n][:, tok], ALU.subtract).then_inc(h_split, 1)

            def along(a, n):
                return a.unsqueeze(2).broadcast_to([P, B, n])

            def pick_first(src, rank, tiles, ones, n):
                chain(V.tensor_reduce(ones[0][:], src[:], AX.X, ALU.max))
                chain(V.tensor_tensor(tiles[0][:], src[:], along(ones[0][:], n), ALU.is_equal))
                chain(V.tensor_tensor(tiles[1][:], tiles[0][:], rank, ALU.mult))
                chain(V.tensor_reduce(ones[1][:], tiles[1][:], AX.X, ALU.max))
                chain(V.tensor_tensor(tiles[2][:], tiles[1][:], along(ones[1][:], n), ALU.is_equal))
                return tiles[2]

            def pick_two(src, less, rank, tiles, ones, n):
                one = pick_first(src, rank, tiles[0:3], ones[0:2], n)
                chain(V.scalar_tensor_tensor(out=less[:], in0=one[:], scalar=-BIG, in1=src[:],
                                             op0=ALU.mult, op1=ALU.add))
                two = pick_first(less, rank, tiles[3:6], ones[2:4], n)
                return one, two

            dve.wait_ge(b3_in, 16)
            V.tensor_copy(b3_s[:], b3_raw[:]).then_inc(b3_hi_done, 1)
            dve.wait_ge(b3_hi_done, 1)
            V.tensor_tensor(b3_s[2 * GP:], b3_raw[2 * GP:], b3_s[2 * GP:], ALU.subtract).then_inc(b3_split, 2)

            logits, shifted = rt[0], rt[1]
            dve.wait_ge(logits_psum, 2)
            dve.wait_ge(rb_in, 16)
            V.tensor_tensor(logits[:], ps_turn[0][:, 0:B * E].rearrange("p (t e) -> p t e", t=B),
                            rb_s[:, 0].unsqueeze(1).broadcast_to([P, B, E]), ALU.add).then_inc(logits_read, 1)
            dve.wait_ge(logits_read, 1)
            chain(V.tensor_reduce(r1[0][:], logits[:], AX.X, ALU.max))
            V.tensor_tensor(shifted[:], logits[:], along(r1[0][:], E), ALU.subtract).then_inc(router_in, 1)
            dve.wait_ge(rank_done, 11)
            rank = rt[2]
            V.tensor_copy(block_no[:], block_no_i[:])
            V.tensor_copy(round_up[:], round_up_i[:])
            chain(V.tensor_copy(rank[:], rank_i[:]))
            dve.wait_ge(router_exp, 1)
            chain(V.tensor_reduce(r1[1][:], shifted[:], AX.X, ALU.add))
            chain(V.reciprocal(r1[2][:], r1[1][:]))
            chain(V.tensor_tensor(shifted[:], shifted[:], along(r1[2][:], E), ALU.mult))
            scores = rt[0]
            chain(V.tensor_tensor(scores[:], shifted[:], rb_s[:, 1].unsqueeze(1).broadcast_to([P, B, E]), ALU.add))
            gate_h(0, 0)
            chain(V.tensor_reduce(rg[0][:], scores[:].rearrange("p t (g m) -> p t g m", g=EG), AX.X, ALU.max))
            one, two = pick_two(rg[0], rg[1], rank[:, :, 0:EG], rg[2:8], r1[3:7], EG)
            gate_h(0, 1)
            chain(V.tensor_tensor(rg[8][:], one[:], two[:], ALU.add))
            chain(V.tensor_scalar(rg[9][:], rg[8][:], -1.0, BIG, ALU.add, ALU.mult))
            kept = rt[1]
            chain(V.tensor_tensor(kept[:].rearrange("p t (g m) -> p (t g) m", g=EG),
                                  scores[:].rearrange("p t (g m) -> p (t g) m", g=EG),
                                  rg[9][:].rearrange("p t g -> p (t g)").unsqueeze(2).broadcast_to([P, B * EG, EM]),
                                  ALU.add))
            picked = pick_two(kept, rt[9], rank[:], rt[3:9], r1[3:7], E)
            masks = rt[10]
            V.tensor_tensor(masks_before[:, B:], picked[0][:], picked[1][:], ALU.add)
            chain(V.tensor_tensor(masks[:], picked[0][:], picked[1][:], ALU.add))
            chain(V.tensor_tensor(sums[0][:, B:], masks[:], masks_before[:, B - 1:2 * B - 1], ALU.add))
            chain(V.tensor_tensor(sums[1][:, B:], sums[0][:, B:], sums[0][:, B - 2:2 * B - 2], ALU.add))
            V.tensor_tensor(cum[:, 1:], sums[1][:, B:], sums[1][:, B - 4:2 * B - 4], ALU.add).then_inc(counts_ready, 1)
            chain(V.tensor_tensor(gates[:, 1:1 + E, :].rearrange("p e t -> p t e"), masks[:], scores[:], ALU.mult))
            V.tensor_copy(gates_hi[:], gates[:]).then_inc(gates_hi_done, 1)
            dve.wait_ge(gates_hi_done, 1)

            def by_tile(a):
                return a[:].rearrange("p e t -> p t e")

            V.tensor_copy(gates3[:, :, 0, 0:E + 1], by_tile(gates_hi)).then_inc(gates_done, 1)
            V.tensor_copy(gates3[:, :, 2, 0:E + 1], by_tile(gates_hi)).then_inc(gates_done, 1)
            V.tensor_tensor(gates3[:, :, 1, 0:E + 1], by_tile(gates), by_tile(gates_hi),
                            ALU.subtract).then_inc(gates_done, 1)

            h_lo(0, 0)
            h_lo(0, 1)

            dve.wait_ge(rank_psum, 1)
            chain(V.tensor_scalar(blocks_i[:], ps_score[1][:, B * E:(B + 1) * E], float(P - 1), None, ALU.add))
            chain(V.tensor_scalar(blocks_i[:], blocks_i[:], P.bit_length() - 1, None, ALU.arith_shift_right))
            V.tensor_copy(nblocks[:], blocks_i[:])
            chain(V.tensor_copy(scan[0][:, E // 2:], blocks_i[:]))
            src, dst = scan
            for d in (1, 2, 4, 8):
                chain(V.tensor_tensor(dst[:, E // 2:], src[:, E // 2:], src[:, E // 2 - d:E // 2 + E - d], ALU.add))
                src, dst = dst, src
            end = src[:, E // 2:]
            chain(V.tensor_tensor(first_slot[:], end, nblocks[:], ALU.subtract))
            slots = rt[2]
            chain(V.scalar_tensor_tensor(
                out=slots[:], in0=first_slot[:].unsqueeze(1).broadcast_to([P, B, E]), scalar=float(P),
                in1=ps_score[1][:, 0:B * E].rearrange("p (t e) -> p t e", t=B), op0=ALU.mult, op1=ALU.add))
            for n in range(TOP):
                chain(V.tensor_tensor(rt[9][:], picked[n][:], slots[:], ALU.mult))
                chain(V.tensor_reduce(slot_f[n][:], rt[9][:], AX.X, ALU.add))
                V.tensor_copy(slot_i[n][:], slot_f[n][:]).then_inc(slots_ready, 1)
            gate_h(1, 0)
            h_lo(1, 0)
            chain(V.tensor_tensor(ended[:], block_no[:].unsqueeze(2).broadcast_to([1, NS, E]),
                                  end[0:1].unsqueeze(1).broadcast_to([1, NS, E]), ALU.is_ge))
            chain(V.tensor_reduce(owner_f[:], ended[:], AX.X, ALU.add))
            V.tensor_scalar(owner[:], owner_f[:], float(E - 1), None, ALU.min).then_inc(owner_ready, 1)
            gate_h(1, 1)
            h_lo(1, 1)
            chain(V.tensor_tensor(stores_i[:], round_up[:], end[0:1, E - 1:E].broadcast_to([1, 2]), ALU.add))
            chain(V.tensor_scalar(stores_i[:], stores_i[:], 1, None, ALU.arith_shift_right))
            V.tensor_scalar(stores_i[:], stores_i[:], 4, None, ALU.logical_shift_left).then_inc(stores_known, 1)
            for n in range(TOP):
                chain(V.tensor_tensor(rt[9][:], picked[n][:], scores[:], ALU.mult))
                last = V.tensor_reduce(gate_raw[:, n], rt[9][:], AX.X, ALU.add)
                if n == 0:
                    chain(last)
            last.then_inc(gate_raw_ready, 1)
            for t in range(B):
                dve.wait_ge(shared_psum, t + 1)
                V.scalar_tensor_tensor(out=acc[:, t], in0=ps_job[t % 2][:], scalar=gain[:, 1:2], in1=acc[:, t],
                                       op0=ALU.mult, op1=ALU.add).then_inc(shared_added, 1)

            def take_hT(b, k):
                dve.wait_ge(hbT_psum, b + 1)
                V.tensor_copy(hT_b[k][:], ps_score[k][:, 0:P]).then_inc(hbT_sbuf, 1)

            def block_step(b, k, pair):
                if not (isinstance(b, int) and b == 0):
                    take_hT(b - 1, 1 - k)
                dve.wait_ge(hb_psum, b + 1)
                dve.wait_ge(bias_b_in[k], 16 * (pair + 2 - k))
                V.tensor_tensor(h_b[k][:], ps_attn[k][:, 0:2 * P], bias_b[k][:], ALU.add).then_inc(hb_biased, 1)
                dve.wait_ge(silu_b_done, b + 1)
                V.tensor_tensor(h_gate_b[k][:], silu_b[k][:], h_b[k][:, P:2 * P], ALU.mult).then_inc(hb_gated, 1)

            pair_loop(dve, block_step)
            take_hT(NB - 1, 0)

            dve.wait_ge(gate_ready, 1)
            for t in range(B):
                dve.wait_ge(y_pick_in[t], 16 * TOP)
                dve.wait_ge(first_added, t + 1)
                V.scalar_tensor_tensor(out=y_pick[:, 1, t], in0=y_pick[:, 1, t], scalar=gate_f[:, 1, t:t + 1],
                                       in1=acc[:, t], op0=ALU.mult, op1=ALU.add).then_inc(final_ready, 1)


def kernel(x, ctx_4096, mask_BxSxS2_bk0, g_xattn, g_ffn, L0_xattn_position_bias, L0_xattn_ln_weight,
           L0_xattn_w_q, L0_xattn_w_k, L0_xattn_w_v, L0_xattn_w_out, L0_ffn_router_w, L0_ffn_router_b,
           L0_ffn_router_bias, L0_ffn_ew1, L0_ffn_eb1, L0_ffn_ew2, L0_ffn_eb2, L0_ffn_ew3, L0_ffn_eb3,
           L0_ffn_sw1, L0_ffn_sb1, L0_ffn_sw2, L0_ffn_sb2, L0_ffn_sw3, L0_ffn_sb3):
    import numpy as np
    import concourse.bacc as bacc
    from concourse.bass_utils import run_bass_kernel_spmd as run

    def chunks(wT, width):
        return wT.reshape(C, P, -1, width).transpose(2, 1, 0, 3)

    wq = chunks(np.asarray(L0_xattn_w_q).T, P)
    wk = chunks(np.asarray(L0_xattn_w_k).T, P)
    wqk = np.stack([wq, wk], axis=2)
    wqk = np.concatenate([wqk, wqk[:1]])
    wv = chunks(np.asarray(L0_xattn_w_v).T, G * P)
    wo = np.asarray(L0_xattn_w_out).T.reshape(NG, G, P, D).transpose(0, 2, 1, 3)

    sw12 = np.concatenate([chunks(np.asarray(L0_ffn_sw1), P).reshape(SH, P, C * P),
                           chunks(np.asarray(L0_ffn_sw2), P).reshape(SH, P, C * P),
                           np.asarray(L0_ffn_sb1).reshape(SH, P, 1), np.asarray(L0_ffn_sb2).reshape(SH, P, 1)], axis=2)
    ew12 = np.concatenate([np.asarray(L0_ffn_ew1).reshape(E, C, P, P), np.asarray(L0_ffn_ew2).reshape(E, C, P, P)],
                          axis=3).transpose(0, 2, 1, 3)
    b3 = np.concatenate([np.asarray(L0_ffn_sb3)[None], np.asarray(L0_ffn_eb3)])
    b3_three = np.zeros((3, GP, D), b3.dtype)
    b3_three[:, :E + 1] = b3
    arrays = {
        "x": np.asarray(x),
        "ctxT": np.asarray(ctx_4096).reshape(T, C, P).transpose(2, 1, 0),
        "mask": np.asarray(mask_BxSxS2_bk0),
        "gains": np.concatenate([np.asarray(g_xattn), np.asarray(g_ffn)]),
        "pbias": np.asarray(L0_xattn_position_bias),
        "lnw": np.asarray(L0_xattn_ln_weight),
        "wqk": wqk,
        "wv": wv,
        "wo": wo,
        "sw12": sw12,
        "sw3": np.asarray(L0_ffn_sw3).reshape(SH, P, D),
        "ew12": ew12,
        "eb12": np.concatenate([np.asarray(L0_ffn_eb1), np.asarray(L0_ffn_eb2)], axis=1),
        "ew3": np.asarray(L0_ffn_ew3),
        "rw": np.asarray(L0_ffn_router_w).reshape(C, P, E).transpose(1, 0, 2),
        "rb": np.stack([np.asarray(L0_ffn_router_b), np.asarray(L0_ffn_router_bias)]),
        "b3": b3_three.reshape(3 * GP, D),
    }
    nc = bacc.Bacc("TRN2", target_bir_lowering=False, num_devices=1)
    args = []
    for name in arrays:
        a = arrays[name] = np.ascontiguousarray(arrays[name])
        args.append(nc.dram_tensor(f"{name}_dram", a.shape, mybir.dt.from_np(a.dtype), kind="ExternalInput").ap())
    out = nc.dram_tensor("out_dram", (B, P, D), F32, kind="ExternalOutput").ap()
    build(nc, *args, out)
    result = run(nc, [{f"{name}_dram": a for name, a in arrays.items()}], core_ids=[0])
    return result.results[0]["out_dram"]
```
